# Optimizing a Trainium2 kernel written in Bass

```python
import numpy as np
import jax
import jax.numpy as jnp

def _softmax(x, axis=-1):
    return jax.nn.softmax(x, axis=axis)

def _gelu(x):
    return jax.nn.gelu(x, approximate=True)

def _silu(x):
    return jax.nn.silu(x)

def _sigmoid(x):
    return jax.nn.sigmoid(x)

def _layernorm(x, axis=-1, eps=1e-05):
    m = jnp.mean(x, axis=axis, keepdims=True)
    v = jnp.var(x, axis=axis, keepdims=True)
    return (x - m) / jnp.sqrt(v + eps)

def _scatter_add(tgt, idx, src, axis=0):
    return tgt.at[idx].add(src)

def _segment_sum(src, seg, n):
    return jax.ops.segment_sum(src, seg, n)
kernel_name = 'mk_seq_postln_d1_jaxref_r4_74fc23'

def setup_inputs(seed: int=0):
    np.random.seed(seed)
    _w = jnp.asarray

    def _L0_attn_setup():
        import jax, jax.numpy as jnp
        import numpy as np
        D_MODEL = 512
        D_INNER = 1024
        D_STATE = 16
        DT_RANK = 128
        D_CONV = 4
        EPS = 1e-05

        def _rmsnorm(x, w):
            return x * jax.lax.rsqrt(jnp.mean(jnp.square(x), axis=-1, keepdims=True) + EPS) * w

        def _depthwise_causal_conv(x, conv_w, conv_b):
            k = conv_w[:, None, :]
            y = jax.lax.conv_general_dilated(x, k, window_strides=(1,), padding=((D_CONV - 1, 0),), dimension_numbers=('NWC', 'WIO', 'NWC'), feature_group_count=D_INNER)
            return y + conv_b

        def _selective_scan(u, delta, A, B, C, D):
            deltaA = jnp.exp(jnp.einsum('bld,dn->bldn', delta, A))
            deltaBu = jnp.einsum('bld,bln,bld->bldn', delta, B, u)
            dA = jnp.moveaxis(deltaA, 1, 0)
            dBu = jnp.moveaxis(deltaBu, 1, 0)
            Ct = jnp.moveaxis(C, 1, 0)
            b, l, d = u.shape
            n = A.shape[1]

            def step(h, inputs):
                dA_t, dBu_t, C_t = inputs
                h = h * dA_t + dBu_t
                y = jnp.einsum('bdn,bn->bd', h, C_t)
                return (h, y)
            h0 = jnp.zeros((b, d, n), u.dtype)
            _, ys = jax.lax.scan(step, h0, (dA, dBu, Ct))
            y = jnp.moveaxis(ys, 0, 1)
            return y + u * D
        key = jax.random.key(seed)
        ks = jax.random.split(key, 10)
        b, l = (1, 256)
        s = 0.02
        x = jax.random.normal(ks[0], (b, l, D_MODEL), jnp.float32)
        w_norm = jnp.ones((D_MODEL,), jnp.float32)
        W_in = jax.random.normal(ks[1], (D_MODEL, 2 * D_INNER), jnp.float32) * s
        conv_w = jax.random.normal(ks[2], (D_CONV, D_INNER), jnp.float32) * 0.3
        conv_b = jnp.zeros((D_INNER,), jnp.float32)
        W_xp = jax.random.normal(ks[3], (D_INNER, DT_RANK + 2 * D_STATE), jnp.float32) * s
        W_dt = jax.random.normal(ks[4], (DT_RANK, D_INNER), jnp.float32) * s
        b_dt = jnp.full((D_INNER,), -4.0, jnp.float32)
        A_log = jnp.log(jnp.tile(jnp.arange(1, D_STATE + 1, dtype=jnp.float32), (D_INNER, 1)))
        D = jnp.ones((D_INNER,), jnp.float32)
        W_out = jax.random.normal(ks[5], (D_INNER, D_MODEL), jnp.float32) * s
        return dict(x=x, w_norm=w_norm, W_in=W_in, conv_w=conv_w, conv_b=conv_b, W_xp=W_xp, W_dt=W_dt, b_dt=b_dt, A_log=A_log, D=D, W_out=W_out)
    _L0_attn_in = _L0_attn_setup()

    def _L0_ffn_setup():
        import jax, jax.numpy as jnp
        import numpy as np
        B, S, D = (2, 512, 512)
        E, H, TOP_K = (8, 352, 2)
        SH = 352
        ROUTED_SCALE = 2.5
        key = jax.random.key(seed)
        ks = jax.random.split(key, 8)
        std = 0.02
        return {'x': jax.random.normal(ks[0], (B, S, D), jnp.float32), 'gate_w': jax.random.normal(ks[1], (E, D), jnp.float32) * std, 'w1': jax.random.normal(ks[2], (E, D, H), jnp.float32) * std, 'w3': jax.random.normal(ks[3], (E, D, H), jnp.float32) * std, 'w2': jax.random.normal(ks[4], (E, H, D), jnp.float32) * std, 'sw1': jax.random.normal(ks[5], (D, SH), jnp.float32) * std, 'sw3': jax.random.normal(ks[6], (D, SH), jnp.float32) * std, 'sw2': jax.random.normal(ks[7], (SH, D), jnp.float32) * std}
    _L0_ffn_in = _L0_ffn_setup()
    _d = {'L0_attn_x': _L0_attn_in['x'], 'L0_attn_w_norm': _L0_attn_in['w_norm'], 'L0_attn_W_in': _L0_attn_in['W_in'], 'L0_attn_conv_w': _L0_attn_in['conv_w'], 'L0_attn_conv_b': _L0_attn_in['conv_b'], 'L0_attn_W_xp': _L0_attn_in['W_xp'], 'L0_attn_W_dt': _L0_attn_in['W_dt'], 'L0_attn_b_dt': _L0_attn_in['b_dt'], 'L0_attn_A_log': _L0_attn_in['A_log'], 'L0_attn_D': _L0_attn_in['D'], 'L0_attn_W_out': _L0_attn_in['W_out'], 'L0_ffn_gate_w': _L0_ffn_in['gate_w'], 'L0_ffn_w1': _L0_ffn_in['w1'], 'L0_ffn_w2': _L0_ffn_in['w2'], 'L0_ffn_w3': _L0_ffn_in['w3'], 'L0_ffn_sw1': _L0_ffn_in['sw1'], 'L0_ffn_sw2': _L0_ffn_in['sw2'], 'L0_ffn_sw3': _L0_ffn_in['sw3']}
    _x0 = _d['L0_attn_x']
    _d['L0_attn_x'] = jax.random.normal(jax.random.fold_in(jax.random.key(seed), 1), (8, 512, 512), dtype=_x0.dtype)
    del _x0
    return _d

def reference(L0_attn_x, L0_attn_w_norm, L0_attn_W_in, L0_attn_conv_w, L0_attn_conv_b, L0_attn_W_xp, L0_attn_W_dt, L0_attn_b_dt, L0_attn_A_log, L0_attn_D, L0_attn_W_out, L0_ffn_gate_w, L0_ffn_w1, L0_ffn_w2, L0_ffn_w3, L0_ffn_sw1, L0_ffn_sw2, L0_ffn_sw3):

    def _L0_attn_ref(x, w_norm, W_in, conv_w, conv_b, W_xp, W_dt, b_dt, A_log, D, W_out):
        import jax, jax.numpy as jnp
        import numpy as np
        D_MODEL = 512
        D_INNER = 1024
        D_STATE = 16
        DT_RANK = 128
        D_CONV = 4
        EPS = 1e-05

        def _rmsnorm(x, w):
            return x * jax.lax.rsqrt(jnp.mean(jnp.square(x), axis=-1, keepdims=True) + EPS) * w

        def _depthwise_causal_conv(x, conv_w, conv_b):
            k = conv_w[:, None, :]
            y = jax.lax.conv_general_dilated(x, k, window_strides=(1,), padding=((D_CONV - 1, 0),), dimension_numbers=('NWC', 'WIO', 'NWC'), feature_group_count=D_INNER)
            return y + conv_b

        def _selective_scan(u, delta, A, B, C, D):
            deltaA = jnp.exp(jnp.einsum('bld,dn->bldn', delta, A))
            deltaBu = jnp.einsum('bld,bln,bld->bldn', delta, B, u)
            dA = jnp.moveaxis(deltaA, 1, 0)
            dBu = jnp.moveaxis(deltaBu, 1, 0)
            Ct = jnp.moveaxis(C, 1, 0)
            b, l, d = u.shape
            n = A.shape[1]

            def step(h, inputs):
                dA_t, dBu_t, C_t = inputs
                h = h * dA_t + dBu_t
                y = jnp.einsum('bdn,bn->bd', h, C_t)
                return (h, y)
            h0 = jnp.zeros((b, d, n), u.dtype)
            _, ys = jax.lax.scan(step, h0, (dA, dBu, Ct))
            y = jnp.moveaxis(ys, 0, 1)
            return y + u * D
        xn = _rmsnorm(x, w_norm)
        xz = xn @ W_in
        xs, res = jnp.split(xz, 2, axis=-1)
        xs = _depthwise_causal_conv(xs, conv_w, conv_b)
        xs = jax.nn.silu(xs)
        A = -jnp.exp(A_log)
        xdbc = xs @ W_xp
        dt_r = xdbc[..., :DT_RANK]
        B = xdbc[..., DT_RANK:DT_RANK + D_STATE]
        C = xdbc[..., DT_RANK + D_STATE:]
        delta = jax.nn.softplus(dt_r @ W_dt + b_dt)
        y = _selective_scan(xs, delta, A, B, C, D)
        y = y * jax.nn.silu(res)
        out = y @ W_out + x
        return out

    def _L0_ffn_ref(x, gate_w, w1, w2, w3, sw1, sw2, sw3):
        import jax, jax.numpy as jnp
        import numpy as np
        B, S, D = (2, 512, 512)
        E, H, TOP_K = (8, 352, 2)
        SH = 352
        ROUTED_SCALE = 2.5
        b, s, d = x.shape
        xt = x.reshape(b * s, d)
        scores = jax.nn.sigmoid(xt @ gate_w.T)
        top_scores, top_idx = jax.lax.top_k(scores, TOP_K)
        top_scores = top_scores / (jnp.sum(top_scores, axis=-1, keepdims=True) + 1e-20)
        top_scores = top_scores * ROUTED_SCALE
        combine = jnp.sum(jax.nn.one_hot(top_idx, E, dtype=xt.dtype) * top_scores[..., None], axis=1)
        h = jnp.einsum('td,edh->eth', xt, w1)
        u = jnp.einsum('td,edh->eth', xt, w3)
        y = jnp.einsum('eth,ehd->etd', jax.nn.silu(h) * u, w2)
        routed = jnp.einsum('etd,te->td', y, combine)
        shared = jax.nn.silu(xt @ sw1) * (xt @ sw3) @ sw2
        return (routed + shared).reshape(b, s, d)
    x = L0_attn_x
    x = _layernorm(x + _L0_attn_ref(x, L0_attn_w_norm, L0_attn_W_in, L0_attn_conv_w, L0_attn_conv_b, L0_attn_W_xp, L0_attn_W_dt, L0_attn_b_dt, L0_attn_A_log, L0_attn_D, L0_attn_W_out), axis=-1)
    x = _layernorm(x + _L0_ffn_ref(x, L0_ffn_gate_w, L0_ffn_w1, L0_ffn_w2, L0_ffn_w3, L0_ffn_sw1, L0_ffn_sw2, L0_ffn_sw3), axis=-1)
    return x

_drawn_inputs = setup_inputs


def setup_inputs(seed=0):
    import zlib

    import numpy as np

    out = dict(_drawn_inputs(seed))
    spreads = {'L0_attn_w_norm': (1.0, 0.6),
     'L0_attn_conv_b': (0.0, 0.8),
     'L0_attn_b_dt': (-4.0, 0.6),
     'L0_attn_D': (1.0, 0.6)}
    factors = {'L0_attn_W_in': 3.67,
     'L0_attn_conv_w': 3.874,
     'L0_attn_W_xp': 8.0,
     'L0_attn_W_dt': 8.0,
     'L0_attn_A_log': 8.0,
     'L0_attn_W_out': 3.623}
    for name, (base, spread) in spreads.items():
        noise = np.random.default_rng([zlib.crc32(name.encode()), seed]).standard_normal(out[name].shape)
        drawn = base * np.exp(spread * noise) if base else spread * noise
        out[name] = jnp.asarray(drawn.astype(out[name].dtype))
    for name, factor in factors.items():
        out[name] = (out[name] * factor).astype(out[name].dtype)
    return out
```

```python
from contextlib import ExitStack

import concourse.bass as bass
from concourse import mybir

F32 = mybir.dt.float32
BF16 = mybir.dt.bfloat16
U32 = mybir.dt.uint32
ALU = mybir.AluOpType
ACT = mybir.ActivationFunctionType

P = 128
NB, L, DM = 8, 512, 512
DI, NS, RANK, TAPS = 1024, 16, 128, 4
KC = DM // P
BLK = DI // P
GB = BLK // 2
TT = L // P
EPS = 1e-5
GROUP_STEPS = NS
STEPS = 2 * GROUP_STEPS
SCANS = STEPS * GB
H_RING, DBU_RING = 8, 4
B_CHUNK = 2
B_LOADS = STEPS // B_CHUNK

FIRST_HALF = {
    0: [("fin", 4, -1), ("fin", 5, -1), ("fin", 6, -1), ("fin", 7, -1)],
    1: [("out", 4, -1)],
    2: [("out", 5, -1)],
    3: [("out", 6, -1), ("delta", 4, 0)],
    4: [("out", 7, -1), ("delta", 5, 0)],
    5: [("res", 4, 0), ("delta", 6, 0)],
    6: [("res", 5, 0), ("delta", 7, 0)],
    7: [("res", 6, 0)],
    8: [("res", 7, 0)],
    9: [("yt", 4, 0), ("yt", 5, 0), ("xt", 0, 1), ("xt", 1, 1)],
    10: [("yt", 6, 0), ("yt", 7, 0)],
    11: [("xt", 2, 1), ("xt", 3, 1)],
    12: [("u", 0, 1)],
    13: [("u", 1, 1)],
    14: [("u", 2, 1)],
    15: [("u", 3, 1)],
}
SECOND_HALF = {
    0: [("u", 4, 1), ("fin", 0, 0)],
    1: [("u", 5, 1), ("fin", 1, 0)],
    2: [("u", 6, 1), ("fin", 2, 0)],
    3: [("u", 7, 1), ("fin", 3, 0)],
    4: [("out", 0, 0)],
    5: [("dt_begin", 0, 1)],
    6: [("dt", 0, 1)],
    7: [("bc_begin", 0, 1)],
    8: [("bc", 0, 1)],
    9: [("delta", 0, 1), ("ct", 0, 1), ("out", 1, 0)],
    10: [("delta", 1, 1), ("out", 2, 0)],
    11: [("delta", 2, 1), ("out", 3, 0)],
    12: [("delta", 3, 1), ("res", 0, 1)],
    13: [("res", 1, 1), ("yt", 0, 1)],
    14: [("res", 2, 1), ("yt", 1, 1), ("yt", 2, 1)],
    15: [("res", 3, 1), ("yt", 3, 1)],
}
JOBS_AT = {**FIRST_HALF, **{k + GROUP_STEPS: v for k, v in SECOND_HALF.items()}}
PER_SEQ = {"xt": TT, "u": BLK, "dt": 1, "bc": 1, "ct": 1, "delta": BLK, "res": BLK, "yt": BLK,
           "fin": BLK, "out": BLK}
_ORDER = [(kind, i) for k in sorted(JOBS_AT) for kind, i, _ in JOBS_AT[k] if kind not in ("dt", "bc")]
BANK_OF = {(kind.removesuffix("_begin"), i): n % 2 for n, (kind, i) in enumerate(_ORDER)}
SQUARE_AT = {7: (0, 1), 10: (2, 3)}
SCALE_AT = {8: (0, 1), 11: (2, 3)}
SILU_U_AT = {GROUP_STEPS: 0, GROUP_STEPS + 4: 1}
SILU_RES_AT = {1: 0, 10: 1}
LAYERNORM_AT = 6

NTOK = NB * L
NT = NTOK // P
E, TOPK, HID = 8, 2, 352
SCALE, NORM_EPS = 2.5, 1e-20
HC = [(lo, min(lo + P, HID)) for lo in range(0, HID, P)]
RING = 4
MOE_TILES = -(-(TOPK * NTOK // P + E - 1) // RING) * RING
LIST_ROWS = MOE_TILES * P


def jobs_at(step, first, last):
    return [(k, i, d) for k, i, d in JOBS_AT.get(step, []) if not (first and d < 0) and not (last and d > 0)]


def finished(jobs):
    return [job for job in jobs if not job[0].endswith("_begin")]


PROLOGUE = [(k, i, 1) for s in sorted(JOBS_AT) for k, i, d in JOBS_AT[s] if d > 0]
EPILOGUE = [(k, i, -1) for s in sorted(JOBS_AT) for k, i, d in JOBS_AT[s] if d < 0]


def snap(eng, v):
    return v if isinstance(v, int) else eng.snap(v)


def mamba(nc, t, counters):
    ctx = ExitStack()
    with ctx:
        def sb(name, shape, dt=F32):
            return ctx.enter_context(nc.sbuf_tensor(name, shape, dt))

        def sem(name):
            return counters.enter_context(nc.semaphore(name))

        w_in = sb("w_in", [P, KC, 2 * DI])
        w_xp = sb("w_xp", [P, BLK, RANK + 2 * NS])
        w_dt = sb("w_dt", [P, DI])
        w_out = sb("w_out", [P, BLK, DM])
        w_norm = sb("w_norm", [P, KC])
        conv_w = sb("conv_w", [P, BLK, TAPS])
        conv_b = sb("conv_b", [P, BLK])
        b_dt = sb("b_dt", [P, BLK])
        skip = sb("skip", [P, BLK])
        a_neg = sb("a_neg", [P, BLK, NS])
        ident = sb("ident", [P, P])
        diag_d = sb("diag_d", [P, BLK, P])
        minus_half = sb("minus_half", [P, TT])
        x_in = sb("x_in", [P, 2, DM])
        x_sq = sb("x_sq", [P, TT])
        x_rstd = sb("x_rstd", [P, TT])
        xn_t = sb("xn_t", [P, KC, L])
        u = sb("u", [P, BLK, L])
        dt_r = sb("dt_r", [P, L])
        bc_t = sb("bc_t", [2 * NS, L])
        c_next = sb("c_next", [P, TT, NS])
        c_now = sb("c_now", [P, TT, NS])
        softp = sb("softp", [P, 2, L])
        delta = sb("delta", [P, BLK, L])
        du = sb("du", [P, BLK, L])
        sres = sb("sres", [P, BLK, L])
        y_t = sb("y_t", [P, 2, TT, GB * P])
        b_bc = sb("b_bc", [P, 2, B_CHUNK, L])
        dbu = sb("dbu", [P, DBU_RING, L])
        h = sb("h", [P, H_RING, L])
        acc = sb("acc", [P, TT, DM])
        x_re = sb("x_re", [P, 2, DM])
        stats = sb("stats", [P, TT, 6])
        ln_both = sb("ln_both", [P, TT, 2])
        ln_gap = sb("ln_gap", [P, TT])
        ln_var = sb("ln_var", [P, TT])
        ln_rstd = sb("ln_rstd", [P, TT])
        ln_shift = sb("ln_shift", [P, TT])

        ps = [ctx.enter_context(nc.psum_tensor(f"ps{i}", [P, 512], F32)) for i in range(8)]
        ht_ps, da_ps, job_ps = ps[0:4], ps[4:6], ps[6:8]

        small = ["a_neg", "w_norm", "conv_w", "conv_b", "b_dt", "skip"]
        small_loaded = sem("small_loaded")
        big = ["w_in", "w_xp", "w_dt", "w_out"]
        loaded = {n: sem(f"loaded_{n}") for n in big}
        filled = {k: sem(f"filled_{k}") for k in PER_SEQ}
        taken = {k: sem(f"taken_{k}") for k in PER_SEQ}
        x_loaded = [sem(f"x_loaded{i}") for i in range(2)]
        re_loaded = [sem(f"re_loaded{i}") for i in range(2)]
        b_loaded = [sem(f"b_loaded{i}") for i in range(2)]
        x1_stored = sem("x1_stored")
        b_stored = sem("b_stored")
        ident_zeroed, ident_made, half_made = sem("ident_zeroed"), sem("ident_made"), sem("half_made")
        norm_folded, a_exped, a_made, diag_made = sem("norm_folded"), sem("a_exped"), sem("a_made"), sem("diag_made")
        x_squared, x_meaned, x_rooted, x_scaled = sem("x_squared"), sem("x_meaned"), sem("x_rooted"), sem("x_scaled")
        tap_made, conv_step, u_made = sem("tap_made"), sem("conv_step"), sem("u_made")
        abs_made, exp_made, ln_made, delta_made = sem("abs_made"), sem("exp_made"), sem("ln_made"), sem("delta_made")
        w_made, back_made, lost_made, lost_added, ln_held = sem("w_made"), sem("back_made"), sem("lost_made"), sem("lost_added"), sem("ln_held")
        du_made, res_made = sem("du_made"), sem("res_made")
        c_copied = sem("c_copied")
        da_made, dbu_made, scanned, turned, summed = sem("da_made"), sem("dbu_made"), sem("scanned"), sem("turned"), sem("summed")
        stats_made, ln_step, ln_biased, ln_rooted, shift_made, x1_made = (
            sem("stats_made"), sem("ln_step"), sem("ln_biased"), sem("ln_rooted"), sem("shift_made"), sem("x1_made"))
        block = ctx.enter_context(nc.Block())

        dram = {"w_in": w_in, "w_xp": w_xp, "w_dt": w_dt, "w_out": w_out, "w_norm": w_norm,
                "conv_w": conv_w, "conv_b": conv_b, "b_dt": b_dt, "skip": skip, "a_neg": a_neg}

        def sequences(eng, body):
            body(0, True, False)
            with eng.Fori(1, NB - 1) as b:
                body(b, False, False)
            body(NB - 1, False, True)

        @block.sync
        def _(sp):
            for n in small:
                sp.dma_start(dram[n][:], t[n]).then_inc(small_loaded, 16)

            def load_x(b, i):
                row = snap(sp, b * L + i * P)
                if not (isinstance(b, int) and b == 0 and i < 2):
                    sp.wait_ge(filled["xt"], TT * b + i - 1)
                sp.dma_start(x_in[:, i % 2, :], t["x"][bass.ds(row, P), :]).then_inc(x_loaded[i % 2], 16)

            def load_re(b, i):
                row = snap(sp, b * L + i * P)
                if not (isinstance(b, int) and b == 0 and i < 2):
                    if i < 2:
                        sp.wait_ge(taken["out"], BLK * (b - 1) + i + 3)
                    else:
                        sp.wait_ge(taken["out"], BLK * b + i - 1)
                sp.dma_start(x_re[:, i % 2, :], t["x"][bass.ds(row, P), :]).then_inc(re_loaded[i % 2], 16)

            def load_b(b, c, begin):
                row = snap(sp, b * NS + (c * B_CHUNK) % NS)
                stored = snap(sp, 16 * b + 16)
                freed = snap(sp, SCANS * b + GB * B_CHUNK * (c - 1))
                if c == 0 or begin:
                    sp.wait_ge(b_stored, stored)
                if not (begin and c < 2):
                    sp.wait_ge(dbu_made, freed)
                src = t["b_rows"][bass.ds(row, B_CHUNK), :]
                sp.dma_start(b_bc[:, c % 2], src.partition_broadcast(P)).then_inc(b_loaded[c % 2], 16)

            def store_b(b):
                row = snap(sp, b * NS)
                sp.wait_ge(taken["bc"], b + 1)
                sp.dma_start(t["b_rows"][bass.ds(row, NS), :], bc_t[0:NS, :]).then_inc(b_stored, 16)

            def store_x1(b):
                for i in range(TT):
                    row = snap(sp, b * L + i * P)
                    sp.wait_ge(x1_made, TT * b + i + 1)
                    sp.dma_start(t["x1"][bass.ds(row, P), :], acc[:, i, :]).then_inc(x1_stored, 16)

            for i in range(2):
                load_x(0, i)
            for n in big:
                sp.dma_start(dram[n][:], t[n]).then_inc(loaded[n], 16)
            for i in range(2, TT):
                load_x(0, i)
            store_b(0)
            load_b(0, 0, True)

            def body(b, first, last):
                for k in range(STEPS):
                    if k % 2 == 0:
                        c = k // 2 + 1
                        if c < B_LOADS:
                            load_b(b, c, first)
                        elif not last:
                            load_b(b + 1, 0, False)
                    if k == LAYERNORM_AT and not first:
                        store_x1(b - 1)
                    if k in (2, 9) and not last:
                        for i in (0, 1) if k == 2 else (2, 3):
                            load_x(b + 1, i)
                    if k in (14, 15, 21, 26):
                        load_re(b, (14, 15, 21, 26).index(k))
                    if k == 25 and not last:
                        store_b(b + 1)

            sequences(sp, body)
            store_x1(NB - 1)
            sp.wait_ge(x1_stored, 16 * TT * NB)

        @block.gpsimd
        def _(pool):
            pool.memset(ident[:], 0.0).then_inc(ident_zeroed, 1)
            pool.memset(minus_half[:], -0.5).then_inc(half_made, 1)
            pool.wait_ge(ident_zeroed, 1)
            pool.affine_select(out=ident[:], in_=ident[:], compare_op=ALU.not_equal, fill=1.0, base=0,
                               pattern=[[-1, P]], channel_multiplier=1).then_inc(ident_made, 1)

            pool.wait_ge(half_made, 1)

            def x_root(b, i):
                pool.wait_ge(x_meaned, TT * b + i + 1)
                pool.tensor_tensor(x_rstd[:, i:i + 1], x_sq[:, i:i + 1], minus_half[:, 0:1], ALU.pow).then_inc(x_rooted, 1)

            def make_lost(b, i):
                pool.wait_ge(back_made, BLK * b + i + 1)
                pool.tensor_tensor(softp[:, i % 2], softp[:, i % 2], du[:, i], ALU.subtract).then_inc(lost_made, 1)
                pool.wait_ge(lost_made, BLK * b + i + 1)
                pool.tensor_tensor(delta[:, i], delta[:, i], softp[:, i % 2], ALU.add).then_inc(lost_added, 1)

            def make_delta(b, i):
                pool.wait_ge(ln_held, BLK * b + i + 1)
                pool.tensor_tensor(delta[:, i], delta[:, i], softp[:, i % 2], ALU.add).then_inc(delta_made, 1)

            def make_du(b, i):
                pool.wait_ge(delta_made, BLK * b + i + 1)
                pool.wait_ge(u_made, 2 * b + i // GB + 1)
                pool.tensor_tensor(du[:, i], delta[:, i], u[:, i], ALU.mult).then_inc(du_made, 1)

            def ln_root(b):
                pool.wait_ge(ln_biased, b + 1)
                if not (isinstance(b, int) and b == 0):
                    pool.wait_ge(x1_made, TT * b)
                pool.tensor_tensor(ln_rstd[:], ln_var[:], minus_half[:], ALU.pow).then_inc(ln_rooted, 1)

            def consume(b, jobs):
                for kind, i, d in jobs:
                    if kind == "delta":
                        make_lost(b + d, i)
                for kind, i, d in jobs:
                    if kind == "delta":
                        make_delta(b + d, i)
                for kind, i, d in jobs:
                    if kind == "delta":
                        make_du(b + d, i)

            for i in range(TT):
                x_root(0, i)
            for job in PROLOGUE:
                consume(-1, [job])

            def body(b, first, last):
                for k in range(STEPS):
                    g, n = k // GROUP_STEPS, k % GROUP_STEPS
                    if k % B_CHUNK == 0:
                        c = k // B_CHUNK
                        pool.wait_ge(b_loaded[c % 2], 16 * (B_LOADS // 2 * b + c // 2 + 1))
                    if n == 0:
                        pool.wait_ge(du_made, BLK * b + GB * (g + 1))
                    for j in range(GB):
                        s = GB * k + j
                        if not (first and s < DBU_RING):
                            pool.wait_ge(scanned, SCANS * b + s - DBU_RING + 1)
                        pool.tensor_tensor(dbu[:, s % DBU_RING], du[:, g * GB + j],
                                           b_bc[:, (k // B_CHUNK) % 2, k % B_CHUNK], ALU.mult).then_inc(dbu_made, 1)

                    if k == 0 and not first:
                        consume(b - 1, jobs_at(STEPS - 1, False, False))
                    if k > 0:
                        consume(b, jobs_at(k - 1, first, last))
                    if not last:
                        for i in SQUARE_AT.get(k, ()):
                            x_root(b + 1, i)
                    if k == LAYERNORM_AT and not first:
                        ln_root(b - 1)

            sequences(pool, body)
            ln_root(NB - 1)

        @block.scalar
        def _(act):
            act.wait_ge(small_loaded, 16 * len(small))
            act.activation(a_neg[:], a_neg[:], ACT.Exp).then_inc(a_exped, 1)

            def square(b, i):
                act.wait_ge(x_loaded[i % 2], 16 * (TT // 2 * b + i // 2 + 1))
                if not (isinstance(b, int) and b == 0):
                    act.wait_ge(x_scaled, TT * (b - 1) + i + 1)
                if not (isinstance(b, int) and b == 0):
                    act.wait_ge(filled["delta"], BLK * b)
                if not (isinstance(b, int) and b == 0 and i == 0):
                    act.wait_ge(x_squared, TT * b + i)
                act.activation(dt_r[:], x_in[:, i % 2], ACT.Square, accum_out=x_sq[:, i:i + 1]).then_inc(x_squared, 1)
                act.wait_ge(x_squared, TT * b + i + 1)
                act.activation(x_sq[:, i:i + 1], x_sq[:, i:i + 1], ACT.Copy, scale=1.0 / DM, bias=EPS).then_inc(x_meaned, 1)

            def scale(b, i):
                act.wait_ge(x_rooted, TT * b + i + 1)
                act.activation(x_in[:, i % 2], x_in[:, i % 2], ACT.Copy, scale=x_rstd[:, i:i + 1]).then_inc(x_scaled, 1)

            def silu_u(b, g):
                act.wait_ge(taken["u"], BLK * b + GB * (g + 1))
                act.activation(u[:, g * GB:(g + 1) * GB], u[:, g * GB:(g + 1) * GB], ACT.Silu).then_inc(u_made, 1)

            def silu_res(b, g):
                act.wait_ge(taken["res"], BLK * b + GB * (g + 1))
                act.activation(sres[:, g * GB:(g + 1) * GB], sres[:, g * GB:(g + 1) * GB], ACT.Silu).then_inc(res_made, 1)

            def consume(b0, jobs):
                for kind, i, d in finished(jobs):
                    b, bank, g = b0 + d, job_ps[BANK_OF[kind, i]], i // GB
                    started = isinstance(b, int) and b == 0
                    if kind in ("xt", "u", "dt", "bc", "delta", "res", "yt"):
                        act.wait_ge(filled[kind], PER_SEQ[kind] * b + i + 1)
                    if kind == "xt":
                        if not started:
                            act.wait_ge(filled["res"], BLK * b)
                            act.wait_ge(filled["u"], BLK * b)
                        act.activation(xn_t[:, :, i * P:(i + 1) * P], bank[:].rearrange("p (c t) -> p c t", c=KC), ACT.Copy).then_inc(taken["xt"], 1)
                    if kind == "u":
                        if not started:
                            act.wait_ge(du_made, BLK * (b - 1) + i + 1)
                            act.wait_ge(filled["yt"], BLK * (b - 1) + GB * (g + 1))
                            act.wait_ge(filled["bc"], b)
                        act.activation(u[:, i], bank[:], ACT.Identity, scale=conv_w[:, i, TAPS - 1:TAPS],
                                       bias=conv_b[:, i:i + 1]).then_inc(tap_made, 1)
                    if kind == "dt":
                        if not started:
                            act.wait_ge(filled["delta"], BLK * b)
                        act.wait_ge(x_squared, TT * b + TT)
                        act.activation(dt_r[:], bank[:], ACT.Copy).then_inc(taken["dt"], 1)
                    if kind == "bc":
                        if not started:
                            act.wait_ge(filled["ct"], b)
                            act.wait_ge(b_stored, 16 * b)
                        act.activation(bc_t[:], bank[0:2 * NS, :], ACT.Copy).then_inc(taken["bc"], 1)
                    if kind == "delta":
                        if not (started and i < 2):
                            act.wait_ge(delta_made, BLK * b + i - 1)
                        act.activation(softp[:, i % 2], bank[:], ACT.Abs, bias=b_dt[:, i:i + 1]).then_inc(abs_made, 1)
                        if not started:
                            act.wait_ge(da_made, SCANS * (b - 1) + GROUP_STEPS * GB * (g + 1))
                            act.wait_ge(du_made, BLK * (b - 1) + i + 1)
                        act.activation(delta[:, i], bank[:], ACT.Relu, bias=b_dt[:, i:i + 1]).then_inc(taken["delta"], 1)
                        act.wait_ge(abs_made, BLK * b + i + 1)
                        act.activation(softp[:, i % 2], softp[:, i % 2], ACT.Exp, scale=-1.0).then_inc(exp_made, 1)
                        if not started:
                            act.wait_ge(dbu_made, SCANS * (b - 1) + GROUP_STEPS * GB * (g + 1))
                        act.wait_ge(exp_made, BLK * b + i + 1)
                        act.activation(du[:, i], softp[:, i % 2], ACT.Identity, bias=1.0).then_inc(w_made, 1)
                        act.wait_ge(w_made, BLK * b + i + 1)
                        act.activation(du[:, i], du[:, i], ACT.Identity, bias=-1.0).then_inc(back_made, 1)
                    if kind == "res":
                        if not started:
                            act.wait_ge(filled["out"], BLK * (b - 1) + GB * (g + 1))
                        act.activation(sres[:, i], bank[:], ACT.Copy).then_inc(taken["res"], 1)
                    if kind == "yt":
                        if not started:
                            act.wait_ge(filled["fin"], BLK * (b - 1) + GB * (g + 1))
                        act.activation(y_t[:, g, i % GB], bank[:], ACT.Copy).then_inc(taken["yt"], 1)
                for kind, i, d in jobs:
                    if kind == "delta":
                        act.wait_ge(lost_added, BLK * (b0 + d) + i + 1)
                        act.activation(softp[:, i % 2], du[:, i], ACT.Ln, bias=1.0).then_inc(ln_made, 1)

            def layernorm(b):
                act.wait_ge(shift_made, b + 1)
                for i in range(TT):
                    act.activation(acc[:, i], acc[:, i], ACT.Identity, scale=ln_rstd[:, i:i + 1],
                                   bias=ln_shift[:, i:i + 1]).then_inc(x1_made, 1)

            def decay(b, s, first):
                k, j = s // GB, s % GB
                g, n = k // GROUP_STEPS, k % GROUP_STEPS
                blk = g * GB + j
                if n == 0:
                    act.wait_ge(delta_made, BLK * b + blk + 1)
                if not (first and s < 2):
                    act.wait_ge(scanned, SCANS * b + s - 1)
                act.activation(da_ps[s % 2][:], delta[:, blk], ACT.Exp, scale=a_neg[:, blk, n:n + 1]).then_inc(da_made, 1)

            for i in range(2):
                square(0, i)
            for i in range(2):
                scale(0, i)
            for kind, i, d in PROLOGUE:
                if (kind, i) == ("xt", 2):
                    for ii in (2, 3):
                        square(0, ii)
                    for ii in (2, 3):
                        scale(0, ii)
                consume(-1, [(kind, i, d)])
                if (kind, i) == ("u", BLK - 1):
                    silu_u(0, 0)
                    silu_u(0, 1)
            act.wait_ge(a_made, 1)
            decay(0, 0, True)
            decay(0, 1, True)

            def body(b, first, last):
                for k in range(STEPS):
                    for s in range(GB * k + 2, GB * k + GB + 2):
                        if s < SCANS:
                            decay(b, s, first)
                        elif not last:
                            decay(b + 1, s - SCANS, False)
                    if k == 0 and not first:
                        consume(b - 1, jobs_at(STEPS - 1, False, False))
                    if k > 0:
                        consume(b, jobs_at(k - 1, first, last))
                    if not last:
                        for i in SQUARE_AT.get(k, ()):
                            square(b + 1, i)
                        for i in SCALE_AT.get(k, ()):
                            scale(b + 1, i)
                        if k in SILU_U_AT:
                            silu_u(b + 1, SILU_U_AT[k])
                    if k in SILU_RES_AT:
                        silu_res(b, SILU_RES_AT[k])
                    if k == LAYERNORM_AT and not first:
                        layernorm(b - 1)

            sequences(act, body)
            layernorm(NB - 1)

        @block.tensor
        def _(pe):
            for n in ("w_xp", "w_dt", "w_out"):
                pe.wait_ge(loaded[n], 16)
            pe.wait_ge(norm_folded, KC)
            pe.wait_ge(ident_made, 1)
            pe.wait_ge(diag_made, BLK)
            bank_user = [None, None]

            def fill(b0, part, i, d):
                kind = part.removesuffix("_begin")
                b, bank, g = b0 + d, job_ps[BANK_OF[kind, i]], i // GB
                user = bank_user[BANK_OF[kind, i]]
                if user is not None and part not in ("dt", "bc", "ct"):
                    k0, i0, d0 = user
                    pe.wait_ge(taken[k0], PER_SEQ[k0] * (b0 + d0) + i0 + 1)
                bank_user[BANK_OF[kind, i]] = (kind, i, d)
                if kind == "xt":
                    pe.wait_ge(x_scaled, TT * b + i + 1)
                    for c in range(KC):
                        last = pe.transpose(bank[:, c * P:(c + 1) * P], x_in[:, i % 2, c * P:(c + 1) * P], ident[:])
                if kind in ("u", "res"):
                    if i == 0:
                        pe.wait_ge(taken["xt"], TT * b + TT)
                    col = (DI if kind == "res" else 0) + i * P
                    for c in range(KC):
                        last = pe.matmul(bank[:], w_in[:, c, col:col + P], xn_t[:, c, :], start=c == 0, stop=c == KC - 1)
                if kind in ("dt", "bc"):
                    if part != kind:
                        pe.wait_ge(u_made, 2 * b + 2)
                    lo, hi = (0, RANK) if kind == "dt" else (RANK, RANK + 2 * NS)
                    for c in range(GB) if part != kind else range(GB, BLK):
                        last = pe.matmul(bank[0:hi - lo, :], w_xp[:, c, lo:hi], u[:, c], start=c == 0, stop=c == BLK - 1)
                if kind == "ct":
                    for c in range(TT):
                        last = pe.transpose(bank[:, c * 2 * NS:(c + 1) * 2 * NS], bc_t[:, c * P:(c + 1) * P],
                                            ident[0:2 * NS, 0:2 * NS])
                if kind == "delta":
                    pe.wait_ge(taken["dt"], b + 1)
                    if i == 0:
                        pe.wait_ge(taken["bc"], b + 1)
                    last = pe.matmul(bank[:], w_dt[:, i * P:(i + 1) * P], dt_r[:], start=True, stop=True)
                if kind == "yt":
                    tt = i % GB
                    for j in range(GB):
                        last = pe.matmul(bank[:, j * P:(j + 1) * P], u[:, g * GB + j, tt * P:(tt + 1) * P],
                                         diag_d[:, g * GB + j], start=True, stop=True)
                if kind == "fin":
                    j = i % GB
                    pe.wait_ge(summed, TT * (STEPS * b + GROUP_STEPS * (g + 1)))
                    for tt in range(TT):
                        last = pe.transpose(bank[:, tt * P:(tt + 1) * P], y_t[:, g, tt, j * P:(j + 1) * P], ident[:])
                if kind == "out":
                    tt = i % GB
                    pe.wait_ge(taken["fin"], BLK * b + GB * (g + 1))
                    for j in range(GB):
                        last = pe.matmul(bank[:], sres[:, g * GB + j, tt * P:(tt + 1) * P], w_out[:, g * GB + j],
                                         start=j == 0, stop=j == GB - 1)
                if part == kind:
                    last.then_inc(filled[kind], 1)

            def rebase():
                for n in range(2):
                    k0, i0, d0 = bank_user[n]
                    bank_user[n] = (k0, i0, d0 - 1)

            for kind, i, d in PROLOGUE:
                fill(-1, kind, i, d)
            rebase()

            def body(b, first, last):
                for k in range(STEPS):
                    for j in range(GB):
                        s = GB * k + j
                        pe.wait_ge(scanned, SCANS * b + s + 1)
                        if j == 0 and not (first and k == 0):
                            pe.wait_ge(summed, TT * (STEPS * b + k))
                        for tt in range(TT):
                            turn = pe.transpose(ht_ps[tt][:, j * P:(j + 1) * P], h[:, s % H_RING, tt * P:(tt + 1) * P], ident[:])
                        turn.then_inc(turned, 1)
                    for kind, i, d in jobs_at(k, first, last):
                        fill(b, kind, i, d)
                rebase()

            sequences(pe, body)
            for kind, i, d in EPILOGUE:
                fill(NB, kind, i, d)

        @block.vector
        def _(dve):
            dve.wait_ge(small_loaded, 16 * len(small))
            dve.wait_ge(loaded["w_in"], 16)
            for c in range(KC):
                dve.tensor_scalar(w_in[:, c], w_in[:, c], w_norm[:, c:c + 1], None, ALU.mult).then_inc(norm_folded, 1)
            dve.wait_ge(a_exped, 1)
            dve.tensor_scalar(a_neg[:], a_neg[:], -1.0, None, ALU.mult).then_inc(a_made, 1)
            dve.wait_ge(ident_made, 1)
            for i in range(BLK):
                dve.tensor_scalar(diag_d[:, i], ident[:], skip[:, i:i + 1], None, ALU.mult).then_inc(diag_made, 1)

            def consume(b0, jobs):
                for kind, i, d in finished(jobs):
                    b, bank, g = b0 + d, job_ps[BANK_OF[kind, i]], i // GB
                    if kind == "u":
                        dve.wait_ge(tap_made, BLK * b + i + 1)
                        for tap in range(1, TAPS):
                            if tap > 1:
                                dve.wait_ge(conv_step, (TAPS - 2) * (BLK * b + i) + tap - 1)
                            add = dve.scalar_tensor_tensor(u[:, i, tap:L], bank[:, 0:L - tap], conv_w[:, i, TAPS - 1 - tap:TAPS - tap],
                                                           u[:, i, tap:L], ALU.mult, ALU.add)
                            if tap < TAPS - 1:
                                add.then_inc(conv_step, 1)
                        add.then_inc(taken["u"], 1)
                    if kind == "delta":
                        dve.wait_ge(ln_made, BLK * b + i + 1)
                        dve.scalar_tensor_tensor(softp[:, i % 2], softp[:, i % 2], 0.0, du[:, i],
                                                 ALU.max, ALU.min).then_inc(ln_held, 1)
                    if kind == "ct":
                        dve.wait_ge(filled["ct"], b + 1)
                        if not (isinstance(b, int) and b == 0):
                            dve.wait_ge(c_copied, b)
                        dve.tensor_copy(c_next[:], bank[:, 0:TT * 2 * NS].rearrange("p (t n) -> p t n", t=TT)[:, :, NS:2 * NS]).then_inc(taken["ct"], 1)
                    if kind == "fin":
                        dve.wait_ge(filled["fin"], BLK * b + i + 1)
                        dve.wait_ge(res_made, 2 * b + (2 if g else 1))
                        dve.tensor_tensor(sres[:, i], bank[:], sres[:, i], ALU.mult).then_inc(taken["fin"], 1)
                    if kind == "out":
                        tt = i % GB
                        dve.wait_ge(filled["out"], BLK * b + i + 1)
                        if g == 0:
                            dve.wait_ge(re_loaded[tt % 2], 16 * (TT // 2 * b + tt // 2 + 1))
                            if not (isinstance(b, int) and b == 0):
                                dve.wait_ge(x1_stored, 16 * TT * b)
                            dve.scalar_tensor_tensor(acc[:, tt], x_re[:, tt % 2], 2.0, bank[:], ALU.mult, ALU.add).then_inc(taken["out"], 1)
                        else:
                            dve.wait_ge(taken["out"], BLK * b + tt + 1)
                            dve.tensor_tensor(acc[:, tt], bank[:], acc[:, tt], ALU.add).then_inc(taken["out"], 1)
                            dve.wait_ge(taken["out"], BLK * b + i + 1)
                            dve.bn_stats(stats[:, tt], acc[:, tt]).then_inc(stats_made, 1)

            def variances(b):
                even, odd = stats[:, :, 1:3], stats[:, :, 4:6]
                dve.wait_ge(stats_made, TT * (b + 1))
                dve.tensor_tensor(ln_both[:], even, odd, ALU.add).then_inc(ln_step, 1)
                dve.tensor_tensor(ln_gap[:], stats[:, :, 1], stats[:, :, 4], ALU.subtract).then_inc(ln_step, 1)
                dve.wait_ge(ln_step, 4 * b + 2)
                dve.tensor_tensor(ln_gap[:], ln_gap[:], ln_gap[:], ALU.mult).then_inc(ln_step, 1)
                dve.wait_ge(ln_step, 4 * b + 3)
                dve.scalar_tensor_tensor(ln_var[:], ln_gap[:], DM / 4.0, ln_both[:, :, 1], ALU.mult, ALU.add).then_inc(ln_step, 1)
                dve.wait_ge(ln_step, 4 * b + 4)
                dve.tensor_scalar(ln_var[:], ln_var[:], 1.0 / DM, EPS, ALU.mult, ALU.add).then_inc(ln_biased, 1)

            def shifts(b):
                dve.wait_ge(ln_rooted, b + 1)
                dve.scalar_tensor_tensor(ln_shift[:], ln_both[:, :, 0], -0.5, ln_rstd[:], ALU.mult, ALU.mult).then_inc(shift_made, 1)

            def sum_states(b, k, first):
                g, n = k // GROUP_STEPS, k % GROUP_STEPS
                if k == 0:
                    dve.wait_ge(taken["ct"], b + 1)
                    if not first:
                        dve.wait_ge(summed, TT * STEPS * b)
                    dve.tensor_copy(c_now[:], c_next[:]).then_inc(c_copied, 1)
                    dve.wait_ge(c_copied, b + 1)
                if n == 0:
                    dve.wait_ge(taken["yt"], BLK * b + GB * (g + 1))
                dve.wait_ge(turned, SCANS * b + GB * (k + 1))
                for tt in range(TT):
                    if n > 0:
                        dve.wait_ge(summed, TT * (STEPS * b + k - 1) + tt + 1)
                    dve.scalar_tensor_tensor(y_t[:, g, tt], ht_ps[tt][:], c_now[:, tt, n:n + 1], y_t[:, g, tt],
                                             ALU.mult, ALU.add).then_inc(summed, 1)

            consume(-1, PROLOGUE)

            def body(b, first, last):
                for k in range(STEPS):
                    for j in range(GB):
                        s = GB * k + j
                        dve.wait_ge(da_made, SCANS * b + s + 1)
                        dve.wait_ge(dbu_made, SCANS * b + s + 1)
                        if not (first and s < H_RING):
                            dve.wait_ge(turned, SCANS * b + s - H_RING + 1)
                        dve.tensor_tensor_scan(h[:, s % H_RING], da_ps[s % 2][:], dbu[:, s % DBU_RING], 0.0,
                                               ALU.mult, ALU.add).then_inc(scanned, 1)
                    if k > 0:
                        sum_states(b, k - 1, first)
                        consume(b, jobs_at(k - 1, first, last))
                    elif not first:
                        sum_states(b - 1, STEPS - 1, False)
                        consume(b - 1, jobs_at(STEPS - 1, False, False))
                    if k == LAYERNORM_AT - 1 and not first:
                        variances(b - 1)
                    if k == LAYERNORM_AT and not first:
                        shifts(b - 1)

            sequences(dve, body)
            sum_states(NB - 1, STEPS - 1, False)
            consume(NB, EPILOGUE)
            variances(NB - 1)
            shifts(NB - 1)


def moe(nc, t, counters):
    ctx = ExitStack()
    with ctx:
        def sb(name, shape, dt=F32):
            return ctx.enter_context(nc.sbuf_tensor(name, shape, dt))

        def sem(name):
            return counters.enter_context(nc.semaphore(name))

        def sems(name, n=RING):
            return [sem(f"{name}{i}") for i in range(n)]

        w13 = sb("w13", [P, E + 1, KC, 2 * HID])
        w2 = sb("w2", [P, E + 1, len(HC), DM])
        gate = sb("gate", [P, KC, E])
        ident = sb("identity", [P, P])
        before = sb("before", [P, P], BF16)
        ones = sb("ones", [P, P], BF16)
        minus_half = sb("minus_halves", [P, 1])
        xg = sb("xg", [P, RING, DM])
        xt = sb("xt", [P, KC, P])
        act_h = sb("act_h", [P, HID])
        gated = sb("gated", [P, HID])
        gt = sb("gt", [P, len(HC), P])
        y = sb("y", [P, 2, DM])
        yg = sb("yg", [P, 2, TOPK, DM])
        scores = sb("scores", [P, NT, E])
        top = sb("top", [P, NT, 8])
        top_at = sb("top_at", [P, NT, 8], U32)
        chosen = sb("chosen", [P, TOPK, NT])
        hot = sb("hot", [P, TOPK, E, NT])
        both = sb("both", [P, E, NT], BF16)
        keep = sb("keep", [P, E, NT])
        former = sb("former", [P, E, NT])
        base = sb("base", [P, E, NT])
        place = sb("place", [P, E, NT])
        dest_f = sb("dest_f", [P, TOPK, NT])
        dest = sb("dest", [P, TOPK, NT], U32)
        total = sb("total", [P, NT])
        share = sb("share", [P, TOPK, NT])
        token = sb("token", [P, NT], U32)
        size = sb("size", [P, E])
        tiles = sb("tiles", [P, E])
        ends = sb("ends", [P, E])
        one_row = sb("one_row", [P, E])
        edge_i = sb("edge_i", [P, NT], U32)
        edge = sb("edge", [P, NT])
        slot_i = sb("slot_i", [P, MOE_TILES], U32)
        slot = sb("slot", [P, MOE_TILES])
        past = sb("past", [P, E, MOE_TILES])
        owner = sb("owner", [P, MOE_TILES])
        starts = sb("starts", [P, E])
        expert = sb("expert", [P, MOE_TILES], U32)
        zero = sb("zero", [P, LIST_ROWS // P], U32)
        put_at = sb("put_at", [P, RING, TOPK], U32)
        put = sb("put", [P, RING], U32)
        got = sb("got", [P, RING], U32)
        take_at = sb("take_at", [P, 2, TOPK], U32)
        stats = sb("row_stats", [P, 2, 6])
        pair = sb("pair", [P, 2, 2])
        gap = sb("gap", [P, 2])
        var = sb("var", [P, 2])
        rstd = sb("rstd", [P, 2])
        shift = sb("shift", [P, 2])

        ps = [ctx.enter_context(nc.psum_tensor(f"moe_ps{i}", [P, 512], F32)) for i in range(7)]
        x_ps, h_ps, u_ps, g_ps, y_ps, route_ps, count_ps = ps

        w_loaded = sem("experts_loaded")
        gate_loaded = sem("gate_loaded")
        rx_loaded, r_turned, r_copied, r_gated, scored = sems("rx_loaded"), sem("r_turned"), sem("r_copied"), sem("r_gated"), sem("scored")
        made = sem("constants_made")
        zeroed, topped, found, routed = sem("zeroed"), sem("topped"), sem("found"), sem("routed")
        both_made, counted, dest_made, rows_made = sem("both_made"), sem("counted"), sem("dest_made"), sem("rows_made")
        table_cleared, put_copied, put_done = sem("table_cleared"), sem("put_copied"), sems("put_done")
        got_loaded, gathered, x_loaded = sems("got_loaded"), sems("gathered"), sems("x_in")
        x_turned, x_copied, upped, h_made, g_made, g_turned, g_copied, downed = (
            sem(n) for n in ("x_turned", "x_copied", "upped", "h_made", "g_made", "g_turned", "g_copied", "downed"))
        y_made, y_stored = sem("y_made"), sems("y_stored", 2)
        take_copied, taken = sem("take_copied"), sems("rows_taken", 2)
        added, row_stated, row_step, row_vared, rooted, shifted, out_made, out_stored = (
            sem("added"), sem("row_stated"), sem("row_step"), sem("row_vared"), sem("rooted"), sem("shifted"), sem("out_made"), sems("out_stored", 2))
        put_ready, gather_ready, take_ready = sem("put_ready"), sem("gather_ready"), sem("take_ready")
        block = ctx.enter_context(nc.Block())

        def rings(eng, n, body):
            turns = n // RING
            body(0, True, False)
            with eng.Fori(1, turns - 1) as r:
                body(r, False, False)
            body(turns - 1, False, True)

        @block.sync
        def _(sp):
            sp.dma_start(gate[:], t["gate"]).then_inc(gate_loaded, 16)

            def load_route(r, first, last):
                for i in range(RING):
                    at = snap(sp, (r * RING + i) * P)
                    if not first:
                        sp.wait_ge(r_turned, RING * (r - 1) + i + 1)
                    sp.dma_start(xg[:, i], t["x1"][bass.ds(at, P), :]).then_inc(rx_loaded[i], 16)

            rings(sp, NT, load_route)
            for e in range(E + 1):
                sp.dma_start(w13[:, e], t["w13"][e]).then_inc(w_loaded, 16)
                sp.dma_start(w2[:, e], t["w2"][e]).then_inc(w_loaded, 16)
            for i in range(RING):
                sp.wait_ge(put_done[i], 16 * TOPK * (NT // RING))

            def load_got(r, first, last):
                for i in range(RING):
                    at = snap(sp, (r * RING + i) * P)
                    if not first:
                        sp.wait_ge(gathered[i], 16 * r)
                    sp.dma_start(got[:, i:i + 1], t["lists"][bass.ds(at, P), :]).then_inc(got_loaded[i], 16)

            rings(sp, MOE_TILES, load_got)

            def load_shared(r, first, last):
                for i in range(RING):
                    at = snap(sp, (r * RING + i) * P)
                    if first:
                        sp.wait_ge(x_turned, MOE_TILES - RING + i + 1)
                    else:
                        sp.wait_ge(added, TOPK * 2 * (RING * (r - 1) + i + 1))
                    sp.dma_start(xg[:, i], t["x1"][bass.ds(at, P), :]).then_inc(x_loaded[i], 16)

            rings(sp, NT, load_shared)

        @block.gpsimd
        def _(pool):
            steps = 0

            def then(ins):
                nonlocal steps
                steps += 1
                ins.then_inc(made, 1)
                pool.wait_ge(made, steps)

            then(pool.memset(zero[:], 0))
            pool.dma_start(t["lists"].rearrange("(p n) a -> p (n a)", p=P), zero[:]).then_inc(table_cleared, 16)
            then(pool.memset(ident[:], 0.0))
            then(pool.affine_select(out=ident[:], in_=ident[:], compare_op=ALU.not_equal, fill=1.0, base=0,
                                    pattern=[[-1, P]], channel_multiplier=1))
            then(pool.memset(before[:], 1.0))
            then(pool.affine_select(out=before[:], in_=before[:], compare_op=ALU.is_gt, fill=0.0, base=0,
                                    pattern=[[1, P]], channel_multiplier=-1))
            then(pool.memset(ones[:], 1.0))
            then(pool.memset(minus_half[:], -0.5))
            then(pool.memset(keep[:], 1.0))
            then(pool.memset(keep[:, :, 0:1], 0.0))
            then(pool.memset(former[:], 0.0))
            then(pool.memset(one_row[:], 1.0))
            then(pool.iota(edge_i[:], pattern=[[P, NT]], base=0, channel_multiplier=0))
            then(pool.iota(slot_i[:], pattern=[[1, MOE_TILES]], base=0, channel_multiplier=0))
            then(pool.iota(token[:], pattern=[[P, NT]], base=0, channel_multiplier=1))
            assert steps == CONSTANTS

            pool.wait_ge(dest_made, 1)
            pool.wait_ge(table_cleared, 16)

            def put_tokens(r, first, last):
                for i in range(RING):
                    if not first:
                        pool.wait_ge(put_done[i], 16 * TOPK * r)
                    pool.tensor_copy(put[:, i:i + 1], token[:, bass.ds(r * RING + i, 1)]).then_inc(put_copied, 1)
                    pool.tensor_copy(put_at[:, i, :], dest[:, :, bass.ds(r * RING + i, 1)]).then_inc(put_copied, 1)
                pool.wait_ge(put_copied, 2 * (RING * r + RING))
                pool.sem_inc(put_ready, 1)
                for i in range(RING):
                    for c in range(TOPK):
                        pool.indirect_dma_start(t["lists"], bass.IndirectOffsetOnAxis(ap=put_at[:, i, c:c + 1], axis=0),
                                                put[:, i:i + 1], None).then_inc(put_done[i], 16)

            rings(pool, NT, put_tokens)

            def gather(r, first, last):
                for i in range(RING):
                    if first:
                        pool.wait_ge(r_turned, NT)
                    else:
                        pool.wait_ge(x_turned, RING * (r - 1) + i + 1)
                    pool.wait_ge(got_loaded[i], 16 * (r + 1))
                    pool.sem_inc(gather_ready, 1)
                    pool.indirect_dma_start(xg[:, i], None, t["x1"],
                                            bass.IndirectOffsetOnAxis(ap=got[:, i:i + 1], axis=0)).then_inc(gathered[i], 16)

            rings(pool, MOE_TILES, gather)

            for n in range(2):
                pool.wait_ge(y_stored[n], 16 * (MOE_TILES // 2))

            def take(r, first, last):
                for i in range(RING):
                    q = RING * r + i
                    if not (first and i < 2):
                        pool.wait_ge(added, TOPK * 2 * (q - 1))
                    pool.tensor_copy(take_at[:, i % 2, :], dest[:, :, bass.ds(q, 1)]).then_inc(take_copied, 1)
                    pool.wait_ge(take_copied, q + 1)
                    pool.sem_inc(take_ready, 1)
                    for c in range(TOPK):
                        pool.indirect_dma_start(yg[:, i % 2, c], None, t["y_rows"],
                                                bass.IndirectOffsetOnAxis(ap=take_at[:, i % 2, c:c + 1], axis=0)).then_inc(taken[i % 2], 16)
                    if not (first and i == 0):
                        root(q - 1, (i - 1) % 2)

            def root(q, n):
                pool.wait_ge(row_vared, q + 1)
                pool.tensor_tensor(rstd[:, n:n + 1], var[:, n:n + 1], minus_half[:], ALU.pow).then_inc(rooted, 1)

            rings(pool, NT, take)
            root(NT - 1, 1)

        @block.tensor
        def _(pe):
            pe.wait_ge(made, CONSTANTS)
            pe.wait_ge(gate_loaded, 16)

            def route(r, first, last):
                for i in range(RING):
                    q = RING * r + i
                    pe.wait_ge(rx_loaded[i], 16 * (r + 1))
                    if not (first and i == 0):
                        pe.wait_ge(r_copied, q)
                    for c in range(KC):
                        turn = pe.transpose(x_ps[:, c * P:(c + 1) * P], xg[:, i, c * P:(c + 1) * P], ident[:])
                    turn.then_inc(r_turned, 1)
                    pe.wait_ge(r_copied, q + 1)
                    if not (first and i == 0):
                        pe.wait_ge(scored, q)
                    for c in range(KC):
                        last_mm = pe.matmul(route_ps[:, 0:E], xt[:, c], gate[:, c], start=c == 0, stop=c == KC - 1)
                    last_mm.then_inc(r_gated, 1)

            rings(pe, NT, route)
            pe.wait_ge(both_made, 1)
            pe.matmul(route_ps[:, 0:E * NT], before[:], both[:].rearrange("p e i -> p (e i)"), start=True, stop=True)
            pe.matmul(count_ps[:, 0:E * NT], ones[:], both[:].rearrange("p e i -> p (e i)"), start=True, stop=True).then_inc(counted, 1)

            def turn_x(q0, r, i):
                pe.wait_ge((x_loaded if q0 else gathered)[i], 16 * (r + 1))
                if not (isinstance(r, int) and q0 + RING * r + i == 0):
                    pe.wait_ge(x_copied, q0 + RING * r + i)
                for c in range(KC):
                    turn = pe.transpose(x_ps[:, c * P:(c + 1) * P], xg[:, i, c * P:(c + 1) * P], ident[:])
                turn.then_inc(x_turned, 1)

            def up(q, e, at_zero):
                pe.wait_ge(x_copied, q + 1)
                if not at_zero:
                    pe.wait_ge(g_made, q)
                for out, lo in ((h_ps, 0), (u_ps, HID)):
                    for c in range(KC):
                        last_mm = pe.matmul(out[:, 0:HID], xt[:, c], w13[:, e, c, lo:lo + HID], start=c == 0, stop=c == KC - 1)
                last_mm.then_inc(upped, 1)

            def turn_g(q, at_zero):
                pe.wait_ge(g_made, q + 1)
                for n, (lo, hi) in enumerate(HC):
                    turn = pe.transpose(g_ps[0:hi - lo, n * P:(n + 1) * P], gated[:, lo:hi], ident[:])
                turn.then_inc(g_turned, 1)

            def down(q, e, at_zero):
                pe.wait_ge(g_copied, q + 1)
                if not at_zero:
                    pe.wait_ge(y_made, q)
                for n, (lo, hi) in enumerate(HC):
                    last_mm = pe.matmul(y_ps[:], gt[0:hi - lo, n], w2[0:hi - lo, e, n], start=n == 0, stop=n == len(HC) - 1)
                last_mm.then_inc(downed, 1)

            pe.wait_ge(w_loaded, 2 * 16 * (E + 1))
            pe.wait_ge(rows_made, 1)

            turn_x(0, 0, 0)

            def experts(r, first, last):
                for i in range(RING):
                    q = RING * r + i
                    here = pe.value_load(expert[0:1, bass.ds(q, 1)], min_val=0, max_val=E - 1)
                    up(q, bass.ds(here, 1), first and i == 0)
                    if i + 1 < RING:
                        turn_x(0, r, i + 1)
                    elif not last:
                        turn_x(0, r + 1, 0)
                    if not (first and i == 0):
                        before_it = pe.value_load(expert[0:1, bass.ds(q - 1, 1)], min_val=0, max_val=E - 1)
                        down(q - 1, bass.ds(before_it, 1), first and i == 1)
                    turn_g(q, first and i == 0)

            rings(pe, MOE_TILES, experts)
            turn_x(MOE_TILES, 0, 0)
            final = pe.value_load(expert[0:1, MOE_TILES - 1:MOE_TILES], min_val=0, max_val=E - 1)
            down(MOE_TILES - 1, bass.ds(final, 1), False)

            def shared(r, first, last):
                for i in range(RING):
                    q = MOE_TILES + RING * r + i
                    up(q, E, False)
                    if i + 1 < RING:
                        turn_x(MOE_TILES, r, i + 1)
                    elif not last:
                        turn_x(MOE_TILES, r + 1, 0)
                    if not (first and i == 0):
                        down(q - 1, E, False)
                    turn_g(q, False)

            rings(pe, NT, shared)
            down(MOE_TILES + NT - 1, E, False)

        @block.scalar
        def _(act):
            def route(r, first, last):
                for i in range(RING):
                    q = RING * r + i
                    act.wait_ge(r_turned, q + 1)
                    if not (first and i == 0):
                        act.wait_ge(r_gated, q)
                    act.activation(xt[:].rearrange("p c t -> p (c t)"), x_ps[:], ACT.Copy).then_inc(r_copied, 1)
                    act.wait_ge(r_gated, q + 1)
                    act.activation(scores[:, bass.ds(q, 1), :], route_ps[:, 0:E], ACT.Sigmoid).then_inc(scored, 1)

            rings(act, NT, route)

            def copy_x(q, at_zero):
                act.wait_ge(x_turned, q + 1)
                if at_zero:
                    act.wait_ge(r_gated, NT)
                else:
                    act.wait_ge(upped, q)
                act.activation(xt[:].rearrange("p c t -> p (c t)"), x_ps[:], ACT.Copy).then_inc(x_copied, 1)

            def silu_h(q, at_zero):
                act.wait_ge(upped, q + 1)
                if not at_zero:
                    act.wait_ge(g_made, q)
                act.activation(act_h[:], h_ps[:, 0:HID], ACT.Silu).then_inc(h_made, 1)

            def give_y(q, n, at, started):
                act.wait_ge(downed, q + 1)
                if started is not None:
                    act.wait_ge(y_stored[n], started)
                act.activation(y[:, n], y_ps[:], ACT.Copy).then_inc(y_made, 1)
                act.wait_ge(y_made, q + 1)
                act.dma_start(t["y_rows"][bass.ds(at, P), :], y[:, n]).then_inc(y_stored[n], 16)

            copy_x(0, True)

            def experts(r, first, last):
                for i in range(RING):
                    q = RING * r + i
                    silu_h(q, first and i == 0)
                    if not (last and i == RING - 1):
                        copy_x(q + 1, False)
                    if not (first and i == 0):
                        at = snap(act, (q - 1) * P)
                        n = (i - 1) % 2
                        uses = 16 * (RING // 2 * r + (i - 1 - n) // 2)
                        give_y(q - 1, n, at, None if first and i < 3 else uses)

            rings(act, MOE_TILES, experts)
            give_y(MOE_TILES - 1, 1, (MOE_TILES - 1) * P, 16 * (MOE_TILES // 2 - 1))
            copy_x(MOE_TILES, False)

            def normalise(q, n, at, started):
                act.wait_ge(shifted, q + 1)
                act.activation(y[:, n], y[:, n], ACT.Identity, scale=rstd[:, n:n + 1], bias=shift[:, n:n + 1]).then_inc(out_made, 1)
                act.wait_ge(out_made, q + 1)
                act.dma_start(t["out"][bass.ds(at, P), :], y[:, n]).then_inc(out_stored[n], 16)

            def shared(r, first, last):
                for i in range(RING):
                    q = RING * r + i
                    silu_h(MOE_TILES + q, False)
                    if not (last and i == RING - 1):
                        copy_x(MOE_TILES + q + 1, False)
                    if not (first and i < 2):
                        at = snap(act, (q - 2) * P)
                        normalise(q - 2, i % 2, at, None)

            rings(act, NT, shared)
            for q in (NT - 2, NT - 1):
                normalise(q, q % 2, q * P, None)
            for n in range(2):
                act.wait_ge(out_stored[n], 16 * (NT // 2))

        @block.vector
        def _(dve):
            steps = 0

            def then(ins):
                nonlocal steps
                steps += 1
                ins.then_inc(routed, 1)
                dve.wait_ge(routed, steps)

            dve.wait_ge(made, CONSTANTS)
            then(dve.tensor_copy(edge[:], edge_i[:]))
            then(dve.tensor_copy(slot[:], slot_i[:]))
            for i in range(NT):
                dve.wait_ge(scored, i + 1)
                dve.max(top[:, i], scores[:, i]).then_inc(topped, 1)
                dve.wait_ge(topped, i + 1)
                dve.max_index(top_at[:, i], top[:, i], scores[:, i]).then_inc(found, 1)
            dve.wait_ge(found, NT)
            then(dve.tensor_copy(chosen[:], top_at[:, :, 0:TOPK].rearrange("p i c -> p c i")))
            for c in range(TOPK):
                for e in range(E):
                    then(dve.tensor_scalar(hot[:, c, e], chosen[:, c], float(e), None, ALU.is_equal))
            dve.tensor_tensor(both[:], hot[:, 0], hot[:, 1], ALU.add).then_inc(both_made, 1)
            then(dve.scalar_tensor_tensor(total[:], top[:, :, 0], NORM_EPS, top[:, :, 1], ALU.add, ALU.add))
            then(dve.reciprocal(total[:], total[:]))
            for c in range(TOPK):
                then(dve.scalar_tensor_tensor(share[:, c], top[:, :, c], SCALE, total[:], ALU.mult, ALU.mult))
            dve.wait_ge(counted, 1)
            counts = count_ps[:, 0:E * NT].rearrange("p (e i) -> p e i", e=E)
            then(dve.tensor_copy(former[:, :, 1:NT], counts[:, :, 0:NT - 1]))
            then(dve.tensor_tensor_scan(base[:].rearrange("p e i -> p (e i)"), keep[:].rearrange("p e i -> p (e i)"),
                                        former[:].rearrange("p e i -> p (e i)"), 0.0, ALU.mult, ALU.add))
            then(dve.tensor_tensor(size[:], base[:, :, NT - 1], counts[:, :, NT - 1], ALU.add))
            for e in range(E):
                then(dve.tensor_scalar(place[:, e], edge[:], size[:, e:e + 1], None, ALU.is_lt))
            then(dve.tensor_reduce(tiles[:], place[:], mybir.AxisListType.X, ALU.add))
            then(dve.tensor_tensor_scan(ends[:], one_row[:], tiles[:], 0.0, ALU.mult, ALU.add))
            then(dve.tensor_tensor(starts[:], ends[:], tiles[:], ALU.subtract))
            then(dve.tensor_scalar(starts[:], starts[:], float(P), None, ALU.mult))
            for e in range(E):
                then(dve.scalar_tensor_tensor(place[:, e], route_ps[:, e * NT:(e + 1) * NT], starts[:, e:e + 1], base[:, e],
                                              ALU.add, ALU.add))
            for c in range(TOPK):
                then(dve.tensor_tensor(hot[:, c], hot[:, c], place[:], ALU.mult))
                then(dve.tensor_reduce(dest_f[:, c], hot[:, c].rearrange("p e i -> p i e"), mybir.AxisListType.X, ALU.add))
            dve.tensor_copy(dest[:], dest_f[:]).then_inc(dest_made, 1)
            for e in range(E):
                then(dve.tensor_scalar(past[:, e], slot[:], ends[:, e:e + 1], None, ALU.is_ge))
            then(dve.tensor_reduce(owner[:], past[:].rearrange("p e s -> p s e"), mybir.AxisListType.X, ALU.add))
            then(dve.tensor_scalar(owner[:], owner[:], float(E - 1), None, ALU.min))
            dve.tensor_copy(expert[:], owner[:]).then_inc(rows_made, 1)

            def gate_u(q, at_zero):
                dve.wait_ge(h_made, q + 1)
                if not at_zero:
                    dve.wait_ge(g_turned, q)
                dve.tensor_tensor(gated[:], u_ps[:, 0:HID], act_h[:], ALU.mult).then_inc(g_made, 1)

            def copy_g(q, at_zero):
                dve.wait_ge(g_turned, q + 1)
                if not at_zero:
                    dve.wait_ge(downed, q)
                tail = HC[-1][1] - HC[-1][0]
                n = len(HC) - 1
                dve.tensor_copy(gt[:, 0:n].rearrange("p n t -> p (n t)"), g_ps[:, 0:n * P])
                dve.tensor_copy(gt[0:tail, n], g_ps[0:tail, n * P:(n + 1) * P]).then_inc(g_copied, 1)

            def experts(r, first, last):
                for i in range(RING):
                    gate_u(RING * r + i, first and i == 0)
                    copy_g(RING * r + i, first and i == 0)

            rings(dve, MOE_TILES, experts)

            def add_up(q, i, begun):
                n = i % 2
                all_q = MOE_TILES + q
                dve.wait_ge(downed, all_q + 1)
                dve.wait_ge(taken[n], 16 * TOPK * ((q - n) // 2 + 1 if isinstance(q, int) else begun + 1))
                if isinstance(q, int) and q < 2:
                    dve.wait_ge(y_stored[n], 16 * (MOE_TILES // 2))
                else:
                    dve.wait_ge(out_stored[n], 16 * ((q - n) // 2) if isinstance(q, int) else 16 * begun)
                dve.tensor_tensor(y[:, n], y_ps[:], xg[:, i], ALU.add).then_inc(y_made, 1)
                dve.wait_ge(y_made, all_q + 1)
                for c in range(TOPK):
                    dve.scalar_tensor_tensor(y[:, n], yg[:, n, c], share[:, c, bass.ds(q, 1)], y[:, n],
                                             ALU.mult, ALU.add).then_inc(added, 2)
                    dve.wait_ge(added, 2 * (TOPK * q + c + 1))
                dve.bn_stats(stats[:, n], y[:, n]).then_inc(row_stated, 1)
                dve.wait_ge(row_stated, q + 1)
                dve.tensor_tensor(pair[:, n], stats[:, n, 1:3], stats[:, n, 4:6], ALU.add).then_inc(row_step, 1)
                dve.tensor_tensor(gap[:, n:n + 1], stats[:, n, 1:2], stats[:, n, 4:5], ALU.subtract).then_inc(row_step, 1)
                dve.wait_ge(row_step, 4 * q + 2)
                dve.tensor_tensor(gap[:, n:n + 1], gap[:, n:n + 1], gap[:, n:n + 1], ALU.mult).then_inc(row_step, 1)
                dve.wait_ge(row_step, 4 * q + 3)
                dve.scalar_tensor_tensor(var[:, n:n + 1], gap[:, n:n + 1], DM / 4.0, pair[:, n, 1:2], ALU.mult, ALU.add).then_inc(row_step, 1)
                dve.wait_ge(row_step, 4 * q + 4)
                dve.tensor_scalar(var[:, n:n + 1], var[:, n:n + 1], 1.0 / DM, EPS, ALU.mult, ALU.add).then_inc(row_vared, 1)

            def shift_of(q, n):
                dve.wait_ge(rooted, q + 1)
                dve.scalar_tensor_tensor(shift[:, n:n + 1], pair[:, n, 0:1], -0.5, rstd[:, n:n + 1], ALU.mult, ALU.mult).then_inc(shifted, 1)

            def shared(r, first, last):
                for i in range(RING):
                    q = RING * r + i
                    gate_u(MOE_TILES + q, False)
                    if not (first and i == 0):
                        add_up(q - 1, (i - 1) % RING, RING // 2 * r + (i - 1) // 2)
                    copy_g(MOE_TILES + q, False)
                    if not (first and i == 0):
                        shift_of(q - 1, (i - 1) % 2)

            rings(dve, NT, shared)
            add_up(NT - 1, RING - 1, NT // 2 - 1)
            shift_of(NT - 1, 1)


CONSTANTS = 14


def kernel(**inputs):
    import numpy as np
    import concourse.bacc as bacc
    from concourse.bass_utils import run_bass_kernel_spmd

    v = {n.removeprefix("L0_attn_").removeprefix("L0_"): np.asarray(a) for n, a in inputs.items()}

    def rows(a):
        return np.ascontiguousarray(a.reshape(-1, P, a.shape[-1]).transpose(1, 0, 2))

    def column(a):
        return np.ascontiguousarray(a.reshape(-1, P).T)

    arrays = {
        "x": np.ascontiguousarray(v["x"].reshape(NB * L, DM)),
        "w_in": rows(v["W_in"]), "w_xp": rows(v["W_xp"]), "w_dt": np.ascontiguousarray(v["W_dt"]),
        "w_out": rows(v["W_out"]), "w_norm": column(v["w_norm"]),
        "conv_w": rows(np.ascontiguousarray(v["conv_w"].T)), "conv_b": column(v["conv_b"]),
        "b_dt": column(v["b_dt"]), "skip": column(v["D"]), "a_neg": rows(v["A_log"]),
        "gate": rows(np.ascontiguousarray(v["ffn_gate_w"].T)),
    }
    both = np.concatenate([np.concatenate([v["ffn_w1"], v["ffn_sw1"][None]]), np.concatenate([v["ffn_w3"], v["ffn_sw3"][None]])], 2)
    down = np.concatenate([v["ffn_w2"], v["ffn_sw2"][None]])
    padded = np.zeros((E + 1, len(HC) * P, DM), down.dtype)
    padded[:, :HID] = down
    arrays |= {
        "w13": np.ascontiguousarray(both.reshape(E + 1, KC, P, 2 * HID).transpose(0, 2, 1, 3)),
        "w2": np.ascontiguousarray(padded.reshape(E + 1, len(HC), P, DM).transpose(0, 2, 1, 3)),
    }
    nc = bacc.Bacc("TRN2", target_bir_lowering=False, num_devices=1)
    t = {n: nc.dram_tensor(n + "_dram", a.shape, mybir.dt.from_np(a.dtype), kind="ExternalInput").ap()
         for n, a in arrays.items()}
    t["b_rows"] = nc.dram_tensor("b_rows_dram", (NB * NS, L), F32, kind="Internal").ap()
    t["x1"] = nc.dram_tensor("x1_dram", (NTOK, DM), F32, kind="Internal").ap()
    t["y_rows"] = nc.dram_tensor("y_rows_dram", (LIST_ROWS, DM), F32, kind="Internal").ap()
    t["lists"] = nc.dram_tensor("lists_dram", (LIST_ROWS, 1), U32, kind="Internal").ap()
    t["out"] = nc.dram_tensor("out_dram", (NTOK, DM), F32, kind="ExternalOutput").ap()
    with ExitStack() as counters:
        mamba(nc, t, counters)
        moe(nc, t, counters)
    r = run_bass_kernel_spmd(nc, [{n + "_dram": a for n, a in arrays.items()}], core_ids=[0])
    return r.results[0]["out_dram"].reshape(NB, L, DM)
```

```python
from contextlib import ExitStack

import concourse.bass as bass
from concourse import mybir

F32 = mybir.dt.float32
BF16 = mybir.dt.bfloat16
U32 = mybir.dt.uint32
ALU = mybir.AluOpType
ACT = mybir.ActivationFunctionType

P = 128
NB, L, DM = 8, 512, 512
DI, NS, RANK, TAPS = 1024, 16, 128, 4
KC = DM // P
BLK = DI // P
GB = BLK // 2
TT = L // P
EPS = 1e-5
GROUP_STEPS = NS
STEPS = 2 * GROUP_STEPS
SCANS = STEPS * GB
H_RING, DBU_RING, SOFTP_RING = 8, 4, 4
B_CHUNK = 1
B_LOADS = STEPS // B_CHUNK

FIRST_HALF = {
    0: [("fin", 4, -1), ("fin", 5, -1), ("fin", 6, -1), ("fin", 7, -1)],
    1: [("out", 4, -1)],
    2: [("out", 5, -1), ("delta", 4, 0)],
    3: [("out", 6, -1)],
    4: [("out", 7, -1), ("delta", 5, 0)],
    5: [("res", 4, 0)],
    6: [("res", 5, 0), ("delta", 6, 0)],
    7: [("res", 6, 0)],
    8: [("res", 7, 0), ("delta", 7, 0)],
    9: [("xt", 0, 1), ("xt", 1, 1), ("xt", 2, 1), ("xt", 3, 1), ("yt", 4, 0)],
    10: [("u", 0, 1), ("yt", 5, 0)],
    11: [("u", 1, 1), ("yt", 6, 0)],
    12: [("u", 2, 1), ("yt", 7, 0)],
    13: [("u", 3, 1)],
    14: [("u", 4, 1)],
    15: [("u", 5, 1)],
}
SECOND_HALF = {
    0: [("u", 6, 1), ("fin", 0, 0)],
    1: [("u", 7, 1), ("fin", 1, 0)],
    2: [("fin", 2, 0), ("fin", 3, 0), ("dt_begin", 0, 1)],
    3: [("out", 0, 0)],
    4: [("dt", 0, 1)],
    5: [("out", 1, 0), ("delta", 0, 1)],
    6: [("delta", 1, 1), ("out", 2, 0)],
    7: [("delta", 2, 1), ("out", 3, 0)],
    8: [("delta", 3, 1), ("bc_begin", 0, 1)],
    9: [("bc", 0, 1)],
    10: [("res", 0, 1), ("ct", 0, 1)],
    11: [("res", 1, 1), ("yt", 0, 1)],
    12: [("res", 2, 1), ("yt", 1, 1)],
    13: [("res", 3, 1), ("yt", 2, 1)],
    14: [("yt", 3, 1)],
}
JOBS_AT = {**FIRST_HALF, **{k + GROUP_STEPS: v for k, v in SECOND_HALF.items()}}
PER_SEQ = {"xt": TT, "u": BLK, "dt": 1, "bc": 1, "ct": 1, "delta": BLK, "res": BLK, "yt": BLK,
           "fin": BLK, "out": BLK}
_ORDER = [(kind, i) for k in sorted(JOBS_AT) for kind, i, _ in JOBS_AT[k] if kind not in ("dt", "bc")]
BANK_OF = {(kind.removesuffix("_begin"), i): n % 2 for n, (kind, i) in enumerate(_ORDER)}
SQUARE_AT, X_ROOT_AT, SCALE_AT = 2, 3, 4
SILU_U_AT = {15: 0, 19: 1}
SILU_RES_AT = {13: 0, 17: 1}
LOST_AT = {4: [(4, 0)], 6: [(5, 0)], 8: [(6, 0)], 10: [(7, 0)],
           23: [(0, 1)], 24: [(1, 1)], 25: [(2, 1)], 26: [(3, 1)]}
LN_AT = {6: [(4, 0), (5, 0)], 11: [(6, 0), (7, 0)], 26: [(0, 1), (1, 1)], 28: [(2, 1), (3, 1)]}
HOLD_AT = {7: [(4, 0), (5, 0)], 12: [(6, 0), (7, 0)], 27: [(0, 1), (1, 1)], 29: [(2, 1), (3, 1)]}
MADE_AT = {8: [(4, 0)], 9: [(5, 0)], 13: [(6, 0)], 14: [(7, 0)],
           28: [(0, 1)], 29: [(1, 1)], 30: [(2, 1)], 31: [(3, 1)]}
VARIANCE_AT, LN_ROOT_AT, SHIFT_AT, LAYERNORM_AT = 5, 6, 6, 8

NTOK = NB * L
NT = NTOK // P
E, TOPK, HID = 8, 2, 352
SCALE, NORM_EPS = 2.5, 1e-20
HC = [(lo, min(lo + P, HID)) for lo in range(0, HID, P)]
RING = 4
MOE_TILES = -(-(TOPK * NTOK // P + E - 1) // RING) * RING
LIST_ROWS = MOE_TILES * P


def jobs_at(step, first, last):
    return [(k, i, d) for k, i, d in JOBS_AT.get(step, []) if not (first and d < 0) and not (last and d > 0)]


def stages_at(table, step, last):
    return [(i, d) for i, d in table.get(step, []) if not (last and d > 0)]


def finished(jobs):
    return [job for job in jobs if not job[0].endswith("_begin")]


PROLOGUE = [(k, i, 1) for s in sorted(JOBS_AT) for k, i, d in JOBS_AT[s] if d > 0]
EPILOGUE = [(k, i, -1) for s in sorted(JOBS_AT) for k, i, d in JOBS_AT[s] if d < 0]


def snap(eng, v):
    return v if isinstance(v, int) else eng.snap(v)


def mamba(nc, t, counters):
    ctx = ExitStack()
    with ctx:
        def sb(name, shape, dt=F32):
            return ctx.enter_context(nc.sbuf_tensor(name, shape, dt))

        def sem(name):
            return counters.enter_context(nc.semaphore(name))

        w_in = sb("w_in", [P, KC, 2 * DI])
        w_xp = sb("w_xp", [P, BLK, RANK + 2 * NS])
        w_dt = sb("w_dt", [P, DI])
        w_out = sb("w_out", [P, BLK, DM])
        w_norm = sb("w_norm", [P, KC])
        conv_w = sb("conv_w", [P, BLK, TAPS])
        conv_b = sb("conv_b", [P, BLK])
        b_dt = sb("b_dt", [P, BLK])
        skip = sb("skip", [P, BLK])
        a_neg = sb("a_neg", [P, BLK, NS])
        ident = sb("ident", [P, P])
        diag_d = sb("diag_d", [P, BLK, P])
        minus_half = sb("minus_half", [P, TT])
        x_in = sb("x_in", [P, TT, DM])
        x_sq = sb("x_sq", [P, TT])
        x_rstd = sb("x_rstd", [P, TT])
        xn_t = sb("xn_t", [P, KC, L])
        u = sb("u", [P, BLK, L])
        dt_r = sb("dt_r", [P, L])
        bc_t = sb("bc_t", [2 * NS, L])
        c_next = sb("c_next", [P, TT, NS])
        c_now = sb("c_now", [P, TT, NS])
        softp = sb("softp", [P, SOFTP_RING, L])
        delta = sb("delta", [P, BLK, L])
        du = sb("du", [P, BLK, L])
        sres = sb("sres", [P, BLK, L])
        y_t = sb("y_t", [P, 2, TT, GB * P])
        b_bc = sb("b_bc", [P, 2, B_CHUNK, L])
        dbu = sb("dbu", [P, DBU_RING, L])
        h = sb("h", [P, H_RING, L])
        acc = sb("acc", [P, TT, DM])
        stats = sb("stats", [P, TT, 6])
        ln_both = sb("ln_both", [P, TT, 2])
        ln_gap = sb("ln_gap", [P, TT])
        ln_var = sb("ln_var", [P, TT])
        ln_rstd = sb("ln_rstd", [P, TT])
        ln_shift = sb("ln_shift", [P, TT])

        ps = [ctx.enter_context(nc.psum_tensor(f"ps{i}", [P, 512], F32)) for i in range(8)]
        ht_ps, da_ps, job_ps = ps[0:4], ps[4:6], ps[6:8]

        small = ["a_neg", "w_norm", "conv_w", "conv_b", "b_dt", "skip"]
        small_loaded = sem("small_loaded")
        big = ["w_in", "w_xp", "w_dt", "w_out"]
        loaded = {n: sem(f"loaded_{n}") for n in big}
        filled = {k: sem(f"filled_{k}") for k in PER_SEQ}
        taken = {k: sem(f"taken_{k}") for k in PER_SEQ}
        x_loaded = sem("x_loaded")
        re_loaded = sem("re_loaded")
        b_loaded = [sem(f"b_loaded{i}") for i in range(2)]
        x1_stored = sem("x1_stored")
        b_stored = sem("b_stored")
        ident_zeroed, ident_made, half_made = sem("ident_zeroed"), sem("ident_made"), sem("half_made")
        norm_folded, a_exped, a_made, diag_made = sem("norm_folded"), sem("a_exped"), sem("a_made"), sem("diag_made")
        x_squared, x_meaned, x_rooted, x_scaled = sem("x_squared"), sem("x_meaned"), sem("x_rooted"), sem("x_scaled")
        tap_made, conv_step, u_made = sem("tap_made"), sem("conv_step"), sem("u_made")
        abs_made, exp_made, ln_made, delta_made = sem("abs_made"), sem("exp_made"), sem("ln_made"), sem("delta_made")
        w_made, back_made, lost_made, lost_added, ln_held = sem("w_made"), sem("back_made"), sem("lost_made"), sem("lost_added"), sem("ln_held")
        du_made, res_made = sem("du_made"), sem("res_made")
        c_copied = sem("c_copied")
        da_made, dbu_made, scanned, turned, summed = sem("da_made"), sem("dbu_made"), sem("scanned"), sem("turned"), sem("summed")
        stats_made, ln_step, ln_biased, ln_rooted, shift_made, x1_made = (
            sem("stats_made"), sem("ln_step"), sem("ln_biased"), sem("ln_rooted"), sem("shift_made"), sem("x1_made"))
        block = ctx.enter_context(nc.Block())

        dram = {"w_in": w_in, "w_xp": w_xp, "w_dt": w_dt, "w_out": w_out, "w_norm": w_norm,
                "conv_w": conv_w, "conv_b": conv_b, "b_dt": b_dt, "skip": skip, "a_neg": a_neg}

        def sequences(eng, body):
            body(0, True, False)
            with eng.Fori(1, NB - 1) as b:
                body(b, False, False)
            body(NB - 1, False, True)

        @block.sync
        def _(sp):
            for n in small:
                sp.dma_start(dram[n][:], t[n]).then_inc(small_loaded, 16)

            def load_x(b):
                row = snap(sp, b * L)
                if not (isinstance(b, int) and b == 0):
                    sp.wait_ge(filled["xt"], TT * b)
                sp.dma_start(x_in[:], t["x"][bass.ds(row, L), :].rearrange("(i p) d -> p i d", p=P)).then_inc(x_loaded, 16)

            def load_re(b, first):
                row = snap(sp, b * L)
                if not first:
                    sp.wait_ge(x1_stored, 16 * b)
                sp.dma_start(acc[:], t["x"][bass.ds(row, L), :].rearrange("(i p) d -> p i d", p=P)).then_inc(re_loaded, 16)

            def load_b(b, c, begin):
                row = snap(sp, b * NS + (c * B_CHUNK) % NS)
                stored = snap(sp, 16 * b + 16)
                freed = snap(sp, SCANS * b + GB * B_CHUNK * (c - 1))
                if c == 0 or begin:
                    sp.wait_ge(b_stored, stored)
                if not (begin and c < 2):
                    sp.wait_ge(dbu_made, freed)
                src = t["b_rows"][bass.ds(row, B_CHUNK), :]
                sp.dma_start(b_bc[:, c % 2], src.partition_broadcast(P)).then_inc(b_loaded[c % 2], 16)

            def store_b(b):
                row = snap(sp, b * NS)
                sp.wait_ge(taken["bc"], b + 1)
                sp.dma_start(t["b_rows"][bass.ds(row, NS), :], bc_t[0:NS, :]).then_inc(b_stored, 16)

            def store_x1(b):
                row = snap(sp, b * L)
                sp.wait_ge(x1_made, TT * (b + 1))
                sp.dma_start(t["x1"][bass.ds(row, L), :].rearrange("(i p) d -> p i d", p=P), acc[:]).then_inc(x1_stored, 16)

            load_x(0)
            for n in big:
                sp.dma_start(dram[n][:], t[n]).then_inc(loaded[n], 16)
            store_b(0)
            load_b(0, 0, True)

            def body(b, first, last):
                for k in range(STEPS):
                    if k % B_CHUNK == 0:
                        c = k // B_CHUNK + 1
                        if c < B_LOADS:
                            load_b(b, c, first)
                        elif not last:
                            load_b(b + 1, 0, False)
                    if k == LAYERNORM_AT and not first:
                        store_x1(b - 1)
                    if k == 0 and not last:
                        load_x(b + 1)
                    if k == LAYERNORM_AT + 3:
                        load_re(b, first)
                    if k == 27 and not last:
                        store_b(b + 1)

            sequences(sp, body)
            store_x1(NB - 1)
            sp.wait_ge(x1_stored, 16 * NB)

        @block.gpsimd
        def _(pool):
            pool.memset(ident[:], 0.0).then_inc(ident_zeroed, 1)
            pool.memset(minus_half[:], -0.5).then_inc(half_made, 1)
            pool.wait_ge(ident_zeroed, 1)
            pool.affine_select(out=ident[:], in_=ident[:], compare_op=ALU.not_equal, fill=1.0, base=0,
                               pattern=[[-1, P]], channel_multiplier=1).then_inc(ident_made, 1)

            pool.wait_ge(half_made, 1)

            def x_root(b):
                pool.wait_ge(x_meaned, TT * (b + 1))
                pool.tensor_tensor(x_rstd[:], x_sq[:], minus_half[:], ALU.pow).then_inc(x_rooted, 1)

            def make_lost(b, i):
                pool.wait_ge(back_made, BLK * b + i + 1)
                pool.tensor_tensor(softp[:, i % SOFTP_RING], softp[:, i % SOFTP_RING], du[:, i], ALU.subtract).then_inc(lost_made, 1)
                pool.wait_ge(lost_made, BLK * b + i + 1)
                pool.tensor_tensor(delta[:, i], delta[:, i], softp[:, i % SOFTP_RING], ALU.add).then_inc(lost_added, 1)

            def make_delta(b, i):
                pool.wait_ge(ln_held, BLK * b + i + 1)
                pool.tensor_tensor(delta[:, i], delta[:, i], softp[:, i % SOFTP_RING], ALU.add).then_inc(delta_made, 1)

            def make_du(b, i):
                pool.wait_ge(delta_made, BLK * b + i + 1)
                pool.wait_ge(u_made, 2 * b + i // GB + 1)
                pool.tensor_tensor(du[:, i], delta[:, i], u[:, i], ALU.mult).then_inc(du_made, 1)

            def ln_root(b):
                pool.wait_ge(ln_biased, b + 1)
                if not (isinstance(b, int) and b == 0):
                    pool.wait_ge(x1_made, TT * b)
                pool.tensor_tensor(ln_rstd[:], ln_var[:], minus_half[:], ALU.pow).then_inc(ln_rooted, 1)

            x_root(0)
            for i in range(GB):
                make_lost(0, i)
            for i in range(GB):
                make_delta(0, i)
                make_du(0, i)

            def body(b, first, last):
                for k in range(STEPS):
                    g, n = k // GROUP_STEPS, k % GROUP_STEPS
                    if k % B_CHUNK == 0:
                        c = k // B_CHUNK
                        pool.wait_ge(b_loaded[c % 2], 16 * (B_LOADS // 2 * b + c // 2 + 1))
                    if n == 0:
                        pool.wait_ge(du_made, BLK * b + GB * (g + 1))
                    for j in range(GB):
                        s = GB * k + j
                        if not (first and s < DBU_RING):
                            pool.wait_ge(scanned, SCANS * b + s - DBU_RING + 1)
                        pool.tensor_tensor(dbu[:, s % DBU_RING], du[:, g * GB + j],
                                           b_bc[:, (k // B_CHUNK) % 2, k % B_CHUNK], ALU.mult).then_inc(dbu_made, 1)

                    for i, d in stages_at(LOST_AT, k, last):
                        make_lost(b + d, i)
                    for i, d in stages_at(MADE_AT, k, last):
                        make_delta(b + d, i)
                        make_du(b + d, i)
                    if k == X_ROOT_AT and not last:
                        x_root(b + 1)
                    if k == LN_ROOT_AT and not first:
                        ln_root(b - 1)

            sequences(pool, body)
            ln_root(NB - 1)

        @block.scalar
        def _(act):
            act.wait_ge(small_loaded, 16 * len(small))
            act.activation(a_neg[:], a_neg[:], ACT.Exp).then_inc(a_exped, 1)

            def square(b, i):
                if i == 0:
                    act.wait_ge(x_loaded, 16 * (b + 1))
                    if not (isinstance(b, int) and b == 0):
                        act.wait_ge(delta_made, BLK * (b - 1) + GB)
                        act.wait_ge(x_rooted, b)
                if not (isinstance(b, int) and b == 0 and i == 0):
                    act.wait_ge(x_squared, TT * b + i)
                act.activation(softp[:, SOFTP_RING - 1], x_in[:, i], ACT.Square, accum_out=x_sq[:, i:i + 1]).then_inc(x_squared, 1)
                act.wait_ge(x_squared, TT * b + i + 1)
                act.activation(x_sq[:, i:i + 1], x_sq[:, i:i + 1], ACT.Copy, scale=1.0 / DM, bias=EPS).then_inc(x_meaned, 1)

            def scale(b, i):
                act.wait_ge(x_rooted, b + 1)
                act.activation(x_in[:, i], x_in[:, i], ACT.Copy, scale=x_rstd[:, i:i + 1]).then_inc(x_scaled, 1)

            def silu_u(b, g):
                act.wait_ge(taken["u"], BLK * b + GB * (g + 1))
                act.activation(u[:, g * GB:(g + 1) * GB], u[:, g * GB:(g + 1) * GB], ACT.Silu).then_inc(u_made, 1)

            def silu_res(b, g):
                act.wait_ge(taken["res"], BLK * b + GB * (g + 1))
                act.activation(sres[:, g * GB:(g + 1) * GB], sres[:, g * GB:(g + 1) * GB], ACT.Silu).then_inc(res_made, 1)

            def consume(b0, jobs):
                for kind, i, d in finished(jobs):
                    b, bank, g = b0 + d, job_ps[BANK_OF[kind, i]], i // GB
                    started = isinstance(b, int) and b == 0
                    if kind in ("xt", "u", "dt", "bc", "delta", "res", "yt"):
                        act.wait_ge(filled[kind], PER_SEQ[kind] * b + i + 1)
                    if kind == "xt":
                        if not started:
                            act.wait_ge(filled["res"], BLK * b)
                            act.wait_ge(filled["u"], BLK * b)
                        act.activation(xn_t[:, :, i * P:(i + 1) * P], bank[:].rearrange("p (c t) -> p c t", c=KC), ACT.Copy).then_inc(taken["xt"], 1)
                    if kind == "u":
                        if not started:
                            act.wait_ge(du_made, BLK * (b - 1) + i + 1)
                            act.wait_ge(filled["yt"], BLK * (b - 1) + GB * (g + 1))
                            act.wait_ge(filled["bc"], b)
                        act.activation(u[:, i], bank[:], ACT.Identity, scale=conv_w[:, i, TAPS - 1:TAPS],
                                       bias=conv_b[:, i:i + 1]).then_inc(tap_made, 1)
                    if kind == "dt":
                        if not started:
                            act.wait_ge(filled["delta"], BLK * b)
                        act.activation(dt_r[:], bank[:], ACT.Copy).then_inc(taken["dt"], 1)
                    if kind == "bc":
                        if not started:
                            act.wait_ge(filled["ct"], b)
                            act.wait_ge(b_stored, 16 * b)
                        act.activation(bc_t[:], bank[0:2 * NS, :], ACT.Copy).then_inc(taken["bc"], 1)
                    if kind == "delta":
                        if not (started and i < SOFTP_RING):
                            act.wait_ge(delta_made, BLK * b + i - SOFTP_RING + 1)
                        act.activation(softp[:, i % SOFTP_RING], bank[:], ACT.Abs, bias=b_dt[:, i:i + 1]).then_inc(abs_made, 1)
                        if not started:
                            act.wait_ge(da_made, SCANS * (b - 1) + GROUP_STEPS * GB * (g + 1))
                            act.wait_ge(du_made, BLK * (b - 1) + i + 1)
                        act.activation(delta[:, i], bank[:], ACT.Relu, bias=b_dt[:, i:i + 1]).then_inc(taken["delta"], 1)
                        act.wait_ge(abs_made, BLK * b + i + 1)
                        act.activation(softp[:, i % SOFTP_RING], softp[:, i % SOFTP_RING], ACT.Exp, scale=-1.0).then_inc(exp_made, 1)
                        if not started:
                            act.wait_ge(dbu_made, SCANS * (b - 1) + GROUP_STEPS * GB * (g + 1))
                        act.wait_ge(exp_made, BLK * b + i + 1)
                        act.activation(du[:, i], softp[:, i % SOFTP_RING], ACT.Identity, bias=1.0).then_inc(w_made, 1)
                        act.wait_ge(w_made, BLK * b + i + 1)
                        act.activation(du[:, i], du[:, i], ACT.Identity, bias=-1.0).then_inc(back_made, 1)
                    if kind == "res":
                        if not started:
                            act.wait_ge(filled["out"], BLK * (b - 1) + GB * (g + 1))
                        act.activation(sres[:, i], bank[:], ACT.Copy).then_inc(taken["res"], 1)
                    if kind == "yt":
                        if not started:
                            act.wait_ge(filled["fin"], BLK * (b - 1) + GB * (g + 1))
                        act.activation(y_t[:, g, i % GB], bank[:], ACT.Copy).then_inc(taken["yt"], 1)

            def take_ln(b, i):
                act.wait_ge(lost_added, BLK * b + i + 1)
                act.activation(softp[:, i % SOFTP_RING], du[:, i], ACT.Ln, bias=1.0).then_inc(ln_made, 1)

            def layernorm(b):
                act.wait_ge(shift_made, b + 1)
                for i in range(TT):
                    act.activation(acc[:, i], acc[:, i], ACT.Identity, scale=ln_rstd[:, i:i + 1],
                                   bias=ln_shift[:, i:i + 1]).then_inc(x1_made, 1)

            def decay(b, s, first):
                k, j = s // GB, s % GB
                g, n = k // GROUP_STEPS, k % GROUP_STEPS
                blk = g * GB + j
                if n == 0:
                    act.wait_ge(delta_made, BLK * b + blk + 1)
                if not (first and s < 2):
                    act.wait_ge(scanned, SCANS * b + s - 1)
                act.activation(da_ps[s % 2][:], delta[:, blk], ACT.Exp, scale=a_neg[:, blk, n:n + 1]).then_inc(da_made, 1)

            for i in range(TT):
                square(0, i)
            for i in range(TT):
                scale(0, i)
            for kind, i, d in PROLOGUE:
                consume(-1, [(kind, i, d)])
                if (kind, i) == ("u", BLK - 1):
                    silu_u(0, 0)
                    silu_u(0, 1)
                if (kind, i) == ("delta", GB - 1):
                    for ii in range(GB):
                        take_ln(0, ii)
            act.wait_ge(a_made, 1)
            decay(0, 0, True)
            decay(0, 1, True)

            def body(b, first, last):
                for k in range(STEPS):
                    for s in range(GB * k + 2, GB * k + GB + 2):
                        if s < SCANS:
                            decay(b, s, first)
                        elif not last:
                            decay(b + 1, s - SCANS, False)
                    if k == 0 and not first:
                        consume(b - 1, jobs_at(STEPS - 1, False, False))
                    if k > 0:
                        consume(b, jobs_at(k - 1, first, last))
                    for i, d in stages_at(LN_AT, k, last):
                        take_ln(b + d, i)
                    if not last:
                        if k == SQUARE_AT:
                            for i in range(TT):
                                square(b + 1, i)
                        if k == SCALE_AT:
                            for i in range(TT):
                                scale(b + 1, i)
                        if k in SILU_U_AT:
                            silu_u(b + 1, SILU_U_AT[k])
                    if k in SILU_RES_AT:
                        silu_res(b, SILU_RES_AT[k])
                    if k == LAYERNORM_AT and not first:
                        layernorm(b - 1)

            sequences(act, body)
            layernorm(NB - 1)

        @block.tensor
        def _(pe):
            for n in ("w_xp", "w_dt", "w_out"):
                pe.wait_ge(loaded[n], 16)
            pe.wait_ge(norm_folded, KC)
            pe.wait_ge(ident_made, 1)
            pe.wait_ge(diag_made, BLK)
            bank_user = [None, None]

            def fill(b0, part, i, d):
                kind = part.removesuffix("_begin")
                b, bank, g = b0 + d, job_ps[BANK_OF[kind, i]], i // GB
                user = bank_user[BANK_OF[kind, i]]
                if user is not None and part not in ("dt", "bc", "ct"):
                    k0, i0, d0 = user
                    pe.wait_ge(taken[k0], PER_SEQ[k0] * (b0 + d0) + i0 + 1)
                bank_user[BANK_OF[kind, i]] = (kind, i, d)
                if kind == "xt":
                    pe.wait_ge(x_scaled, TT * b + i + 1)
                    for c in range(KC):
                        last = pe.transpose(bank[:, c * P:(c + 1) * P], x_in[:, i, c * P:(c + 1) * P], ident[:])
                if kind in ("u", "res"):
                    if (kind, i) == ("u", 0):
                        pe.wait_ge(taken["xt"], TT * b + TT)
                    if (kind, i) == ("res", 0):
                        pe.wait_ge(taken["bc"], b + 1)
                    col = (DI if kind == "res" else 0) + i * P
                    for c in range(KC):
                        last = pe.matmul(bank[:], w_in[:, c, col:col + P], xn_t[:, c, :], start=c == 0, stop=c == KC - 1)
                if kind in ("dt", "bc"):
                    pe.wait_ge(u_made, 2 * b + (1 if part != kind else 2))
                    lo, hi = (0, RANK) if kind == "dt" else (RANK, RANK + 2 * NS)
                    for c in range(GB) if part != kind else range(GB, BLK):
                        last = pe.matmul(bank[0:hi - lo, :], w_xp[:, c, lo:hi], u[:, c], start=c == 0, stop=c == BLK - 1)
                if kind == "ct":
                    for c in range(TT):
                        last = pe.transpose(bank[:, c * 2 * NS:(c + 1) * 2 * NS], bc_t[:, c * P:(c + 1) * P],
                                            ident[0:2 * NS, 0:2 * NS])
                if kind == "delta":
                    pe.wait_ge(taken["dt"], b + 1)
                    last = pe.matmul(bank[:], w_dt[:, i * P:(i + 1) * P], dt_r[:], start=True, stop=True)
                if kind == "yt":
                    tt = i % GB
                    for j in range(GB):
                        last = pe.matmul(bank[:, j * P:(j + 1) * P], u[:, g * GB + j, tt * P:(tt + 1) * P],
                                         diag_d[:, g * GB + j], start=True, stop=True)
                if kind == "fin":
                    j = i % GB
                    pe.wait_ge(summed, TT * (STEPS * b + GROUP_STEPS * (g + 1)))
                    for tt in range(TT):
                        last = pe.transpose(bank[:, tt * P:(tt + 1) * P], y_t[:, g, tt, j * P:(j + 1) * P], ident[:])
                if kind == "out":
                    tt = i % GB
                    pe.wait_ge(taken["fin"], BLK * b + GB * (g + 1))
                    for j in range(GB):
                        last = pe.matmul(bank[:], sres[:, g * GB + j, tt * P:(tt + 1) * P], w_out[:, g * GB + j],
                                         start=j == 0, stop=j == GB - 1)
                if part == kind:
                    last.then_inc(filled[kind], 1)

            def rebase():
                for n in range(2):
                    k0, i0, d0 = bank_user[n]
                    bank_user[n] = (k0, i0, d0 - 1)

            for kind, i, d in PROLOGUE:
                fill(-1, kind, i, d)
            rebase()

            def body(b, first, last):
                for k in range(STEPS):
                    for j in range(GB):
                        s = GB * k + j
                        pe.wait_ge(scanned, SCANS * b + s + 1)
                        if j == 0 and not (first and k == 0):
                            pe.wait_ge(summed, TT * (STEPS * b + k))
                        for tt in range(TT):
                            turn = pe.transpose(ht_ps[tt][:, j * P:(j + 1) * P], h[:, s % H_RING, tt * P:(tt + 1) * P], ident[:])
                        turn.then_inc(turned, 1)
                    for kind, i, d in jobs_at(k, first, last):
                        fill(b, kind, i, d)
                rebase()

            sequences(pe, body)
            for kind, i, d in EPILOGUE:
                fill(NB, kind, i, d)

        @block.vector
        def _(dve):
            dve.wait_ge(small_loaded, 16 * len(small))
            dve.wait_ge(loaded["w_in"], 16)
            for c in range(KC):
                dve.tensor_scalar(w_in[:, c], w_in[:, c], w_norm[:, c:c + 1], None, ALU.mult).then_inc(norm_folded, 1)
            dve.wait_ge(a_exped, 1)
            dve.tensor_scalar(a_neg[:], a_neg[:], -1.0, None, ALU.mult).then_inc(a_made, 1)
            dve.wait_ge(ident_made, 1)
            for i in range(BLK):
                dve.tensor_scalar(diag_d[:, i], ident[:], skip[:, i:i + 1], None, ALU.mult).then_inc(diag_made, 1)

            def consume(b0, jobs):
                for kind, i, d in finished(jobs):
                    b, bank, g = b0 + d, job_ps[BANK_OF[kind, i]], i // GB
                    if kind == "u":
                        dve.wait_ge(tap_made, BLK * b + i + 1)
                        for tap in range(1, TAPS):
                            if tap > 1:
                                dve.wait_ge(conv_step, (TAPS - 2) * (BLK * b + i) + tap - 1)
                            add = dve.scalar_tensor_tensor(u[:, i, tap:L], bank[:, 0:L - tap], conv_w[:, i, TAPS - 1 - tap:TAPS - tap],
                                                           u[:, i, tap:L], ALU.mult, ALU.add)
                            if tap < TAPS - 1:
                                add.then_inc(conv_step, 1)
                        add.then_inc(taken["u"], 1)
                    if kind == "ct":
                        dve.wait_ge(filled["ct"], b + 1)
                        if not (isinstance(b, int) and b == 0):
                            dve.wait_ge(c_copied, b)
                        dve.tensor_copy(c_next[:], bank[:, 0:TT * 2 * NS].rearrange("p (t n) -> p t n", t=TT)[:, :, NS:2 * NS]).then_inc(taken["ct"], 1)
                    if kind == "fin":
                        dve.wait_ge(filled["fin"], BLK * b + i + 1)
                        dve.wait_ge(res_made, 2 * b + (2 if g else 1))
                        dve.tensor_tensor(sres[:, i], bank[:], sres[:, i], ALU.mult).then_inc(taken["fin"], 1)
                    if kind == "out":
                        tt = i % GB
                        dve.wait_ge(filled["out"], BLK * b + i + 1)
                        if g == 0:
                            if tt == 0:
                                dve.wait_ge(re_loaded, 16 * (b + 1))
                            dve.scalar_tensor_tensor(acc[:, tt], acc[:, tt], 2.0, bank[:], ALU.mult, ALU.add).then_inc(taken["out"], 1)
                        else:
                            dve.wait_ge(taken["out"], BLK * b + tt + 1)
                            dve.tensor_tensor(acc[:, tt], bank[:], acc[:, tt], ALU.add).then_inc(taken["out"], 1)
                            dve.wait_ge(taken["out"], BLK * b + i + 1)
                            dve.bn_stats(stats[:, tt], acc[:, tt]).then_inc(stats_made, 1)

            def hold_ln(b, i):
                dve.wait_ge(ln_made, BLK * b + i + 1)
                dve.scalar_tensor_tensor(softp[:, i % SOFTP_RING], softp[:, i % SOFTP_RING], 0.0, du[:, i],
                                         ALU.max, ALU.min).then_inc(ln_held, 1)

            def variances(b):
                even, odd = stats[:, :, 1:3], stats[:, :, 4:6]
                dve.wait_ge(stats_made, TT * (b + 1))
                dve.tensor_tensor(ln_both[:], even, odd, ALU.add).then_inc(ln_step, 1)
                dve.tensor_tensor(ln_gap[:], stats[:, :, 1], stats[:, :, 4], ALU.subtract).then_inc(ln_step, 1)
                dve.wait_ge(ln_step, 4 * b + 2)
                dve.tensor_tensor(ln_gap[:], ln_gap[:], ln_gap[:], ALU.mult).then_inc(ln_step, 1)
                dve.wait_ge(ln_step, 4 * b + 3)
                dve.scalar_tensor_tensor(ln_var[:], ln_gap[:], DM / 4.0, ln_both[:, :, 1], ALU.mult, ALU.add).then_inc(ln_step, 1)
                dve.wait_ge(ln_step, 4 * b + 4)
                dve.tensor_scalar(ln_var[:], ln_var[:], 1.0 / DM, EPS, ALU.mult, ALU.add).then_inc(ln_biased, 1)

            def shifts(b):
                dve.wait_ge(ln_rooted, b + 1)
                dve.scalar_tensor_tensor(ln_shift[:], ln_both[:, :, 0], -0.5, ln_rstd[:], ALU.mult, ALU.mult).then_inc(shift_made, 1)

            def sum_states(b, k, first):
                g, n = k // GROUP_STEPS, k % GROUP_STEPS
                if k == 0:
                    dve.wait_ge(taken["ct"], b + 1)
                    if not first:
                        dve.wait_ge(summed, TT * STEPS * b)
                    dve.tensor_copy(c_now[:], c_next[:]).then_inc(c_copied, 1)
                    dve.wait_ge(c_copied, b + 1)
                if n == 0:
                    dve.wait_ge(taken["yt"], BLK * b + GB * (g + 1))
                dve.wait_ge(turned, SCANS * b + GB * (k + 1))
                for tt in range(TT):
                    if n > 0:
                        dve.wait_ge(summed, TT * (STEPS * b + k - 1) + tt + 1)
                    dve.scalar_tensor_tensor(y_t[:, g, tt], ht_ps[tt][:], c_now[:, tt, n:n + 1], y_t[:, g, tt],
                                             ALU.mult, ALU.add).then_inc(summed, 1)

            for kind, i, d in PROLOGUE:
                consume(-1, [(kind, i, d)])
                if (kind, i) == ("delta", GB - 1):
                    for ii in range(GB):
                        hold_ln(0, ii)

            def body(b, first, last):
                for k in range(STEPS):
                    for j in range(GB):
                        s = GB * k + j
                        dve.wait_ge(da_made, SCANS * b + s + 1)
                        dve.wait_ge(dbu_made, SCANS * b + s + 1)
                        if not (first and s < H_RING):
                            dve.wait_ge(turned, SCANS * b + s - H_RING + 1)
                        dve.tensor_tensor_scan(h[:, s % H_RING], da_ps[s % 2][:], dbu[:, s % DBU_RING], 0.0,
                                               ALU.mult, ALU.add).then_inc(scanned, 1)
                    if k > 0:
                        sum_states(b, k - 1, first)
                        consume(b, jobs_at(k - 1, first, last))
                    elif not first:
                        sum_states(b - 1, STEPS - 1, False)
                        consume(b - 1, jobs_at(STEPS - 1, False, False))
                    for i, d in stages_at(HOLD_AT, k, last):
                        hold_ln(b + d, i)
                    if k == VARIANCE_AT and not first:
                        variances(b - 1)
                    if k == SHIFT_AT and not first:
                        shifts(b - 1)

            sequences(dve, body)
            sum_states(NB - 1, STEPS - 1, False)
            consume(NB, EPILOGUE)
            variances(NB - 1)
            shifts(NB - 1)


def moe(nc, t, counters):
    ctx = ExitStack()
    with ctx:
        def sb(name, shape, dt=F32):
            return ctx.enter_context(nc.sbuf_tensor(name, shape, dt))

        def sem(name):
            return counters.enter_context(nc.semaphore(name))

        def sems(name, n=RING):
            return [sem(f"{name}{i}") for i in range(n)]

        w13 = sb("w13", [P, E + 1, KC, 2 * HID])
        w2 = sb("w2", [P, E + 1, len(HC), DM])
        gate = sb("gate", [P, KC, E])
        ident = sb("identity", [P, P])
        before = sb("before", [P, P], BF16)
        ones = sb("ones", [P, P], BF16)
        minus_half = sb("minus_halves", [P, 1])
        xg = sb("xg", [P, RING, DM])
        xt = sb("xt", [P, KC, P])
        act_h = sb("act_h", [P, HID])
        gated = sb("gated", [P, HID])
        gt = sb("gt", [P, len(HC), P])
        y = sb("y", [P, 2, DM])
        yg = sb("yg", [P, 2, TOPK, DM])
        scores = sb("scores", [P, NT, E])
        top = sb("top", [P, NT, 8])
        top_at = sb("top_at", [P, NT, 8], U32)
        chosen = sb("chosen", [P, TOPK, NT])
        hot = sb("hot", [P, TOPK, E, NT])
        both = sb("both", [P, E, NT], BF16)
        keep = sb("keep", [P, E, NT])
        former = sb("former", [P, E, NT])
        base = sb("base", [P, E, NT])
        place = sb("place", [P, E, NT])
        dest_f = sb("dest_f", [P, TOPK, NT])
        dest = sb("dest", [P, TOPK, NT], U32)
        total = sb("total", [P, NT])
        share = sb("share", [P, TOPK, NT])
        token = sb("token", [P, NT], U32)
        size = sb("size", [P, E])
        tiles = sb("tiles", [P, E])
        ends = sb("ends", [P, E])
        one_row = sb("one_row", [P, E])
        edge_i = sb("edge_i", [P, NT], U32)
        edge = sb("edge", [P, NT])
        slot_i = sb("slot_i", [P, MOE_TILES], U32)
        slot = sb("slot", [P, MOE_TILES])
        past = sb("past", [P, E, MOE_TILES])
        owner = sb("owner", [P, MOE_TILES])
        starts = sb("starts", [P, E])
        expert = sb("expert", [P, MOE_TILES], U32)
        zero = sb("zero", [P, LIST_ROWS // P], U32)
        put_at = sb("put_at", [P, RING, TOPK], U32)
        put = sb("put", [P, RING], U32)
        got = sb("got", [P, RING], U32)
        take_at = sb("take_at", [P, 2, TOPK], U32)
        stats = sb("row_stats", [P, 2, 6])
        pair = sb("pair", [P, 2, 2])
        gap = sb("gap", [P, 2])
        var = sb("var", [P, 2])
        rstd = sb("rstd", [P, 2])
        shift = sb("shift", [P, 2])

        ps = [ctx.enter_context(nc.psum_tensor(f"moe_ps{i}", [P, 512], F32)) for i in range(7)]
        x_ps, h_ps, u_ps, g_ps, y_ps, route_ps, count_ps = ps

        w_loaded = sem("experts_loaded")
        gate_loaded = sem("gate_loaded")
        rx_loaded, r_turned, r_copied, r_gated, scored = sems("rx_loaded"), sem("r_turned"), sem("r_copied"), sem("r_gated"), sem("scored")
        made = sem("constants_made")
        zeroed, topped, found, routed = sem("zeroed"), sem("topped"), sem("found"), sem("routed")
        both_made, counted, dest_made, rows_made = sem("both_made"), sem("counted"), sem("dest_made"), sem("rows_made")
        table_cleared, put_copied, put_done = sem("table_cleared"), sem("put_copied"), sems("put_done")
        got_loaded, gathered, x_loaded = sems("got_loaded"), sems("gathered"), sems("x_in")
        x_turned, x_copied, upped, h_made, g_made, g_turned, g_copied, downed = (
            sem(n) for n in ("x_turned", "x_copied", "upped", "h_made", "g_made", "g_turned", "g_copied", "downed"))
        y_made, y_stored = sem("y_made"), sems("y_stored", 2)
        take_copied, taken = sem("take_copied"), sems("rows_taken", 2)
        added, row_stated, row_step, row_vared, rooted, shifted, out_made, out_stored = (
            sem("added"), sem("row_stated"), sem("row_step"), sem("row_vared"), sem("rooted"), sem("shifted"), sem("out_made"), sems("out_stored", 2))
        put_ready, gather_ready, take_ready = sem("put_ready"), sem("gather_ready"), sem("take_ready")
        block = ctx.enter_context(nc.Block())

        def rings(eng, n, body):
            turns = n // RING
            body(0, True, False)
            with eng.Fori(1, turns - 1) as r:
                body(r, False, False)
            body(turns - 1, False, True)

        @block.sync
        def _(sp):
            sp.dma_start(gate[:], t["gate"]).then_inc(gate_loaded, 16)

            def load_route(r, first, last):
                for i in range(RING):
                    at = snap(sp, (r * RING + i) * P)
                    if not first:
                        sp.wait_ge(r_turned, RING * (r - 1) + i + 1)
                    sp.dma_start(xg[:, i], t["x1"][bass.ds(at, P), :]).then_inc(rx_loaded[i], 16)

            rings(sp, NT, load_route)
            for e in range(E + 1):
                sp.dma_start(w13[:, e], t["w13"][e]).then_inc(w_loaded, 16)
                sp.dma_start(w2[:, e], t["w2"][e]).then_inc(w_loaded, 16)
            for i in range(RING):
                sp.wait_ge(put_done[i], 16 * TOPK * (NT // RING))

            def load_got(r, first, last):
                for i in range(RING):
                    at = snap(sp, (r * RING + i) * P)
                    if not first:
                        sp.wait_ge(gathered[i], 16 * r)
                    sp.dma_start(got[:, i:i + 1], t["lists"][bass.ds(at, P), :]).then_inc(got_loaded[i], 16)

            rings(sp, MOE_TILES, load_got)

            def load_shared(r, first, last):
                for i in range(RING):
                    at = snap(sp, (r * RING + i) * P)
                    if first:
                        sp.wait_ge(x_turned, MOE_TILES - RING + i + 1)
                    else:
                        sp.wait_ge(added, TOPK * 2 * (RING * (r - 1) + i + 1))
                    sp.dma_start(xg[:, i], t["x1"][bass.ds(at, P), :]).then_inc(x_loaded[i], 16)

            rings(sp, NT, load_shared)

        @block.gpsimd
        def _(pool):
            steps = 0

            def then(ins):
                nonlocal steps
                steps += 1
                ins.then_inc(made, 1)
                pool.wait_ge(made, steps)

            then(pool.memset(zero[:], 0))
            pool.dma_start(t["lists"].rearrange("(p n) a -> p (n a)", p=P), zero[:]).then_inc(table_cleared, 16)
            then(pool.memset(ident[:], 0.0))
            then(pool.affine_select(out=ident[:], in_=ident[:], compare_op=ALU.not_equal, fill=1.0, base=0,
                                    pattern=[[-1, P]], channel_multiplier=1))
            then(pool.memset(before[:], 1.0))
            then(pool.affine_select(out=before[:], in_=before[:], compare_op=ALU.is_gt, fill=0.0, base=0,
                                    pattern=[[1, P]], channel_multiplier=-1))
            then(pool.memset(ones[:], 1.0))
            then(pool.memset(minus_half[:], -0.5))
            then(pool.memset(keep[:], 1.0))
            then(pool.memset(keep[:, :, 0:1], 0.0))
            then(pool.memset(former[:], 0.0))
            then(pool.memset(one_row[:], 1.0))
            then(pool.iota(edge_i[:], pattern=[[P, NT]], base=0, channel_multiplier=0))
            then(pool.iota(slot_i[:], pattern=[[1, MOE_TILES]], base=0, channel_multiplier=0))
            then(pool.iota(token[:], pattern=[[P, NT]], base=0, channel_multiplier=1))
            assert steps == CONSTANTS

            pool.wait_ge(dest_made, 1)
            pool.wait_ge(table_cleared, 16)

            def put_tokens(r, first, last):
                for i in range(RING):
                    if not first:
                        pool.wait_ge(put_done[i], 16 * TOPK * r)
                    pool.tensor_copy(put[:, i:i + 1], token[:, bass.ds(r * RING + i, 1)]).then_inc(put_copied, 1)
                    pool.tensor_copy(put_at[:, i, :], dest[:, :, bass.ds(r * RING + i, 1)]).then_inc(put_copied, 1)
                pool.wait_ge(put_copied, 2 * (RING * r + RING))
                pool.sem_inc(put_ready, 1)
                for i in range(RING):
                    for c in range(TOPK):
                        pool.indirect_dma_start(t["lists"], bass.IndirectOffsetOnAxis(ap=put_at[:, i, c:c + 1], axis=0),
                                                put[:, i:i + 1], None).then_inc(put_done[i], 16)

            rings(pool, NT, put_tokens)

            def gather(r, first, last):
                for i in range(RING):
                    if first:
                        pool.wait_ge(r_turned, NT)
                    else:
                        pool.wait_ge(x_turned, RING * (r - 1) + i + 1)
                    pool.wait_ge(got_loaded[i], 16 * (r + 1))
                    pool.sem_inc(gather_ready, 1)
                    pool.indirect_dma_start(xg[:, i], None, t["x1"],
                                            bass.IndirectOffsetOnAxis(ap=got[:, i:i + 1], axis=0)).then_inc(gathered[i], 16)

            rings(pool, MOE_TILES, gather)

            for n in range(2):
                pool.wait_ge(y_stored[n], 16 * (MOE_TILES // 2))

            def take(r, first, last):
                for i in range(RING):
                    q = RING * r + i
                    if not (first and i < 2):
                        pool.wait_ge(added, TOPK * 2 * (q - 1))
                    pool.tensor_copy(take_at[:, i % 2, :], dest[:, :, bass.ds(q, 1)]).then_inc(take_copied, 1)
                    pool.wait_ge(take_copied, q + 1)
                    pool.sem_inc(take_ready, 1)
                    for c in range(TOPK):
                        pool.indirect_dma_start(yg[:, i % 2, c], None, t["y_rows"],
                                                bass.IndirectOffsetOnAxis(ap=take_at[:, i % 2, c:c + 1], axis=0)).then_inc(taken[i % 2], 16)
                    if not (first and i == 0):
                        root(q - 1, (i - 1) % 2)

            def root(q, n):
                pool.wait_ge(row_vared, q + 1)
                pool.tensor_tensor(rstd[:, n:n + 1], var[:, n:n + 1], minus_half[:], ALU.pow).then_inc(rooted, 1)

            rings(pool, NT, take)
            root(NT - 1, 1)

        @block.tensor
        def _(pe):
            pe.wait_ge(made, CONSTANTS)
            pe.wait_ge(gate_loaded, 16)

            def route(r, first, last):
                for i in range(RING):
                    q = RING * r + i
                    pe.wait_ge(rx_loaded[i], 16 * (r + 1))
                    if not (first and i == 0):
                        pe.wait_ge(r_copied, q)
                    for c in range(KC):
                        turn = pe.transpose(x_ps[:, c * P:(c + 1) * P], xg[:, i, c * P:(c + 1) * P], ident[:])
                    turn.then_inc(r_turned, 1)
                    pe.wait_ge(r_copied, q + 1)
                    if not (first and i == 0):
                        pe.wait_ge(scored, q)
                    for c in range(KC):
                        last_mm = pe.matmul(route_ps[:, 0:E], xt[:, c], gate[:, c], start=c == 0, stop=c == KC - 1)
                    last_mm.then_inc(r_gated, 1)

            rings(pe, NT, route)
            pe.wait_ge(both_made, 1)
            pe.matmul(route_ps[:, 0:E * NT], before[:], both[:].rearrange("p e i -> p (e i)"), start=True, stop=True)
            pe.matmul(count_ps[:, 0:E * NT], ones[:], both[:].rearrange("p e i -> p (e i)"), start=True, stop=True).then_inc(counted, 1)

            def turn_x(q0, r, i):
                pe.wait_ge((x_loaded if q0 else gathered)[i], 16 * (r + 1))
                if not (isinstance(r, int) and q0 + RING * r + i == 0):
                    pe.wait_ge(x_copied, q0 + RING * r + i)
                for c in range(KC):
                    turn = pe.transpose(x_ps[:, c * P:(c + 1) * P], xg[:, i, c * P:(c + 1) * P], ident[:])
                turn.then_inc(x_turned, 1)

            def up(q, e, at_zero):
                pe.wait_ge(x_copied, q + 1)
                if not at_zero:
                    pe.wait_ge(g_made, q)
                for out, lo in ((h_ps, 0), (u_ps, HID)):
                    for c in range(KC):
                        last_mm = pe.matmul(out[:, 0:HID], xt[:, c], w13[:, e, c, lo:lo + HID], start=c == 0, stop=c == KC - 1)
                last_mm.then_inc(upped, 1)

            def turn_g(q, at_zero):
                pe.wait_ge(g_made, q + 1)
                for n, (lo, hi) in enumerate(HC):
                    turn = pe.transpose(g_ps[0:hi - lo, n * P:(n + 1) * P], gated[:, lo:hi], ident[:])
                turn.then_inc(g_turned, 1)

            def down(q, e, at_zero):
                pe.wait_ge(g_copied, q + 1)
                if not at_zero:
                    pe.wait_ge(y_made, q)
                for n, (lo, hi) in enumerate(HC):
                    last_mm = pe.matmul(y_ps[:], gt[0:hi - lo, n], w2[0:hi - lo, e, n], start=n == 0, stop=n == len(HC) - 1)
                last_mm.then_inc(downed, 1)

            pe.wait_ge(w_loaded, 2 * 16 * (E + 1))
            pe.wait_ge(rows_made, 1)

            turn_x(0, 0, 0)

            def experts(r, first, last):
                for i in range(RING):
                    q = RING * r + i
                    here = pe.value_load(expert[0:1, bass.ds(q, 1)], min_val=0, max_val=E - 1)
                    up(q, bass.ds(here, 1), first and i == 0)
                    if i + 1 < RING:
                        turn_x(0, r, i + 1)
                    elif not last:
                        turn_x(0, r + 1, 0)
                    if not (first and i == 0):
                        before_it = pe.value_load(expert[0:1, bass.ds(q - 1, 1)], min_val=0, max_val=E - 1)
                        down(q - 1, bass.ds(before_it, 1), first and i == 1)
                    turn_g(q, first and i == 0)

            rings(pe, MOE_TILES, experts)
            turn_x(MOE_TILES, 0, 0)
            final = pe.value_load(expert[0:1, MOE_TILES - 1:MOE_TILES], min_val=0, max_val=E - 1)
            down(MOE_TILES - 1, bass.ds(final, 1), False)

            def shared(r, first, last):
                for i in range(RING):
                    q = MOE_TILES + RING * r + i
                    up(q, E, False)
                    if i + 1 < RING:
                        turn_x(MOE_TILES, r, i + 1)
                    elif not last:
                        turn_x(MOE_TILES, r + 1, 0)
                    if not (first and i == 0):
                        down(q - 1, E, False)
                    turn_g(q, False)

            rings(pe, NT, shared)
            down(MOE_TILES + NT - 1, E, False)

        @block.scalar
        def _(act):
            def route(r, first, last):
                for i in range(RING):
                    q = RING * r + i
                    act.wait_ge(r_turned, q + 1)
                    if not (first and i == 0):
                        act.wait_ge(r_gated, q)
                    act.activation(xt[:].rearrange("p c t -> p (c t)"), x_ps[:], ACT.Copy).then_inc(r_copied, 1)
                    act.wait_ge(r_gated, q + 1)
                    act.activation(scores[:, bass.ds(q, 1), :], route_ps[:, 0:E], ACT.Sigmoid).then_inc(scored, 1)

            rings(act, NT, route)

            def copy_x(q, at_zero):
                act.wait_ge(x_turned, q + 1)
                if at_zero:
                    act.wait_ge(r_gated, NT)
                else:
                    act.wait_ge(upped, q)
                act.activation(xt[:].rearrange("p c t -> p (c t)"), x_ps[:], ACT.Copy).then_inc(x_copied, 1)

            def silu_h(q, at_zero):
                act.wait_ge(upped, q + 1)
                if not at_zero:
                    act.wait_ge(g_made, q)
                act.activation(act_h[:], h_ps[:, 0:HID], ACT.Silu).then_inc(h_made, 1)

            def give_y(q, n, at, started):
                act.wait_ge(downed, q + 1)
                if started is not None:
                    act.wait_ge(y_stored[n], started)
                act.activation(y[:, n], y_ps[:], ACT.Copy).then_inc(y_made, 1)
                act.wait_ge(y_made, q + 1)
                act.dma_start(t["y_rows"][bass.ds(at, P), :], y[:, n]).then_inc(y_stored[n], 16)

            copy_x(0, True)

            def experts(r, first, last):
                for i in range(RING):
                    q = RING * r + i
                    silu_h(q, first and i == 0)
                    if not (last and i == RING - 1):
                        copy_x(q + 1, False)
                    if not (first and i == 0):
                        at = snap(act, (q - 1) * P)
                        n = (i - 1) % 2
                        uses = 16 * (RING // 2 * r + (i - 1 - n) // 2)
                        give_y(q - 1, n, at, None if first and i < 3 else uses)

            rings(act, MOE_TILES, experts)
            give_y(MOE_TILES - 1, 1, (MOE_TILES - 1) * P, 16 * (MOE_TILES // 2 - 1))
            copy_x(MOE_TILES, False)

            def normalise(q, n, at, started):
                act.wait_ge(shifted, q + 1)
                act.activation(y[:, n], y[:, n], ACT.Identity, scale=rstd[:, n:n + 1], bias=shift[:, n:n + 1]).then_inc(out_made, 1)
                act.wait_ge(out_made, q + 1)
                act.dma_start(t["out"][bass.ds(at, P), :], y[:, n]).then_inc(out_stored[n], 16)

            def shared(r, first, last):
                for i in range(RING):
                    q = RING * r + i
                    silu_h(MOE_TILES + q, False)
                    if not (last and i == RING - 1):
                        copy_x(MOE_TILES + q + 1, False)
                    if not (first and i < 2):
                        at = snap(act, (q - 2) * P)
                        normalise(q - 2, i % 2, at, None)

            rings(act, NT, shared)
            for q in (NT - 2, NT - 1):
                normalise(q, q % 2, q * P, None)
            for n in range(2):
                act.wait_ge(out_stored[n], 16 * (NT // 2))

        @block.vector
        def _(dve):
            steps = 0

            def then(ins):
                nonlocal steps
                steps += 1
                ins.then_inc(routed, 1)
                dve.wait_ge(routed, steps)

            dve.wait_ge(made, CONSTANTS)
            then(dve.tensor_copy(edge[:], edge_i[:]))
            then(dve.tensor_copy(slot[:], slot_i[:]))
            for i in range(NT):
                dve.wait_ge(scored, i + 1)
                dve.max(top[:, i], scores[:, i]).then_inc(topped, 1)
                dve.wait_ge(topped, i + 1)
                dve.max_index(top_at[:, i], top[:, i], scores[:, i]).then_inc(found, 1)
            dve.wait_ge(found, NT)
            then(dve.tensor_copy(chosen[:], top_at[:, :, 0:TOPK].rearrange("p i c -> p c i")))
            for c in range(TOPK):
                for e in range(E):
                    then(dve.tensor_scalar(hot[:, c, e], chosen[:, c], float(e), None, ALU.is_equal))
            dve.tensor_tensor(both[:], hot[:, 0], hot[:, 1], ALU.add).then_inc(both_made, 1)
            then(dve.scalar_tensor_tensor(total[:], top[:, :, 0], NORM_EPS, top[:, :, 1], ALU.add, ALU.add))
            then(dve.reciprocal(total[:], total[:]))
            for c in range(TOPK):
                then(dve.scalar_tensor_tensor(share[:, c], top[:, :, c], SCALE, total[:], ALU.mult, ALU.mult))
            dve.wait_ge(counted, 1)
            counts = count_ps[:, 0:E * NT].rearrange("p (e i) -> p e i", e=E)
            then(dve.tensor_copy(former[:, :, 1:NT], counts[:, :, 0:NT - 1]))
            then(dve.tensor_tensor_scan(base[:].rearrange("p e i -> p (e i)"), keep[:].rearrange("p e i -> p (e i)"),
                                        former[:].rearrange("p e i -> p (e i)"), 0.0, ALU.mult, ALU.add))
            then(dve.tensor_tensor(size[:], base[:, :, NT - 1], counts[:, :, NT - 1], ALU.add))
            for e in range(E):
                then(dve.tensor_scalar(place[:, e], edge[:], size[:, e:e + 1], None, ALU.is_lt))
            then(dve.tensor_reduce(tiles[:], place[:], mybir.AxisListType.X, ALU.add))
            then(dve.tensor_tensor_scan(ends[:], one_row[:], tiles[:], 0.0, ALU.mult, ALU.add))
            then(dve.tensor_tensor(starts[:], ends[:], tiles[:], ALU.subtract))
            then(dve.tensor_scalar(starts[:], starts[:], float(P), None, ALU.mult))
            for e in range(E):
                then(dve.scalar_tensor_tensor(place[:, e], route_ps[:, e * NT:(e + 1) * NT], starts[:, e:e + 1], base[:, e],
                                              ALU.add, ALU.add))
            for c in range(TOPK):
                then(dve.tensor_tensor(hot[:, c], hot[:, c], place[:], ALU.mult))
                then(dve.tensor_reduce(dest_f[:, c], hot[:, c].rearrange("p e i -> p i e"), mybir.AxisListType.X, ALU.add))
            dve.tensor_copy(dest[:], dest_f[:]).then_inc(dest_made, 1)
            for e in range(E):
                then(dve.tensor_scalar(past[:, e], slot[:], ends[:, e:e + 1], None, ALU.is_ge))
            then(dve.tensor_reduce(owner[:], past[:].rearrange("p e s -> p s e"), mybir.AxisListType.X, ALU.add))
            then(dve.tensor_scalar(owner[:], owner[:], float(E - 1), None, ALU.min))
            dve.tensor_copy(expert[:], owner[:]).then_inc(rows_made, 1)

            def gate_u(q, at_zero):
                dve.wait_ge(h_made, q + 1)
                if not at_zero:
                    dve.wait_ge(g_turned, q)
                dve.tensor_tensor(gated[:], u_ps[:, 0:HID], act_h[:], ALU.mult).then_inc(g_made, 1)

            def copy_g(q, at_zero):
                dve.wait_ge(g_turned, q + 1)
                if not at_zero:
                    dve.wait_ge(downed, q)
                tail = HC[-1][1] - HC[-1][0]
                n = len(HC) - 1
                dve.tensor_copy(gt[:, 0:n].rearrange("p n t -> p (n t)"), g_ps[:, 0:n * P])
                dve.tensor_copy(gt[0:tail, n], g_ps[0:tail, n * P:(n + 1) * P]).then_inc(g_copied, 1)

            def experts(r, first, last):
                for i in range(RING):
                    gate_u(RING * r + i, first and i == 0)
                    copy_g(RING * r + i, first and i == 0)

            rings(dve, MOE_TILES, experts)

            def add_up(q, i, begun):
                n = i % 2
                all_q = MOE_TILES + q
                dve.wait_ge(downed, all_q + 1)
                dve.wait_ge(taken[n], 16 * TOPK * ((q - n) // 2 + 1 if isinstance(q, int) else begun + 1))
                if isinstance(q, int) and q < 2:
                    dve.wait_ge(y_stored[n], 16 * (MOE_TILES // 2))
                else:
                    dve.wait_ge(out_stored[n], 16 * ((q - n) // 2) if isinstance(q, int) else 16 * begun)
                dve.tensor_tensor(y[:, n], y_ps[:], xg[:, i], ALU.add).then_inc(y_made, 1)
                dve.wait_ge(y_made, all_q + 1)
                for c in range(TOPK):
                    dve.scalar_tensor_tensor(y[:, n], yg[:, n, c], share[:, c, bass.ds(q, 1)], y[:, n],
                                             ALU.mult, ALU.add).then_inc(added, 2)
                    dve.wait_ge(added, 2 * (TOPK * q + c + 1))
                dve.bn_stats(stats[:, n], y[:, n]).then_inc(row_stated, 1)
                dve.wait_ge(row_stated, q + 1)
                dve.tensor_tensor(pair[:, n], stats[:, n, 1:3], stats[:, n, 4:6], ALU.add).then_inc(row_step, 1)
                dve.tensor_tensor(gap[:, n:n + 1], stats[:, n, 1:2], stats[:, n, 4:5], ALU.subtract).then_inc(row_step, 1)
                dve.wait_ge(row_step, 4 * q + 2)
                dve.tensor_tensor(gap[:, n:n + 1], gap[:, n:n + 1], gap[:, n:n + 1], ALU.mult).then_inc(row_step, 1)
                dve.wait_ge(row_step, 4 * q + 3)
                dve.scalar_tensor_tensor(var[:, n:n + 1], gap[:, n:n + 1], DM / 4.0, pair[:, n, 1:2], ALU.mult, ALU.add).then_inc(row_step, 1)
                dve.wait_ge(row_step, 4 * q + 4)
                dve.tensor_scalar(var[:, n:n + 1], var[:, n:n + 1], 1.0 / DM, EPS, ALU.mult, ALU.add).then_inc(row_vared, 1)

            def shift_of(q, n):
                dve.wait_ge(rooted, q + 1)
                dve.scalar_tensor_tensor(shift[:, n:n + 1], pair[:, n, 0:1], -0.5, rstd[:, n:n + 1], ALU.mult, ALU.mult).then_inc(shifted, 1)

            def shared(r, first, last):
                for i in range(RING):
                    q = RING * r + i
                    gate_u(MOE_TILES + q, False)
                    if not (first and i == 0):
                        add_up(q - 1, (i - 1) % RING, RING // 2 * r + (i - 1) // 2)
                    copy_g(MOE_TILES + q, False)
                    if not (first and i == 0):
                        shift_of(q - 1, (i - 1) % 2)

            rings(dve, NT, shared)
            add_up(NT - 1, RING - 1, NT // 2 - 1)
            shift_of(NT - 1, 1)


CONSTANTS = 14


def kernel(**inputs):
    import numpy as np
    import concourse.bacc as bacc
    from concourse.bass_utils import run_bass_kernel_spmd

    v = {n.removeprefix("L0_attn_").removeprefix("L0_"): np.asarray(a) for n, a in inputs.items()}

    def rows(a):
        return np.ascontiguousarray(a.reshape(-1, P, a.shape[-1]).transpose(1, 0, 2))

    def column(a):
        return np.ascontiguousarray(a.reshape(-1, P).T)

    arrays = {
        "x": np.ascontiguousarray(v["x"].reshape(NB * L, DM)),
        "w_in": rows(v["W_in"]), "w_xp": rows(v["W_xp"]), "w_dt": np.ascontiguousarray(v["W_dt"]),
        "w_out": rows(v["W_out"]), "w_norm": column(v["w_norm"]),
        "conv_w": rows(np.ascontiguousarray(v["conv_w"].T)), "conv_b": column(v["conv_b"]),
        "b_dt": column(v["b_dt"]), "skip": column(v["D"]), "a_neg": rows(v["A_log"]),
        "gate": rows(np.ascontiguousarray(v["ffn_gate_w"].T)),
    }
    both = np.concatenate([np.concatenate([v["ffn_w1"], v["ffn_sw1"][None]]), np.concatenate([v["ffn_w3"], v["ffn_sw3"][None]])], 2)
    down = np.concatenate([v["ffn_w2"], v["ffn_sw2"][None]])
    padded = np.zeros((E + 1, len(HC) * P, DM), down.dtype)
    padded[:, :HID] = down
    arrays |= {
        "w13": np.ascontiguousarray(both.reshape(E + 1, KC, P, 2 * HID).transpose(0, 2, 1, 3)),
        "w2": np.ascontiguousarray(padded.reshape(E + 1, len(HC), P, DM).transpose(0, 2, 1, 3)),
    }
    nc = bacc.Bacc("TRN2", target_bir_lowering=False, num_devices=1)
    t = {n: nc.dram_tensor(n + "_dram", a.shape, mybir.dt.from_np(a.dtype), kind="ExternalInput").ap()
         for n, a in arrays.items()}
    t["b_rows"] = nc.dram_tensor("b_rows_dram", (NB * NS, L), F32, kind="Internal").ap()
    t["x1"] = nc.dram_tensor("x1_dram", (NTOK, DM), F32, kind="Internal").ap()
    t["y_rows"] = nc.dram_tensor("y_rows_dram", (LIST_ROWS, DM), F32, kind="Internal").ap()
    t["lists"] = nc.dram_tensor("lists_dram", (LIST_ROWS, 1), U32, kind="Internal").ap()
    t["out"] = nc.dram_tensor("out_dram", (NTOK, DM), F32, kind="ExternalOutput").ap()
    with ExitStack() as counters:
        mamba(nc, t, counters)
        moe(nc, t, counters)
    r = run_bass_kernel_spmd(nc, [{n + "_dram": a for n, a in arrays.items()}], core_ids=[0])
    return r.results[0]["out_dram"].reshape(NB, L, DM)
```

```python
from contextlib import ExitStack

import concourse.bass as bass
from concourse import mybir

F32 = mybir.dt.float32
BF16 = mybir.dt.bfloat16
U32 = mybir.dt.uint32
ALU = mybir.AluOpType
ACT = mybir.ActivationFunctionType

P = 128
NB, L, DM = 8, 512, 512
DI, NS, RANK, TAPS = 1024, 16, 128, 4
KC = DM // P
BLK = DI // P
GB = BLK // 2
TT = L // P
EPS = 1e-5
GROUP_STEPS = NS
STEPS = 2 * GROUP_STEPS
SCANS = STEPS * GB
H_RING, DBU_RING, SOFTP_RING = 8, 4, 4
B_CHUNK = 1
B_LOADS = STEPS // B_CHUNK

FIRST_HALF = {
    0: [("fin", 4, -1), ("fin", 5, -1)],
    1: [("fin", 6, -1), ("fin", 7, -1)],
    2: [("out", 4, -1), ("yt", 4, 0)],
    3: [("out", 5, -1), ("yt", 5, 0)],
    4: [("out", 6, -1), ("yt", 6, 0)],
    5: [("out", 7, -1), ("delta", 4, 0)],
    6: [("res", 4, 0), ("delta", 5, 0)],
    7: [("res", 5, 0), ("delta", 6, 0)],
    8: [("res", 6, 0), ("delta", 7, 0)],
    9: [("res", 7, 0)],
    10: [("xt", 0, 1), ("xt", 1, 1), ("xt", 2, 1), ("xt", 3, 1)],
    11: [("u", 0, 1)],
    12: [("u", 1, 1)],
    13: [("u", 2, 1), ("yt", 7, 0)],
    14: [("u", 3, 1)],
    15: [("u", 4, 1)],
}
SECOND_HALF = {
    0: [("u", 5, 1), ("fin", 0, 0)],
    1: [("u", 6, 1), ("fin", 1, 0)],
    2: [("u", 7, 1), ("fin", 2, 0)],
    3: [("fin", 3, 0), ("dt_begin", 0, 1)],
    4: [("out", 0, 0), ("dt", 0, 1)],
    5: [("out", 1, 0), ("delta", 0, 1)],
    6: [("out", 2, 0), ("delta", 1, 1)],
    7: [("out", 3, 0), ("delta", 2, 1)],
    8: [("delta", 3, 1)],
    9: [("bc_begin", 0, 1)],
    10: [("bc", 0, 1)],
    11: [("res", 0, 1), ("ct", 0, 1)],
    12: [("res", 1, 1), ("yt", 0, 1)],
    13: [("res", 2, 1), ("yt", 1, 1)],
    14: [("res", 3, 1), ("yt", 2, 1)],
    15: [("yt", 3, 1)],
}
JOBS_AT = {**FIRST_HALF, **{k + GROUP_STEPS: v for k, v in SECOND_HALF.items()}}
PER_SEQ = {"xt": TT, "u": BLK, "dt": 1, "bc": 1, "ct": 1, "delta": BLK, "res": BLK, "yt": BLK,
           "fin": BLK, "out": BLK}
SQUARE_AT, X_ROOT_AT, SCALE_AT = 2, 3, 5
SILU_U_AT = {16: 0, 20: 1}
SILU_RES_AT = {15: 0, 17: 1}
LOST_AT = {7: [(4, 0)], 8: [(5, 0)], 9: [(6, 0)], 11: [(7, 0)],
           23: [(0, 1)], 24: [(1, 1)], 25: [(2, 1)], 26: [(3, 1)]}
LN_AT = {10: [(4, 0), (5, 0)], 12: [(6, 0), (7, 0)],
         26: [(0, 1), (1, 1)], 28: [(2, 1), (3, 1)]}
HOLD_AT = {11: [(4, 0), (5, 0)], 13: [(6, 0), (7, 0)],
           27: [(0, 1)], 28: [(1, 1)], 29: [(2, 1), (3, 1)]}
MADE_AT = {12: [(4, 0)], 13: [(5, 0)], 14: [(6, 0)], 15: [(7, 0)],
           28: [(0, 1)], 29: [(1, 1)], 30: [(2, 1)], 31: [(3, 1)]}
VARIANCE_AT, LN_ROOT_AT, SHIFT_AT, LAYERNORM_AT = 6, 7, 7, 13
STORE_B_AT = 29

NTOK = NB * L
NT = NTOK // P
E, TOPK, HID = 8, 2, 352
SCALE, NORM_EPS = 2.5, 1e-20
HC = [(lo, min(lo + P, HID)) for lo in range(0, HID, P)]
RING = 4
MOE_TILES = -(-(TOPK * NTOK // P + E - 1) // RING) * RING
LIST_ROWS = MOE_TILES * P
KEPT, KEPT_RING = NT // RING, 3


def jobs_at(step, first, last):
    own = [("res", step, 0)] if first and step < GB else []
    return own + [(k, i, d) for k, i, d in JOBS_AT.get(step, []) if not (first and d < 0) and not (last and d > 0)]


def stages_at(table, step, last):
    return [(i, d) for i, d in table.get(step, []) if not (last and d > 0)]


def finished(jobs):
    return [job for job in jobs if not job[0].endswith("_begin")]


PROLOGUE = [(k, i, 1) for s in sorted(JOBS_AT) for k, i, d in JOBS_AT[s] if d > 0 and k != "res"]
EPILOGUE = [(k, i, -1) for s in sorted(JOBS_AT) for k, i, d in JOBS_AT[s] if d < 0]


def banks_of(jobs):
    begun = [(kind.removesuffix("_begin"), i) for kind, i, _ in jobs if kind not in ("dt", "bc")]
    return {job: n % 2 for n, job in enumerate(begun)}


STEP_BANKS = banks_of([job for s in sorted(JOBS_AT) for job in JOBS_AT[s]])
PROLOGUE_BANKS, EPILOGUE_BANKS = banks_of(PROLOGUE), banks_of(EPILOGUE)


def snap(eng, v):
    return v if isinstance(v, int) else eng.snap(v)


def mamba(nc, t, counters):
    ctx = ExitStack()
    with ctx:
        def sb(name, shape, dt=F32):
            return ctx.enter_context(nc.sbuf_tensor(name, shape, dt))

        def sem(name):
            return counters.enter_context(nc.semaphore(name))

        w_in = sb("w_in", [P, KC, 2 * DI])
        w_xp = sb("w_xp", [P, BLK, RANK + 2 * NS])
        w_dt = sb("w_dt", [P, DI])
        w_out = sb("w_out", [P, BLK, DM])
        w_norm = sb("w_norm", [P, KC])
        conv_w = sb("conv_w", [P, BLK, TAPS])
        conv_b = sb("conv_b", [P, BLK])
        b_dt = sb("b_dt", [P, BLK])
        skip = sb("skip", [P, BLK])
        a_neg = sb("a_neg", [P, BLK, NS])
        ident = sb("ident", [P, P])
        diag_d = sb("diag_d", [P, BLK, P])
        minus_half = sb("minus_half", [P, TT])
        x_in = sb("x_in", [P, TT, DM])
        x_sq = sb("x_sq", [P, TT])
        x_rstd = sb("x_rstd", [P, TT])
        xn_t = sb("xn_t", [P, KC, L])
        u = sb("u", [P, BLK, L])
        dt_r = sb("dt_r", [P, L])
        bc_t = sb("bc_t", [2 * NS, L])
        c_next = sb("c_next", [P, TT, NS])
        c_now = sb("c_now", [P, TT, NS])
        softp = sb("softp", [P, SOFTP_RING, L])
        delta = sb("delta", [P, BLK, L])
        du = sb("du", [P, BLK, L])
        sres = sb("sres", [P, BLK, L])
        y_t = sb("y_t", [P, 2, TT, GB * P])
        b_bc = sb("b_bc", [P, 2, B_CHUNK, L])
        dbu = sb("dbu", [P, DBU_RING, L])
        h = sb("h", [P, H_RING, L])
        acc = sb("acc", [P, TT, DM])
        stats = sb("stats", [P, TT, 6])
        ln_both = sb("ln_both", [P, TT, 2])
        ln_gap = sb("ln_gap", [P, TT])
        ln_var = sb("ln_var", [P, TT])
        ln_rstd = sb("ln_rstd", [P, TT])
        ln_shift = sb("ln_shift", [P, TT])

        ps = [ctx.enter_context(nc.psum_tensor(f"ps{i}", [P, 512], F32)) for i in range(8)]
        ht_ps, da_ps, job_ps = ps[0:4], ps[4:6], ps[6:8]

        small = ["a_neg", "w_norm", "conv_w", "conv_b", "b_dt", "skip"]
        small_loaded = sem("small_loaded")
        w_in_loaded = [sem(f"w_in_loaded{c}") for c in range(KC)]
        big = ["w_xp", "w_dt", "w_out"]
        loaded = {n: sem(f"loaded_{n}") for n in big}
        filled = {k: sem(f"filled_{k}") for k in PER_SEQ}
        taken = {k: sem(f"taken_{k}") for k in PER_SEQ}
        x_loaded = sem("x_loaded")
        re_loaded = sem("re_loaded")
        b_loaded = [sem(f"b_loaded{i}") for i in range(2)]
        x1_stored = sem("x1_stored")
        b_stored = sem("b_stored")
        ident_zeroed, ident_made, half_made = sem("ident_zeroed"), sem("ident_made"), sem("half_made")
        norm_folded, a_exped, a_made, diag_made = sem("norm_folded"), sem("a_exped"), sem("a_made"), sem("diag_made")
        x_squared, x_meaned, x_rooted, x_scaled = sem("x_squared"), sem("x_meaned"), sem("x_rooted"), sem("x_scaled")
        tap_made, conv_step, u_made = sem("tap_made"), sem("conv_step"), sem("u_made")
        abs_made, exp_made, ln_made, delta_made = sem("abs_made"), sem("exp_made"), sem("ln_made"), sem("delta_made")
        w_made, back_made, lost_made, lost_added, ln_held = sem("w_made"), sem("back_made"), sem("lost_made"), sem("lost_added"), sem("ln_held")
        du_made, res_made = sem("du_made"), sem("res_made")
        c_copied = sem("c_copied")
        da_made, dbu_made, scanned, turned, summed = sem("da_made"), sem("dbu_made"), sem("scanned"), sem("turned"), sem("summed")
        stats_made, ln_step, ln_biased, ln_rooted, shift_made, x1_made = (
            sem("stats_made"), sem("ln_step"), sem("ln_biased"), sem("ln_rooted"), sem("shift_made"), sem("x1_made"))
        block = ctx.enter_context(nc.Block())

        dram = {"w_in": w_in, "w_xp": w_xp, "w_dt": w_dt, "w_out": w_out, "w_norm": w_norm,
                "conv_w": conv_w, "conv_b": conv_b, "b_dt": b_dt, "skip": skip, "a_neg": a_neg}

        def sequences(eng, body):
            body(0, True, False)
            with eng.Fori(1, NB - 1) as b:
                body(b, False, False)
            body(NB - 1, False, True)

        @block.sync
        def _(sp):
            for n in small:
                sp.dma_start(dram[n][:], t[n]).then_inc(small_loaded, 16)

            def load_x(b):
                row = snap(sp, b * L)
                if not (isinstance(b, int) and b == 0):
                    sp.wait_ge(filled["xt"], TT * b)
                sp.dma_start(x_in[:], t["x"][bass.ds(row, L), :].rearrange("(i p) d -> p i d", p=P)).then_inc(x_loaded, 16)

            def load_re(b, first):
                row = snap(sp, b * L)
                if not first:
                    sp.wait_ge(x1_stored, 16 * b)
                sp.dma_start(acc[:], t["x"][bass.ds(row, L), :].rearrange("(i p) d -> p i d", p=P)).then_inc(re_loaded, 16)

            def load_b(b, c, begin):
                row = snap(sp, b * NS + (c * B_CHUNK) % NS)
                stored = snap(sp, 16 * b + 16)
                freed = snap(sp, SCANS * b + GB * B_CHUNK * (c - 1))
                if c == 0 or begin:
                    sp.wait_ge(b_stored, stored)
                if not (begin and c < 2):
                    sp.wait_ge(dbu_made, freed)
                src = t["b_rows"][bass.ds(row, B_CHUNK), :]
                sp.dma_start(b_bc[:, c % 2], src.partition_broadcast(P)).then_inc(b_loaded[c % 2], 16)

            def store_b(b):
                row = snap(sp, b * NS)
                sp.wait_ge(taken["bc"], b + 1)
                sp.dma_start(t["b_rows"][bass.ds(row, NS), :], bc_t[0:NS, :]).then_inc(b_stored, 16)

            def store_x1(b):
                row = snap(sp, b * L)
                sp.wait_ge(x1_made, TT * (b + 1))
                sp.dma_start(t["x1"][bass.ds(row, L), :].rearrange("(i p) d -> p i d", p=P), acc[:]).then_inc(x1_stored, 16)

            load_x(0)
            for c in range(KC):
                sp.dma_start(w_in[:, c], t["w_in"][:, c]).then_inc(w_in_loaded[c], 16)
            for n in big:
                sp.dma_start(dram[n][:], t[n]).then_inc(loaded[n], 16)
            store_b(0)
            load_b(0, 0, True)

            def body(b, first, last):
                for k in range(STEPS):
                    if k % B_CHUNK == 0:
                        c = k // B_CHUNK + 1
                        if c < B_LOADS:
                            load_b(b, c, first)
                        elif not last:
                            load_b(b + 1, 0, False)
                    if k == LAYERNORM_AT and not first:
                        store_x1(b - 1)
                    if k == 0 and not last:
                        load_x(b + 1)
                    if k == LAYERNORM_AT + 3:
                        load_re(b, first)
                    if k == STORE_B_AT and not last:
                        store_b(b + 1)

            sequences(sp, body)
            store_x1(NB - 1)
            sp.wait_ge(x1_stored, 16 * NB)

        @block.gpsimd
        def _(pool):
            pool.memset(ident[:], 0.0).then_inc(ident_zeroed, 1)
            pool.memset(minus_half[:], -0.5).then_inc(half_made, 1)
            pool.wait_ge(ident_zeroed, 1)
            pool.affine_select(out=ident[:], in_=ident[:], compare_op=ALU.not_equal, fill=1.0, base=0,
                               pattern=[[-1, P]], channel_multiplier=1).then_inc(ident_made, 1)

            pool.wait_ge(half_made, 1)

            def x_root(b):
                pool.wait_ge(x_meaned, TT * (b + 1))
                pool.tensor_tensor(x_rstd[:], x_sq[:], minus_half[:], ALU.pow).then_inc(x_rooted, 1)

            def make_lost(b, i):
                pool.wait_ge(back_made, BLK * b + i + 1)
                pool.tensor_tensor(softp[:, i % SOFTP_RING], softp[:, i % SOFTP_RING], du[:, i], ALU.subtract).then_inc(lost_made, 1)
                pool.wait_ge(lost_made, BLK * b + i + 1)
                pool.tensor_tensor(delta[:, i], delta[:, i], softp[:, i % SOFTP_RING], ALU.add).then_inc(lost_added, 1)

            def make_delta(b, i):
                pool.wait_ge(ln_held, BLK * b + i + 1)
                pool.tensor_tensor(delta[:, i], delta[:, i], softp[:, i % SOFTP_RING], ALU.add).then_inc(delta_made, 1)

            def make_du(b, i):
                pool.wait_ge(delta_made, BLK * b + i + 1)
                pool.wait_ge(u_made, 2 * b + i // GB + 1)
                pool.tensor_tensor(du[:, i], delta[:, i], u[:, i], ALU.mult).then_inc(du_made, 1)

            def ln_root(b):
                pool.wait_ge(ln_biased, b + 1)
                pool.tensor_tensor(ln_rstd[:], ln_var[:], minus_half[:], ALU.pow).then_inc(ln_rooted, 1)

            x_root(0)
            for i in range(GB):
                make_lost(0, i)
                if i >= 2:
                    make_delta(0, i - 2)
                    make_du(0, i - 2)
            for i in range(2, GB):
                make_delta(0, i)
                make_du(0, i)

            def body(b, first, last):
                for k in range(STEPS):
                    g, n = k // GROUP_STEPS, k % GROUP_STEPS
                    if k % B_CHUNK == 0:
                        c = k // B_CHUNK
                        pool.wait_ge(b_loaded[c % 2], 16 * (B_LOADS // 2 * b + c // 2 + 1))
                    if n == 0:
                        pool.wait_ge(du_made, BLK * b + GB * (g + 1))
                    for j in range(GB):
                        s = GB * k + j
                        if not (first and s < DBU_RING):
                            pool.wait_ge(scanned, SCANS * b + s - DBU_RING + 1)
                        pool.tensor_tensor(dbu[:, s % DBU_RING], du[:, g * GB + j],
                                           b_bc[:, (k // B_CHUNK) % 2, k % B_CHUNK], ALU.mult).then_inc(dbu_made, 1)

                    for i, d in stages_at(LOST_AT, k, last):
                        make_lost(b + d, i)
                    for i, d in stages_at(MADE_AT, k, last):
                        make_delta(b + d, i)
                        make_du(b + d, i)
                    if k == X_ROOT_AT and not last:
                        x_root(b + 1)
                    if k == LN_ROOT_AT and not first:
                        ln_root(b - 1)

            sequences(pool, body)
            ln_root(NB - 1)

        @block.scalar
        def _(act):
            act.wait_ge(small_loaded, 16 * len(small))
            act.activation(a_neg[:], a_neg[:], ACT.Exp).then_inc(a_exped, 1)

            def square(b, i):
                if i == 0:
                    act.wait_ge(x_loaded, 16 * (b + 1))
                    if not (isinstance(b, int) and b == 0):
                        act.wait_ge(delta_made, BLK * (b - 1) + GB)
                        act.wait_ge(x_rooted, b)
                if not (isinstance(b, int) and b == 0 and i == 0):
                    act.wait_ge(x_squared, TT * b + i)
                act.activation(softp[:, SOFTP_RING - 1], x_in[:, i], ACT.Square, accum_out=x_sq[:, i:i + 1]).then_inc(x_squared, 1)
                act.wait_ge(x_squared, TT * b + i + 1)
                act.activation(x_sq[:, i:i + 1], x_sq[:, i:i + 1], ACT.Copy, scale=1.0 / DM, bias=EPS).then_inc(x_meaned, 1)

            def scale(b, i):
                act.wait_ge(x_rooted, b + 1)
                act.activation(x_in[:, i], x_in[:, i], ACT.Copy, scale=x_rstd[:, i:i + 1]).then_inc(x_scaled, 1)

            def silu_u(b, g):
                act.wait_ge(taken["u"], BLK * b + GB * (g + 1))
                act.activation(u[:, g * GB:(g + 1) * GB], u[:, g * GB:(g + 1) * GB], ACT.Silu).then_inc(u_made, 1)

            def silu_res(b, g):
                act.wait_ge(taken["res"], BLK * b + GB * (g + 1))
                act.activation(sres[:, g * GB:(g + 1) * GB], sres[:, g * GB:(g + 1) * GB], ACT.Silu).then_inc(res_made, 1)

            def consume(b0, jobs, banks=STEP_BANKS):
                for kind, i, d in finished(jobs):
                    b, bank, g = b0 + d, job_ps[banks[kind, i]], i // GB
                    started = isinstance(b, int) and b == 0
                    if kind in ("xt", "u", "dt", "bc", "delta", "res", "yt"):
                        act.wait_ge(filled[kind], PER_SEQ[kind] * b + i + 1)
                    if kind == "xt":
                        if not started:
                            act.wait_ge(filled["res"], BLK * b)
                            act.wait_ge(filled["u"], BLK * b)
                        act.activation(xn_t[:, :, i * P:(i + 1) * P], bank[:].rearrange("p (c t) -> p c t", c=KC), ACT.Copy).then_inc(taken["xt"], 1)
                    if kind == "u":
                        if not started:
                            act.wait_ge(du_made, BLK * (b - 1) + i + 1)
                            act.wait_ge(filled["yt"], BLK * (b - 1) + GB * (g + 1))
                            act.wait_ge(filled["bc"], b)
                        act.activation(u[:, i], bank[:], ACT.Identity, scale=conv_w[:, i, TAPS - 1:TAPS],
                                       bias=conv_b[:, i:i + 1]).then_inc(tap_made, 1)
                    if kind == "dt":
                        if not started:
                            act.wait_ge(filled["delta"], BLK * b)
                        act.activation(dt_r[:], bank[:], ACT.Copy).then_inc(taken["dt"], 1)
                    if kind == "bc":
                        if not started:
                            act.wait_ge(filled["ct"], b)
                            act.wait_ge(b_stored, 16 * b)
                        act.activation(bc_t[:], bank[0:2 * NS, :], ACT.Copy).then_inc(taken["bc"], 1)
                    if kind == "delta":
                        if not (started and i < SOFTP_RING):
                            act.wait_ge(delta_made, BLK * b + i - SOFTP_RING + 1)
                        act.activation(softp[:, i % SOFTP_RING], bank[:], ACT.Abs, bias=b_dt[:, i:i + 1]).then_inc(abs_made, 1)
                        if not started:
                            act.wait_ge(da_made, SCANS * (b - 1) + GROUP_STEPS * GB * (g + 1))
                            act.wait_ge(du_made, BLK * (b - 1) + i + 1)
                        act.activation(delta[:, i], bank[:], ACT.Relu, bias=b_dt[:, i:i + 1]).then_inc(taken["delta"], 1)
                        act.wait_ge(abs_made, BLK * b + i + 1)
                        act.activation(softp[:, i % SOFTP_RING], softp[:, i % SOFTP_RING], ACT.Exp, scale=-1.0).then_inc(exp_made, 1)
                        if not started:
                            act.wait_ge(dbu_made, SCANS * (b - 1) + GROUP_STEPS * GB * (g + 1))
                        act.wait_ge(exp_made, BLK * b + i + 1)
                        act.activation(du[:, i], softp[:, i % SOFTP_RING], ACT.Identity, bias=1.0).then_inc(w_made, 1)
                        act.wait_ge(w_made, BLK * b + i + 1)
                        act.activation(du[:, i], du[:, i], ACT.Identity, bias=-1.0).then_inc(back_made, 1)
                    if kind == "res":
                        if not started:
                            act.wait_ge(filled["out"], BLK * (b - 1) + GB * (g + 1))
                        act.activation(sres[:, i], bank[:], ACT.Copy).then_inc(taken["res"], 1)
                    if kind == "yt":
                        if not started:
                            act.wait_ge(filled["fin"], BLK * (b - 1) + GB * (g + 1))
                        act.activation(y_t[:, g, i % GB], bank[:], ACT.Copy).then_inc(taken["yt"], 1)

            def take_ln(b, i):
                act.wait_ge(lost_added, BLK * b + i + 1)
                act.activation(softp[:, i % SOFTP_RING], du[:, i], ACT.Ln, bias=1.0).then_inc(ln_made, 1)

            def layernorm(b):
                act.wait_ge(shift_made, b + 1)
                for i in range(TT):
                    act.activation(acc[:, i], acc[:, i], ACT.Identity, scale=ln_rstd[:, i:i + 1],
                                   bias=ln_shift[:, i:i + 1]).then_inc(x1_made, 1)

            def decay(b, s, first):
                k, j = s // GB, s % GB
                g, n = k // GROUP_STEPS, k % GROUP_STEPS
                blk = g * GB + j
                if n == 0:
                    act.wait_ge(delta_made, BLK * b + blk + 1)
                if not (first and s < 2):
                    act.wait_ge(scanned, SCANS * b + s - 1)
                act.activation(da_ps[s % 2][:], delta[:, blk], ACT.Exp, scale=a_neg[:, blk, n:n + 1]).then_inc(da_made, 1)

            for i in range(TT):
                square(0, i)
            for i in range(TT):
                scale(0, i)
            for kind, i, d in PROLOGUE:
                consume(-1, [(kind, i, d)], PROLOGUE_BANKS)
                if (kind, i) == ("u", GB):
                    silu_u(0, 0)
                if (kind, i) == ("u", BLK - 1):
                    silu_u(0, 1)
                if (kind, i) == ("delta", 2):
                    take_ln(0, 0)
                    take_ln(0, 1)
                if (kind, i) == ("delta", 3):
                    take_ln(0, 2)
                    take_ln(0, 3)
            act.wait_ge(a_made, 1)
            decay(0, 0, True)
            decay(0, 1, True)

            def body(b, first, last):
                for k in range(STEPS):
                    for s in range(GB * k + 2, GB * k + GB + 2):
                        if s < SCANS:
                            decay(b, s, first)
                        elif not last:
                            decay(b + 1, s - SCANS, False)
                    if k == 0 and not first:
                        consume(b - 1, jobs_at(STEPS - 1, False, False))
                    if k > 0:
                        consume(b, jobs_at(k - 1, first, last))
                    for i, d in stages_at(LN_AT, k, last):
                        take_ln(b + d, i)
                    if not last:
                        if k == SQUARE_AT:
                            for i in range(TT):
                                square(b + 1, i)
                        if k == SCALE_AT:
                            for i in range(TT):
                                scale(b + 1, i)
                        if k in SILU_U_AT:
                            silu_u(b + 1, SILU_U_AT[k])
                    if k in SILU_RES_AT:
                        silu_res(b, SILU_RES_AT[k])
                    if k == LAYERNORM_AT and not first:
                        layernorm(b - 1)

            sequences(act, body)
            layernorm(NB - 1)

        @block.tensor
        def _(pe):
            first_use = {("dt_begin", 0): "w_xp", ("delta", 0): "w_dt", ("yt", 0): "w_out"}
            pe.wait_ge(norm_folded, KC)
            pe.wait_ge(ident_made, 1)
            pe.wait_ge(diag_made, BLK)
            bank_user = [None, None]

            def fill(b0, part, i, d, banks=STEP_BANKS):
                kind = part.removesuffix("_begin")
                b, bank, g = b0 + d, job_ps[banks[kind, i]], i // GB
                user = bank_user[banks[kind, i]]
                if user is not None and part not in ("dt", "bc", "ct"):
                    k0, i0, d0 = user
                    pe.wait_ge(taken[k0], PER_SEQ[k0] * (b0 + d0) + i0 + 1)
                bank_user[banks[kind, i]] = (kind, i, d)
                if kind == "xt":
                    pe.wait_ge(x_scaled, TT * b + i + 1)
                    for c in range(KC):
                        last = pe.transpose(bank[:, c * P:(c + 1) * P], x_in[:, i, c * P:(c + 1) * P], ident[:])
                if kind in ("u", "res"):
                    if (kind, i) == ("u", 0):
                        pe.wait_ge(taken["xt"], TT * b + TT)
                    if (kind, i) == ("res", 0):
                        pe.wait_ge(taken["bc"], b + 1)
                    col = (DI if kind == "res" else 0) + i * P
                    for c in range(KC):
                        last = pe.matmul(bank[:], w_in[:, c, col:col + P], xn_t[:, c, :], start=c == 0, stop=c == KC - 1)
                if kind in ("dt", "bc"):
                    pe.wait_ge(u_made, 2 * b + (1 if part != kind else 2))
                    lo, hi = (0, RANK) if kind == "dt" else (RANK, RANK + 2 * NS)
                    for c in range(GB) if part != kind else range(GB, BLK):
                        last = pe.matmul(bank[0:hi - lo, :], w_xp[:, c, lo:hi], u[:, c], start=c == 0, stop=c == BLK - 1)
                if kind == "ct":
                    for c in range(TT):
                        last = pe.transpose(bank[:, c * 2 * NS:(c + 1) * 2 * NS], bc_t[:, c * P:(c + 1) * P],
                                            ident[0:2 * NS, 0:2 * NS])
                if kind == "delta":
                    pe.wait_ge(taken["dt"], b + 1)
                    last = pe.matmul(bank[:], w_dt[:, i * P:(i + 1) * P], dt_r[:], start=True, stop=True)
                if kind == "yt":
                    tt = i % GB
                    for j in range(GB):
                        last = pe.matmul(bank[:, j * P:(j + 1) * P], u[:, g * GB + j, tt * P:(tt + 1) * P],
                                         diag_d[:, g * GB + j], start=True, stop=True)
                if kind == "fin":
                    j = i % GB
                    pe.wait_ge(summed, TT * (STEPS * b + GROUP_STEPS * (g + 1)))
                    for tt in range(TT):
                        last = pe.transpose(bank[:, tt * P:(tt + 1) * P], y_t[:, g, tt, j * P:(j + 1) * P], ident[:])
                if kind == "out":
                    tt = i % GB
                    pe.wait_ge(taken["fin"], BLK * b + GB * (g + 1))
                    for j in range(GB):
                        last = pe.matmul(bank[:], sres[:, g * GB + j, tt * P:(tt + 1) * P], w_out[:, g * GB + j],
                                         start=j == 0, stop=j == GB - 1)
                if part == kind:
                    last.then_inc(filled[kind], 1)

            def rebase():
                for n in range(2):
                    k0, i0, d0 = bank_user[n]
                    bank_user[n] = (k0, i0, d0 - 1)

            for kind, i, d in PROLOGUE:
                if (kind, i) in first_use:
                    pe.wait_ge(loaded[first_use[kind, i]], 16)
                if kind == "ct":
                    pe.wait_ge(taken["bc"], 1)
                fill(-1, kind, i, d, PROLOGUE_BANKS)
            rebase()

            def body(b, first, last):
                for k in range(STEPS):
                    for j in range(GB):
                        s = GB * k + j
                        pe.wait_ge(scanned, SCANS * b + s + 1)
                        if j == 0 and not (first and k == 0):
                            pe.wait_ge(summed, TT * (STEPS * b + k))
                        for tt in range(TT):
                            turn = pe.transpose(ht_ps[tt][:, j * P:(j + 1) * P], h[:, s % H_RING, tt * P:(tt + 1) * P], ident[:])
                        turn.then_inc(turned, 1)
                    for kind, i, d in jobs_at(k, first, last):
                        fill(b, kind, i, d)
                rebase()

            sequences(pe, body)
            for kind, i, d in EPILOGUE:
                fill(NB, kind, i, d, EPILOGUE_BANKS)

        @block.vector
        def _(dve):
            dve.wait_ge(small_loaded, 16 * len(small))
            for c in range(KC):
                dve.wait_ge(w_in_loaded[c], 16)
                dve.tensor_scalar(w_in[:, c], w_in[:, c], w_norm[:, c:c + 1], None, ALU.mult).then_inc(norm_folded, 1)
            dve.wait_ge(a_exped, 1)
            dve.tensor_scalar(a_neg[:], a_neg[:], -1.0, None, ALU.mult).then_inc(a_made, 1)
            dve.wait_ge(ident_made, 1)
            for i in range(BLK):
                dve.tensor_scalar(diag_d[:, i], ident[:], skip[:, i:i + 1], None, ALU.mult).then_inc(diag_made, 1)

            def consume(b0, jobs, banks=STEP_BANKS):
                for kind, i, d in finished(jobs):
                    b, bank, g = b0 + d, job_ps[banks[kind, i]], i // GB
                    if kind == "u":
                        dve.wait_ge(tap_made, BLK * b + i + 1)
                        for tap in range(1, TAPS):
                            if tap > 1:
                                dve.wait_ge(conv_step, (TAPS - 2) * (BLK * b + i) + tap - 1)
                            add = dve.scalar_tensor_tensor(u[:, i, tap:L], bank[:, 0:L - tap], conv_w[:, i, TAPS - 1 - tap:TAPS - tap],
                                                           u[:, i, tap:L], ALU.mult, ALU.add)
                            if tap < TAPS - 1:
                                add.then_inc(conv_step, 1)
                        add.then_inc(taken["u"], 1)
                    if kind == "ct":
                        dve.wait_ge(filled["ct"], b + 1)
                        if not (isinstance(b, int) and b == 0):
                            dve.wait_ge(c_copied, b)
                        dve.tensor_copy(c_next[:], bank[:, 0:TT * 2 * NS].rearrange("p (t n) -> p t n", t=TT)[:, :, NS:2 * NS]).then_inc(taken["ct"], 1)
                    if kind == "fin":
                        dve.wait_ge(filled["fin"], BLK * b + i + 1)
                        dve.wait_ge(res_made, 2 * b + (2 if g else 1))
                        dve.tensor_tensor(sres[:, i], bank[:], sres[:, i], ALU.mult).then_inc(taken["fin"], 1)
                    if kind == "out":
                        tt = i % GB
                        dve.wait_ge(filled["out"], BLK * b + i + 1)
                        if g == 0:
                            if tt == 0:
                                dve.wait_ge(re_loaded, 16 * (b + 1))
                            dve.scalar_tensor_tensor(acc[:, tt], acc[:, tt], 2.0, bank[:], ALU.mult, ALU.add).then_inc(taken["out"], 1)
                        else:
                            dve.wait_ge(taken["out"], BLK * b + tt + 1)
                            dve.tensor_tensor(acc[:, tt], bank[:], acc[:, tt], ALU.add).then_inc(taken["out"], 1)
                            dve.wait_ge(taken["out"], BLK * b + i + 1)
                            dve.bn_stats(stats[:, tt], acc[:, tt]).then_inc(stats_made, 1)

            def hold_ln(b, i):
                dve.wait_ge(ln_made, BLK * b + i + 1)
                dve.scalar_tensor_tensor(softp[:, i % SOFTP_RING], softp[:, i % SOFTP_RING], 0.0, du[:, i],
                                         ALU.max, ALU.min).then_inc(ln_held, 1)

            def variances(b):
                even, odd = stats[:, :, 1:3], stats[:, :, 4:6]
                dve.wait_ge(stats_made, TT * (b + 1))
                dve.tensor_tensor(ln_both[:], even, odd, ALU.add).then_inc(ln_step, 1)
                dve.tensor_tensor(ln_gap[:], stats[:, :, 1], stats[:, :, 4], ALU.subtract).then_inc(ln_step, 1)
                dve.wait_ge(ln_step, 4 * b + 2)
                dve.tensor_tensor(ln_gap[:], ln_gap[:], ln_gap[:], ALU.mult).then_inc(ln_step, 1)
                dve.wait_ge(ln_step, 4 * b + 3)
                dve.scalar_tensor_tensor(ln_var[:], ln_gap[:], DM / 4.0, ln_both[:, :, 1], ALU.mult, ALU.add).then_inc(ln_step, 1)
                dve.wait_ge(ln_step, 4 * b + 4)
                dve.tensor_scalar(ln_var[:], ln_var[:], 1.0 / DM, EPS, ALU.mult, ALU.add).then_inc(ln_biased, 1)

            def shifts(b):
                dve.wait_ge(ln_rooted, b + 1)
                dve.scalar_tensor_tensor(ln_shift[:], ln_both[:, :, 0], -0.5, ln_rstd[:], ALU.mult, ALU.mult).then_inc(shift_made, 1)

            def sum_states(b, k, first):
                g, n = k // GROUP_STEPS, k % GROUP_STEPS
                if k == 0:
                    dve.wait_ge(taken["ct"], b + 1)
                    if not first:
                        dve.wait_ge(summed, TT * STEPS * b)
                    dve.tensor_copy(c_now[:], c_next[:]).then_inc(c_copied, 1)
                    dve.wait_ge(c_copied, b + 1)
                if n == 0:
                    dve.wait_ge(taken["yt"], BLK * b + GB * (g + 1))
                dve.wait_ge(turned, SCANS * b + GB * (k + 1))
                for tt in range(TT):
                    if n > 0:
                        dve.wait_ge(summed, TT * (STEPS * b + k - 1) + tt + 1)
                    dve.scalar_tensor_tensor(y_t[:, g, tt], ht_ps[tt][:], c_now[:, tt, n:n + 1], y_t[:, g, tt],
                                             ALU.mult, ALU.add).then_inc(summed, 1)

            for kind, i, d in PROLOGUE:
                consume(-1, [(kind, i, d)], PROLOGUE_BANKS)
                if (kind, i) == ("delta", GB - 1):
                    for ii in range(GB):
                        hold_ln(0, ii)

            def body(b, first, last):
                for k in range(STEPS):
                    for j in range(GB):
                        s = GB * k + j
                        dve.wait_ge(da_made, SCANS * b + s + 1)
                        dve.wait_ge(dbu_made, SCANS * b + s + 1)
                        if not (first and s < H_RING):
                            dve.wait_ge(turned, SCANS * b + s - H_RING + 1)
                        dve.tensor_tensor_scan(h[:, s % H_RING], da_ps[s % 2][:], dbu[:, s % DBU_RING], 0.0,
                                               ALU.mult, ALU.add).then_inc(scanned, 1)
                    if k > 0:
                        sum_states(b, k - 1, first)
                        consume(b, jobs_at(k - 1, first, last))
                    elif not first:
                        sum_states(b - 1, STEPS - 1, False)
                        consume(b - 1, jobs_at(STEPS - 1, False, False))
                    for i, d in stages_at(HOLD_AT, k, last):
                        hold_ln(b + d, i)
                    if k == VARIANCE_AT and not first:
                        variances(b - 1)
                    if k == SHIFT_AT and not first:
                        shifts(b - 1)

            sequences(dve, body)
            sum_states(NB - 1, STEPS - 1, False)
            consume(NB, EPILOGUE, EPILOGUE_BANKS)
            variances(NB - 1)
            shifts(NB - 1)


def moe(nc, t, counters):
    ctx = ExitStack()
    with ctx:
        def sb(name, shape, dt=F32):
            return ctx.enter_context(nc.sbuf_tensor(name, shape, dt))

        def sem(name):
            return counters.enter_context(nc.semaphore(name))

        def sems(name, n=RING):
            return [sem(f"{name}{i}") for i in range(n)]

        w13 = sb("w13", [P, E + 1, KC, 2 * HID])
        w2 = sb("w2", [P, E + 1, len(HC), DM])
        gate = sb("gate", [P, KC, E])
        ident = sb("identity", [P, P])
        before = sb("before", [P, P], BF16)
        ones = sb("ones", [P, P], BF16)
        minus_half = sb("minus_halves", [P, 1])
        xg = sb("xg", [P, RING, DM])
        xt = sb("xt", [P, 2, KC, P])
        act_h = sb("act_h", [P, HID])
        gated = sb("gated", [P, HID])
        gt = sb("gt", [P, len(HC), P])
        y = sb("y", [P, RING, DM])
        yg = sb("yg", [P, 2, TOPK, DM])
        by_expert = sb("by_expert", [E, 2, P])
        scores = sb("scores", [P, NT, E])
        top = sb("top", [P, NT, 8])
        top_at = sb("top_at", [P, NT, 8], U32)
        chosen = sb("chosen", [P, TOPK, NT])
        hot = sb("hot", [P, TOPK, E, NT])
        both = sb("both", [P, E, NT], BF16)
        keep = sb("keep", [P, E, NT])
        former = sb("former", [P, E, NT])
        base = sb("base", [P, E, NT])
        place = sb("place", [P, E, NT])
        dest_f = sb("dest_f", [P, TOPK, NT])
        dest = sb("dest", [P, TOPK, NT], U32)
        total = sb("total", [P, NT])
        share = sb("share", [P, TOPK, NT])
        token = sb("token", [P, NT], U32)
        size = sb("size", [P, E])
        tiles = sb("tiles", [P, E])
        ends = sb("ends", [P, E])
        one_row = sb("one_row", [P, E])
        edge_i = sb("edge_i", [P, NT], U32)
        edge = sb("edge", [P, NT])
        slot_i = sb("slot_i", [P, MOE_TILES], U32)
        slot = sb("slot", [P, MOE_TILES])
        past = sb("past", [P, E, MOE_TILES])
        owner = sb("owner", [P, MOE_TILES])
        starts = sb("starts", [P, E])
        expert = sb("expert", [P, MOE_TILES], U32)
        zero = sb("zero", [P, LIST_ROWS // P], U32)
        put_at = sb("put_at", [P, TOPK, 2 * RING], U32)
        put = sb("put", [P, 2 * RING], U32)
        got = sb("got", [P, RING], U32)
        take_at = sb("take_at", [P, 2, TOPK], U32)
        stats = sb("row_stats", [P, RING, 6])
        pair = sb("pair", [P, RING, 2])
        gap = sb("gap", [P, RING])
        var = sb("var", [P, RING])
        rstd = sb("rstd", [P, RING])
        shift = sb("shift", [P, RING])

        ps = [ctx.enter_context(nc.psum_tensor(f"moe_ps{i}", [P, 512], F32)) for i in range(7)]
        x_ps, h_ps, u_ps, g_ps, y_ps, route_ps, count_ps = ps
        r_x_ps, r_gate_ps, r_back_ps = (x_ps, h_ps), (u_ps, g_ps), (y_ps, route_ps)

        w_loaded = sem("experts_loaded")
        gate_loaded = sem("gate_loaded")
        rx_loaded, r_turned, r_copied, r_gated, r_scored, r_backed, r_taken = (
            sems("rx_loaded"), sem("r_turned"), sem("r_copied"), sem("r_gated"), sem("r_scored"), sem("r_backed"), sem("r_taken"))
        made = sem("constants_made")
        zeroed, topped, found, routed = sem("zeroed"), sem("topped"), sem("found"), sem("routed")
        both_made, counted, dest_made, rows_made = sem("both_made"), sem("counted"), sem("dest_made"), sem("rows_made")
        table_cleared, put_copied, put_done = sem("table_cleared"), sem("put_copied"), sems("put_done", 2)
        got_loaded, gathered, x_loaded = sems("got_loaded"), sems("gathered"), sems("x_in")
        x_turned, x_copied, upped, h_made, g_made, g_turned, g_copied, downed = (
            sem(n) for n in ("x_turned", "x_copied", "upped", "h_made", "g_made", "g_turned", "g_copied", "downed"))
        y_made, y_stored = sem("y_made"), sems("y_stored", 2)
        shared_loaded, kept_loaded, kept_stored = sem("shared_loaded"), sems("kept_loaded", KEPT_RING), sems("kept_stored", 2)
        take_copied, taken = sem("take_copied"), sems("rows_taken", 2)
        added, row_stated, row_step, row_vared, rooted, shifted, out_made, out_stored = (
            sem("added"), sem("row_stated"), sem("row_step"), sem("row_vared"), sem("rooted"), sem("shifted"), sem("out_made"), sems("out_stored"))
        put_ready, gather_ready, take_ready = sem("put_ready"), sem("gather_ready"), sem("take_ready")
        block = ctx.enter_context(nc.Block())

        def rings(eng, n, body, peeled=1):
            turns = n // RING
            for r in range(peeled):
                body(r, r == 0, False)
            with eng.Fori(peeled, turns - 1) as r:
                body(r, False, False)
            body(turns - 1, False, True)

        @block.sync
        def _(sp):
            sp.dma_start(gate[:], t["gate"]).then_inc(gate_loaded, 16)

            def load_route(r, first, last):
                for i in range(RING):
                    at = snap(sp, (r * RING + i) * P)
                    if not first:
                        sp.wait_ge(r_turned, RING * (r - 1) + i + 1)
                    sp.dma_start(xg[:, i], t["x1"][bass.ds(at, P), :]).then_inc(rx_loaded[i], 16)

            rings(sp, NT, load_route)
            sp.dma_start(w13[:, E], t["w13"][E]).then_inc(shared_loaded, 16)
            sp.dma_start(w2[:, E], t["w2"][E]).then_inc(shared_loaded, 16)
            for n in range(max(E, KEPT)):
                if n < KEPT:
                    at = RING * n * P
                    if n < KEPT_RING:
                        sp.wait_ge(r_turned, NT - RING + n + 1)
                    else:
                        sp.wait_ge(y_made, n - KEPT_RING + 1)
                    sp.dma_start(xg[:, n % KEPT_RING], t["x1"][at:at + P, :]).then_inc(kept_loaded[n % KEPT_RING], 16)
                if n < E:
                    sp.dma_start(w13[:, n], t["w13"][n]).then_inc(w_loaded, 16)
                    sp.dma_start(w2[:, n], t["w2"][n]).then_inc(w_loaded, 16)
            for half in range(2):
                sp.wait_ge(put_done[half], 16 * TOPK * NT // 2)

            def load_got(r, first, last):
                for i in range(RING):
                    at = snap(sp, (r * RING + i) * P)
                    if not first:
                        sp.wait_ge(gathered[i], 16 * r)
                    sp.dma_start(got[:, i:i + 1], t["lists"][bass.ds(at, P), :]).then_inc(got_loaded[i], 16)

            rings(sp, MOE_TILES, load_got)

            for n in range(2):
                sp.wait_ge(kept_stored[n], 16 * KEPT // 2)

            def load_shared(r, first, last):
                for i in range(RING):
                    at = snap(sp, (r * RING + i) * P)
                    if first:
                        sp.wait_ge(x_turned, KEPT + MOE_TILES - RING + i + 1)
                    elif i:
                        sp.wait_ge(y_made, KEPT + MOE_TILES + (RING - 1) * (r - 1) + i)
                    else:
                        sp.wait_ge(added, TOPK * (RING * (r - 1) + 1))
                    src = t["x1"] if i else t["out"]
                    sp.dma_start(xg[:, i], src[bass.ds(at, P), :]).then_inc(x_loaded[i], 16)

            rings(sp, NT, load_shared)

        @block.gpsimd
        def _(pool):
            steps = 0

            def then(ins):
                nonlocal steps
                steps += 1
                ins.then_inc(made, 1)
                pool.wait_ge(made, steps)

            then(pool.memset(zero[:], 0))
            pool.dma_start(t["lists"].rearrange("(p n) a -> p (n a)", p=P), zero[:]).then_inc(table_cleared, 16)
            then(pool.memset(ident[:], 0.0))
            then(pool.affine_select(out=ident[:], in_=ident[:], compare_op=ALU.not_equal, fill=1.0, base=0,
                                    pattern=[[-1, P]], channel_multiplier=1))
            then(pool.memset(before[:], 1.0))
            then(pool.affine_select(out=before[:], in_=before[:], compare_op=ALU.is_gt, fill=0.0, base=0,
                                    pattern=[[1, P]], channel_multiplier=-1))
            then(pool.memset(ones[:], 1.0))
            then(pool.memset(minus_half[:], -0.5))
            then(pool.memset(keep[:], 1.0))
            then(pool.memset(keep[:, :, 0:1], 0.0))
            then(pool.memset(former[:], 0.0))
            then(pool.memset(one_row[:], 1.0))
            then(pool.iota(edge_i[:], pattern=[[P, NT]], base=0, channel_multiplier=0))
            then(pool.iota(slot_i[:], pattern=[[1, MOE_TILES]], base=0, channel_multiplier=0))
            then(pool.iota(token[:], pattern=[[P, NT]], base=0, channel_multiplier=1))
            assert steps == CONSTANTS

            pool.wait_ge(dest_made, 1)
            pool.wait_ge(table_cleared, 16)

            def put_tokens(r, first, last):
                for half in range(2):
                    slots = range(half * RING, (half + 1) * RING)
                    if not first:
                        pool.wait_ge(put_done[half], 16 * TOPK * RING * r)
                    lo, hi = slots[0], slots[-1] + 1
                    pool.tensor_copy(put[:, lo:hi], token[:, bass.ds(r * 2 * RING + lo, RING)]).then_inc(put_copied, 1)
                    pool.tensor_copy(put_at[:, :, lo:hi], dest[:, :, bass.ds(r * 2 * RING + lo, RING)]).then_inc(put_copied, 1)
                    pool.wait_ge(put_copied, 2 * (2 * r + half + 1))
                    pool.sem_inc(put_ready, 1)
                    for i in slots:
                        for c in range(TOPK):
                            pool.indirect_dma_start(t["lists"], bass.IndirectOffsetOnAxis(ap=put_at[:, c, i:i + 1], axis=0),
                                                    put[:, i:i + 1], None).then_inc(put_done[half], 16)

            rings(pool, NT // 2, put_tokens)

            def gather(r, first, last):
                for i in range(RING):
                    if not first:
                        pool.wait_ge(x_turned, KEPT + RING * (r - 1) + i + 1)
                    elif i < KEPT_RING:
                        pool.wait_ge(y_made, max(range(i, KEPT, KEPT_RING)) + 1)
                    else:
                        pool.wait_ge(r_turned, NT - RING + i + 1)
                    pool.wait_ge(got_loaded[i], 16 * (r + 1))
                    pool.sem_inc(gather_ready, 1)
                    pool.indirect_dma_start(xg[:, i], None, t["x1"],
                                            bass.IndirectOffsetOnAxis(ap=got[:, i:i + 1], axis=0)).then_inc(gathered[i], 16)

            rings(pool, MOE_TILES, gather)

            for n in range(2):
                pool.wait_ge(y_stored[n], 16 * (MOE_TILES // 2))

            def take(r, first, last):
                for i in range(RING):
                    q = RING * r + i
                    if not (first and i < 2):
                        pool.wait_ge(added, TOPK * (q - 1))
                    pool.tensor_copy(take_at[:, i % 2, :], dest[:, :, bass.ds(q, 1)]).then_inc(take_copied, 1)
                    pool.wait_ge(take_copied, q + 1)
                    pool.sem_inc(take_ready, 1)
                    for c in range(TOPK):
                        pool.indirect_dma_start(yg[:, i % 2, c], None, t["y_rows"],
                                                bass.IndirectOffsetOnAxis(ap=take_at[:, i % 2, c:c + 1], axis=0)).then_inc(taken[i % 2], 16)
                    if not (first and i == 0):
                        root(q - 1, (i - 1) % RING)

            def root(q, n):
                pool.wait_ge(row_vared, q + 1)
                pool.tensor_tensor(rstd[:, n:n + 1], var[:, n:n + 1], minus_half[:], ALU.pow).then_inc(rooted, 1)

            rings(pool, NT, take)
            root(NT - 1, RING - 1)

        @block.tensor
        def _(pe):
            pe.wait_ge(made, CONSTANTS)
            pe.wait_ge(gate_loaded, 16)

            def weigh(q, n):
                pe.wait_ge(r_copied, q + 1)
                if not (isinstance(q, int) and q == 0):
                    pe.wait_ge(r_scored, q)
                if not (isinstance(q, int) and q < 3):
                    pe.wait_ge(r_taken, q - 2)
                for c in range(KC):
                    last_mm = pe.matmul(r_gate_ps[n][0:E, 0:P], gate[:, c], xt[:, n, c], start=c == 0, stop=c == KC - 1)
                last_mm.then_inc(r_gated, 1)

            def turn_back(n):
                pe.transpose(r_back_ps[n][:, 0:E], by_expert[:, n], ident[0:E, 0:E]).then_inc(r_backed, 1)

            def route(r, first, last):
                for i in range(RING):
                    q = RING * r + i
                    pe.wait_ge(rx_loaded[i], 16 * (r + 1))
                    if not (first and i < 2):
                        pe.wait_ge(r_copied, q - 1)
                    for c in range(KC):
                        turn = pe.transpose(r_x_ps[i % 2][:, c * P:(c + 1) * P], xg[:, i, c * P:(c + 1) * P], ident[:])
                    turn.then_inc(r_turned, 1)
                    if not (first and i == 0):
                        weigh(q - 1, (i - 1) % 2)
                    if not (first and i < 2):
                        turn_back(i % 2)

            rings(pe, NT, route)
            weigh(NT - 1, 1)
            turn_back(0)
            pe.wait_ge(r_scored, NT)
            pe.wait_ge(r_taken, NT - 2)
            turn_back(1)
            pe.wait_ge(both_made, 1)
            pe.matmul(route_ps[:, 0:E * NT], before[:], both[:].rearrange("p e i -> p (e i)"), start=True, stop=True)
            pe.matmul(count_ps[:, 0:E * NT], ones[:], both[:].rearrange("p e i -> p (e i)"), start=True, stop=True).then_inc(counted, 1)

            def turn_x(q, slot, loaded, count):
                pe.wait_ge(loaded, count)
                if not (isinstance(q, int) and q == 0):
                    pe.wait_ge(x_copied, q)
                for c in range(KC):
                    turn = pe.transpose(x_ps[:, c * P:(c + 1) * P], xg[:, slot, c * P:(c + 1) * P], ident[:])
                turn.then_inc(x_turned, 1)

            def up(q, e, at_zero):
                pe.wait_ge(x_copied, q + 1)
                if not at_zero:
                    pe.wait_ge(g_made, q)
                for out, lo in ((h_ps, 0), (u_ps, HID)):
                    for c in range(KC):
                        last_mm = pe.matmul(out[:, 0:HID], xt[:, 0, c], w13[:, e, c, lo:lo + HID], start=c == 0, stop=c == KC - 1)
                last_mm.then_inc(upped, 1)

            def turn_g(q, at_zero):
                pe.wait_ge(g_made, q + 1)
                for n, (lo, hi) in enumerate(HC):
                    turn = pe.transpose(g_ps[0:hi - lo, n * P:(n + 1) * P], gated[:, lo:hi], ident[:])
                turn.then_inc(g_turned, 1)

            def down(q, e, at_zero):
                pe.wait_ge(g_copied, q + 1)
                if not at_zero:
                    pe.wait_ge(y_made, q)
                for n, (lo, hi) in enumerate(HC):
                    last_mm = pe.matmul(y_ps[:], gt[0:hi - lo, n], w2[0:hi - lo, e, n], start=n == 0, stop=n == len(HC) - 1)
                last_mm.then_inc(downed, 1)

            pe.wait_ge(shared_loaded, 2 * 16)
            turn_x(0, 0, kept_loaded[0], 16)
            for g in range(KEPT):
                up(g, E, g == 0)
                if g + 1 < KEPT:
                    turn_x(g + 1, (g + 1) % KEPT_RING, kept_loaded[(g + 1) % KEPT_RING], 16 * ((g + 1) // KEPT_RING + 1))
                if g > 0:
                    down(g - 1, E, g == 1)
                turn_g(g, g == 0)
            down(KEPT - 1, E, False)

            pe.wait_ge(w_loaded, 2 * 16 * E)
            pe.wait_ge(rows_made, 1)
            turn_x(KEPT, 0, gathered[0], 16)

            def experts(r, first, last):
                for i in range(RING):
                    q = RING * r + i
                    here = pe.value_load(expert[0:1, bass.ds(q, 1)], min_val=0, max_val=E - 1)
                    up(KEPT + q, bass.ds(here, 1), False)
                    if i + 1 < RING:
                        turn_x(KEPT + q + 1, i + 1, gathered[i + 1], 16 * (r + 1))
                    elif not last:
                        turn_x(KEPT + q + 1, 0, gathered[0], 16 * (r + 2))
                    if not (first and i == 0):
                        before_it = pe.value_load(expert[0:1, bass.ds(q - 1, 1)], min_val=0, max_val=E - 1)
                        down(KEPT + q - 1, bass.ds(before_it, 1), False)
                    turn_g(KEPT + q, False)

            rings(pe, MOE_TILES, experts)
            turn_x(KEPT + MOE_TILES, 1, x_loaded[1], 16)
            final = pe.value_load(expert[0:1, MOE_TILES - 1:MOE_TILES], min_val=0, max_val=E - 1)
            down(KEPT + MOE_TILES - 1, bass.ds(final, 1), False)

            def shared(r, first, last):
                for i in range(1, RING):
                    q = KEPT + MOE_TILES + (RING - 1) * r + i - 1
                    up(q, E, False)
                    if i + 1 < RING:
                        turn_x(q + 1, i + 1, x_loaded[i + 1], 16 * (r + 1))
                    elif not last:
                        turn_x(q + 1, 1, x_loaded[1], 16 * (r + 2))
                    if not (first and i == 1):
                        down(q - 1, E, False)
                    turn_g(q, False)

            rings(pe, NT, shared)
            down(MOE_TILES + NT - 1, E, False)

        @block.scalar
        def _(act):
            def score(q, n):
                act.wait_ge(r_gated, q + 1)
                act.activation(by_expert[:, n], r_gate_ps[n][0:E, 0:P], ACT.Sigmoid).then_inc(r_scored, 1)

            def route(r, first, last):
                for i in range(RING):
                    q = RING * r + i
                    act.wait_ge(r_turned, q + 1)
                    if not (first and i < 2):
                        act.wait_ge(r_gated, q - 1)
                    act.activation(xt[:, i % 2].rearrange("p c t -> p (c t)"), r_x_ps[i % 2][:], ACT.Copy).then_inc(r_copied, 1)
                    if not (first and i == 0):
                        score(q - 1, (i - 1) % 2)

            rings(act, NT, route)
            score(NT - 1, 1)

            def copy_x(q, at_zero):
                act.wait_ge(x_turned, q + 1)
                if at_zero:
                    act.wait_ge(r_gated, NT)
                else:
                    act.wait_ge(upped, q)
                act.activation(xt[:, 0].rearrange("p c t -> p (c t)"), x_ps[:], ACT.Copy).then_inc(x_copied, 1)

            def silu_h(q, at_zero):
                act.wait_ge(upped, q + 1)
                if not at_zero:
                    act.wait_ge(g_made, q)
                act.activation(act_h[:], h_ps[:, 0:HID], ACT.Silu).then_inc(h_made, 1)

            def keep_tile(g):
                act.wait_ge(y_made, g + 1)
                at = RING * g * P
                act.dma_start(t["out"][at:at + P, :], y[:, g % 2]).then_inc(kept_stored[g % 2], 16)

            copy_x(0, True)
            for g in range(KEPT):
                silu_h(g, g == 0)
                if g + 1 < KEPT:
                    copy_x(g + 1, False)
                if g > 0:
                    keep_tile(g - 1)
            keep_tile(KEPT - 1)
            copy_x(KEPT, False)

            def give_y(q, n, at, count):
                act.wait_ge(downed, KEPT + q + 1)
                act.wait_ge(kept_stored[n] if count is None else y_stored[n], 16 * KEPT // 2 if count is None else count)
                act.activation(y[:, n], y_ps[:], ACT.Copy).then_inc(y_made, 1)
                act.wait_ge(y_made, KEPT + q + 1)
                act.dma_start(t["y_rows"][bass.ds(at, P), :], y[:, n]).then_inc(y_stored[n], 16)

            def experts(r, first, last):
                for i in range(RING):
                    q = RING * r + i
                    silu_h(KEPT + q, False)
                    if not (last and i == RING - 1):
                        copy_x(KEPT + q + 1, False)
                    if not (first and i == 0):
                        at = snap(act, (q - 1) * P)
                        n = (i - 1) % 2
                        uses = 16 * (RING // 2 * r + (i - 1 - n) // 2)
                        give_y(q - 1, n, at, None if first and i < 3 else uses)

            rings(act, MOE_TILES, experts)
            copy_x(KEPT + MOE_TILES, False)
            give_y(MOE_TILES - 1, 1, (MOE_TILES - 1) * P, 16 * (MOE_TILES // 2 - 1))

            def normalise(r, i):
                q = RING * r + i
                at = snap(act, q * P)
                act.wait_ge(shifted, q + 1)
                act.activation(y[:, i], y[:, i], ACT.Identity, scale=rstd[:, i:i + 1], bias=shift[:, i:i + 1]).then_inc(out_made, 1)
                act.wait_ge(out_made, q + 1)
                act.dma_start(t["out"][bass.ds(at, P), :], y[:, i]).then_inc(out_stored[i], 16)

            def shared(r, first, last):
                for i in range(1, RING):
                    q = KEPT + MOE_TILES + (RING - 1) * r + i - 1
                    silu_h(q, False)
                    if not (last and i == RING - 1):
                        copy_x(q + 1, False)
                    if i == RING - 1:
                        normalise(r, 0)
                        normalise(r, 1)
                    elif not first:
                        normalise(r - 1, i + 1)

            rings(act, NT, shared)
            for i in (2, 3):
                normalise(NT // RING - 1, i)
            for i in range(RING):
                act.wait_ge(out_stored[i], 16 * (NT // RING))

        @block.vector
        def _(dve):
            steps = 0

            def then(ins):
                nonlocal steps
                steps += 1
                ins.then_inc(routed, 1)
                dve.wait_ge(routed, steps)

            dve.wait_ge(made, CONSTANTS)
            then(dve.tensor_copy(edge[:], edge_i[:]))
            then(dve.tensor_copy(slot[:], slot_i[:]))
            for i in range(NT):
                dve.wait_ge(r_backed, i + 1)
                dve.tensor_copy(scores[:, i], r_back_ps[i % 2][:, 0:E]).then_inc(r_taken, 1)
                dve.wait_ge(r_taken, i + 1)
                dve.max(top[:, i], scores[:, i]).then_inc(topped, 1)
                dve.wait_ge(topped, i + 1)
                dve.max_index(top_at[:, i], top[:, i], scores[:, i]).then_inc(found, 1)
            dve.wait_ge(found, NT)
            then(dve.tensor_copy(chosen[:], top_at[:, :, 0:TOPK].rearrange("p i c -> p c i")))
            for c in range(TOPK):
                for e in range(E):
                    then(dve.tensor_scalar(hot[:, c, e], chosen[:, c], float(e), None, ALU.is_equal))
            dve.tensor_tensor(both[:], hot[:, 0], hot[:, 1], ALU.add).then_inc(both_made, 1)
            then(dve.scalar_tensor_tensor(total[:], top[:, :, 0], NORM_EPS, top[:, :, 1], ALU.add, ALU.add))
            then(dve.reciprocal(total[:], total[:]))
            for c in range(TOPK):
                then(dve.scalar_tensor_tensor(share[:, c], top[:, :, c], SCALE, total[:], ALU.mult, ALU.mult))
            dve.wait_ge(counted, 1)
            counts = count_ps[:, 0:E * NT].rearrange("p (e i) -> p e i", e=E)
            then(dve.tensor_copy(former[:, :, 1:NT], counts[:, :, 0:NT - 1]))
            then(dve.tensor_tensor_scan(base[:].rearrange("p e i -> p (e i)"), keep[:].rearrange("p e i -> p (e i)"),
                                        former[:].rearrange("p e i -> p (e i)"), 0.0, ALU.mult, ALU.add))
            then(dve.tensor_tensor(size[:], base[:, :, NT - 1], counts[:, :, NT - 1], ALU.add))
            for e in range(E):
                then(dve.tensor_scalar(place[:, e], edge[:], size[:, e:e + 1], None, ALU.is_lt))
            then(dve.tensor_reduce(tiles[:], place[:], mybir.AxisListType.X, ALU.add))
            then(dve.tensor_tensor_scan(ends[:], one_row[:], tiles[:], 0.0, ALU.mult, ALU.add))
            then(dve.tensor_tensor(starts[:], ends[:], tiles[:], ALU.subtract))
            then(dve.tensor_scalar(starts[:], starts[:], float(P), None, ALU.mult))
            for e in range(E):
                then(dve.scalar_tensor_tensor(place[:, e], route_ps[:, e * NT:(e + 1) * NT], starts[:, e:e + 1], base[:, e],
                                              ALU.add, ALU.add))
            for c in range(TOPK):
                then(dve.tensor_tensor(hot[:, c], hot[:, c], place[:], ALU.mult))
                then(dve.tensor_reduce(dest_f[:, c], hot[:, c].rearrange("p e i -> p i e"), mybir.AxisListType.X, ALU.add))
            dve.tensor_copy(dest[:], dest_f[:]).then_inc(dest_made, 1)
            for e in range(E):
                then(dve.tensor_scalar(past[:, e], slot[:], ends[:, e:e + 1], None, ALU.is_ge))
            then(dve.tensor_reduce(owner[:], past[:].rearrange("p e s -> p s e"), mybir.AxisListType.X, ALU.add))
            then(dve.tensor_scalar(owner[:], owner[:], float(E - 1), None, ALU.min))
            dve.tensor_copy(expert[:], owner[:]).then_inc(rows_made, 1)

            def gate_u(q, at_zero):
                dve.wait_ge(h_made, q + 1)
                if not at_zero:
                    dve.wait_ge(g_turned, q)
                dve.tensor_tensor(gated[:], u_ps[:, 0:HID], act_h[:], ALU.mult).then_inc(g_made, 1)

            def copy_g(q, at_zero):
                dve.wait_ge(g_turned, q + 1)
                if not at_zero:
                    dve.wait_ge(downed, q)
                tail = HC[-1][1] - HC[-1][0]
                n = len(HC) - 1
                dve.tensor_copy(gt[:, 0:n].rearrange("p n t -> p (n t)"), g_ps[:, 0:n * P])
                dve.tensor_copy(gt[0:tail, n], g_ps[0:tail, n * P:(n + 1) * P]).then_inc(g_copied, 1)

            def add_kept(g):
                dve.wait_ge(downed, g + 1)
                if g >= 2:
                    dve.wait_ge(kept_stored[g % 2], 16 * (g // 2))
                dve.tensor_tensor(y[:, g % 2], y_ps[:], xg[:, g % KEPT_RING], ALU.add).then_inc(y_made, 1)

            for g in range(KEPT):
                gate_u(g, g == 0)
                if g > 0:
                    add_kept(g - 1)
                copy_g(g, g == 0)
            add_kept(KEPT - 1)

            def experts(r, first, last):
                for i in range(RING):
                    gate_u(KEPT + RING * r + i, False)
                    copy_g(KEPT + RING * r + i, False)

            rings(dve, MOE_TILES, experts)

            def add_up(r, i):
                q, worked = RING * r + i, KEPT + MOE_TILES + (RING - 1) * r + i - 1
                dve.wait_ge(taken[i % 2], 16 * TOPK * (RING // 2 * r + i // 2 + 1))
                if not (isinstance(r, int) and r == 0):
                    dve.wait_ge(out_stored[i], 16 * r)
                elif i < 2:
                    dve.wait_ge(y_stored[i], 16 * (MOE_TILES // 2))
                if i:
                    dve.wait_ge(downed, worked + 1)
                    dve.tensor_tensor(y[:, i], y_ps[:], xg[:, i], ALU.add).then_inc(y_made, 1)
                    dve.wait_ge(y_made, worked + 1)
                else:
                    dve.wait_ge(x_loaded[i], 16 * (r + 1))
                for c in range(TOPK):
                    so_far = xg[:, i] if i == 0 and c == 0 else y[:, i]
                    dve.scalar_tensor_tensor(y[:, i], yg[:, i % 2, c], share[:, c, bass.ds(q, 1)], so_far,
                                             ALU.mult, ALU.add).then_inc(added, 1)
                    dve.wait_ge(added, TOPK * q + c + 1)
                dve.bn_stats(stats[:, i], y[:, i]).then_inc(row_stated, 1)
                dve.wait_ge(row_stated, q + 1)
                dve.tensor_tensor(pair[:, i], stats[:, i, 1:3], stats[:, i, 4:6], ALU.add).then_inc(row_step, 1)
                dve.tensor_tensor(gap[:, i:i + 1], stats[:, i, 1:2], stats[:, i, 4:5], ALU.subtract).then_inc(row_step, 1)
                dve.wait_ge(row_step, 4 * q + 2)
                dve.tensor_tensor(gap[:, i:i + 1], gap[:, i:i + 1], gap[:, i:i + 1], ALU.mult).then_inc(row_step, 1)
                dve.wait_ge(row_step, 4 * q + 3)
                dve.scalar_tensor_tensor(var[:, i:i + 1], gap[:, i:i + 1], DM / 4.0, pair[:, i, 1:2], ALU.mult, ALU.add).then_inc(row_step, 1)
                dve.wait_ge(row_step, 4 * q + 4)
                dve.tensor_scalar(var[:, i:i + 1], var[:, i:i + 1], 1.0 / DM, EPS, ALU.mult, ALU.add).then_inc(row_vared, 1)

            def shift_of(r, i):
                dve.wait_ge(rooted, RING * r + i + 1)
                dve.scalar_tensor_tensor(shift[:, i:i + 1], pair[:, i, 0:1], -0.5, rstd[:, i:i + 1], ALU.mult, ALU.mult).then_inc(shifted, 1)

            def shared(r, first, last):
                for i in range(1, RING):
                    q = KEPT + MOE_TILES + (RING - 1) * r + i - 1
                    gate_u(q, False)
                    if i == 1:
                        former = [] if first else [(r - 1, RING - 1)]
                    else:
                        former = [(r, n) for n in ((0, 1) if i == 2 else (i - 1,))]
                    for at in former:
                        add_up(*at)
                    copy_g(q, False)
                    for at in former:
                        shift_of(*at)

            rings(dve, NT, shared, peeled=2)
            add_up(NT // RING - 1, RING - 1)
            shift_of(NT // RING - 1, RING - 1)


CONSTANTS = 14


def kernel(**inputs):
    import numpy as np
    import concourse.bacc as bacc
    from concourse.bass_utils import run_bass_kernel_spmd

    v = {n.removeprefix("L0_attn_").removeprefix("L0_"): np.asarray(a) for n, a in inputs.items()}

    def rows(a):
        return np.ascontiguousarray(a.reshape(-1, P, a.shape[-1]).transpose(1, 0, 2))

    def column(a):
        return np.ascontiguousarray(a.reshape(-1, P).T)

    arrays = {
        "x": np.ascontiguousarray(v["x"].reshape(NB * L, DM)),
        "w_in": rows(v["W_in"]), "w_xp": rows(v["W_xp"]), "w_dt": np.ascontiguousarray(v["W_dt"]),
        "w_out": rows(v["W_out"]), "w_norm": column(v["w_norm"]),
        "conv_w": rows(np.ascontiguousarray(v["conv_w"].T)), "conv_b": column(v["conv_b"]),
        "b_dt": column(v["b_dt"]), "skip": column(v["D"]), "a_neg": rows(v["A_log"]),
        "gate": rows(np.ascontiguousarray(v["ffn_gate_w"].T)),
    }
    both = np.concatenate([np.concatenate([v["ffn_w1"], v["ffn_sw1"][None]]), np.concatenate([v["ffn_w3"], v["ffn_sw3"][None]])], 2)
    down = np.concatenate([v["ffn_w2"], v["ffn_sw2"][None]])
    padded = np.zeros((E + 1, len(HC) * P, DM), down.dtype)
    padded[:, :HID] = down
    arrays |= {
        "w13": np.ascontiguousarray(both.reshape(E + 1, KC, P, 2 * HID).transpose(0, 2, 1, 3)),
        "w2": np.ascontiguousarray(padded.reshape(E + 1, len(HC), P, DM).transpose(0, 2, 1, 3)),
    }
    nc = bacc.Bacc("TRN2", target_bir_lowering=False, num_devices=1)
    t = {n: nc.dram_tensor(n + "_dram", a.shape, mybir.dt.from_np(a.dtype), kind="ExternalInput").ap()
         for n, a in arrays.items()}
    t["b_rows"] = nc.dram_tensor("b_rows_dram", (NB * NS, L), F32, kind="Internal").ap()
    t["x1"] = nc.dram_tensor("x1_dram", (NTOK, DM), F32, kind="Internal").ap()
    t["y_rows"] = nc.dram_tensor("y_rows_dram", (LIST_ROWS, DM), F32, kind="Internal").ap()
    t["lists"] = nc.dram_tensor("lists_dram", (LIST_ROWS, 1), U32, kind="Internal").ap()
    t["out"] = nc.dram_tensor("out_dram", (NTOK, DM), F32, kind="ExternalOutput").ap()
    with ExitStack() as counters:
        mamba(nc, t, counters)
        moe(nc, t, counters)
    r = run_bass_kernel_spmd(nc, [{n + "_dram": a for n, a in arrays.items()}], core_ids=[0])
    return r.results[0]["out_dram"].reshape(NB, L, DM)
```
